# Optimizing a Trainium2 kernel written in Bass

```python
import numpy as np
import jax
import jax.numpy as jnp

def _softmax(x, axis=-1):
    return jax.nn.softmax(x, axis=axis)

def _gelu(x):
    return jax.nn.gelu(x, approximate=True)

def _silu(x):
    return jax.nn.silu(x)

def _sigmoid(x):
    return jax.nn.sigmoid(x)

def _layernorm(x, axis=-1, eps=1e-05):
    m = jnp.mean(x, axis=axis, keepdims=True)
    v = jnp.var(x, axis=axis, keepdims=True)
    return (x - m) / jnp.sqrt(v + eps)

def _scatter_add(tgt, idx, src, axis=0):
    return tgt.at[idx].add(src)

def _segment_sum(src, seg, n):
    return jax.ops.segment_sum(src, seg, n)
kernel_name = 'mk_gnn_preln_d4_gnn_r64_3184e3'

def setup_inputs(seed: int=0):
    np.random.seed(seed)
    _w = jnp.asarray

    def _rec_inputs():
        import jax
        import jax.numpy as jnp
        _gk = jax.random.key(seed)
        x = -0.000124 + 1 * jax.random.normal(jax.random.fold_in(_gk, 1), (18870, 256), jnp.float32)
        src = jax.random.randint(jax.random.fold_in(_gk, 2), (9435,), 0, 18870, jnp.int32)
        dst = jax.random.randint(jax.random.fold_in(_gk, 3), (9435,), 0, 18870, jnp.int32)
        _o = jnp.argsort(dst, stable=True)
        src = src[_o]
        dst = dst[_o]
        edge_attr_256 = -8.16379e-05 + 0.999858 * jax.random.normal(jax.random.fold_in(_gk, 12), (9435, 256), jnp.float32)
        edge_type_240 = jax.random.randint(jax.random.fold_in(_gk, 14), (9435,), 0, 240, jnp.int32)
        edge_weight = jax.random.uniform(jax.random.fold_in(_gk, 15), (9435,), jnp.float32, 0.0, 0.999998)
        return (x, src, dst, edge_attr_256, edge_type_240, edge_weight)
    x, src, dst, edge_attr_256, edge_type_240, edge_weight = _rec_inputs()

    def _L0_gnn_setup():
        import jax, jax.numpy as jnp
        import numpy as np
        N, D, E, L = (18870, 256, 9435, 4)
        EPS = 1e-05

        def _layer_norm(x, scale, bias):
            mu = jnp.mean(x, axis=-1, keepdims=True)
            var = jnp.mean(jnp.square(x - mu), axis=-1, keepdims=True)
            return (x - mu) * jax.lax.rsqrt(var + EPS) * scale + bias
        key = jax.random.key(seed)
        ks = jax.random.split(key, 8)
        x = jax.random.normal(ks[0], (N, D), dtype=jnp.float32)
        edge_index = jax.random.randint(ks[1], (2, E), 0, N, dtype=jnp.int64)
        edge_weight = jax.random.uniform(ks[2], (E,), dtype=jnp.float32)
        ln_scale = jnp.ones((L, D), jnp.float32)
        ln_bias = jnp.zeros((L, D), jnp.float32)
        conv_w = jax.random.normal(ks[3], (L, D, D), dtype=jnp.float32) * 0.05
        conv_b = jnp.zeros((L, D), jnp.float32)
        post_w = jax.random.normal(ks[4], (D, D), dtype=jnp.float32) * 0.05
        post_b = jnp.zeros((D,), jnp.float32)
        return {'x': x, 'edge_weight': edge_weight, 'ln_scale': ln_scale, 'ln_bias': ln_bias, 'conv_w': conv_w, 'conv_b': conv_b, 'post_w': post_w, 'post_b': post_b, 'edge_index': edge_index}
    _L0_gnn_all = _L0_gnn_setup()
    _L0_gnn_in = {k: v for k, v in _L0_gnn_all.items() if k in ('ln_scale', 'ln_bias', 'conv_w', 'conv_b', 'post_w', 'post_b')}
    del _L0_gnn_all

    def _L1_gnn_setup():
        import jax, jax.numpy as jnp
        import numpy as np
        THR_A = 0.1
        THR_W = 0.1
        N, M, F_IN, F_OUT = (50000, 6250, 256, 256)
        key = jax.random.key(seed)
        k1, k2, k3, k4, k5, k6 = jax.random.split(key, 6)
        x = jax.random.normal(k1, (N, F_IN), dtype=jnp.float32)
        edge_index = jax.random.randint(k2, (2, M), 0, N, dtype=jnp.int64)
        edge_weight = jax.random.uniform(k3, (M,), dtype=jnp.float32)
        node_lock = jax.random.randint(k4, (1000,), 0, N, dtype=jnp.int64)
        W = jax.random.normal(k5, (F_OUT, F_IN), dtype=jnp.float32) / np.sqrt(F_IN)
        b = jax.random.normal(k6, (F_OUT,), dtype=jnp.float32) * 0.01
        return {'x': x, 'edge_index': edge_index, 'edge_weight': edge_weight, 'node_lock': node_lock, 'W': W, 'b': b}
    _L1_gnn_all = _L1_gnn_setup()
    _L1_gnn_in = {k: v for k, v in _L1_gnn_all.items() if k in ('node_lock', 'W', 'b')}
    del _L1_gnn_all

    def _L2_gnn_setup():
        import jax, jax.numpy as jnp
        import numpy as np
        N = 50000
        R = 240
        D = 256
        B = 10
        E = 5000
        RATE = 0.1
        LN_EPS = 1e-05

        def _time_decay(etimes, current_time):
            td = jnp.maximum(current_time - etimes, 0.0)
            td = td / (td.max() + 1e-08)
            return jnp.exp(-RATE * td)[:, None]

        def _rgcn_layer(h, basis, comp, loop_w, bias, src, dst, etypes, enorm):
            hsrc = h[src]
            coef = comp[etypes]
            msg = jnp.zeros_like(hsrc)
            for b in range(basis.shape[0]):
                msg = msg + coef[:, b:b + 1] * (hsrc @ basis[b])
            msg = msg * enorm
            agg = jax.ops.segment_sum(msg, dst, num_segments=h.shape[0])
            return agg + bias + h @ loop_w
        key = jax.random.key(seed)
        ks = jax.random.split(key, 16)
        s = 1.0 / np.sqrt(D)
        return {'entity_emb': jax.random.normal(ks[0], (N, D), jnp.float32) * s, 'basis1': jax.random.normal(ks[1], (B, D, D), jnp.float32) * s, 'comp1': jax.random.normal(ks[2], (R, B), jnp.float32) * 0.3, 'loop_w1': jax.random.normal(ks[3], (D, D), jnp.float32) * s, 'bias1': jnp.zeros((D,), jnp.float32), 'basis2': jax.random.normal(ks[4], (B, D, D), jnp.float32) * s, 'comp2': jax.random.normal(ks[5], (R, B), jnp.float32) * 0.3, 'loop_w2': jax.random.normal(ks[6], (D, D), jnp.float32) * s, 'bias2': jnp.zeros((D,), jnp.float32), 'ln_g': jnp.ones((D,), jnp.float32), 'ln_b': jnp.zeros((D,), jnp.float32), 'etimes': jax.random.uniform(ks[7], (E,), jnp.float32), 'current_time': jnp.float32(1.0), 'src': jax.random.randint(ks[8], (E,), 0, N), 'dst': jax.random.randint(ks[9], (E,), 0, N), 'etypes': jax.random.randint(ks[10], (E,), 0, R)}
    _L2_gnn_all = _L2_gnn_setup()
    _L2_gnn_in = {k: v for k, v in _L2_gnn_all.items() if k in ('basis1', 'comp1', 'loop_w1', 'bias1', 'basis2', 'comp2', 'loop_w2', 'bias2', 'ln_g', 'ln_b', 'current_time')}
    del _L2_gnn_all

    def _L3_gnn_setup():
        import jax, jax.numpy as jnp
        import numpy as np
        BN_EPS = 1e-05

        def _batchnorm(x, gamma, beta):
            mu = jnp.mean(x, axis=0)
            var = jnp.var(x, axis=0)
            return gamma * (x - mu) * jax.lax.rsqrt(var + BN_EPS) + beta
        key = jax.random.key(seed)
        ks = jax.random.split(key, 8)
        N, E, D = (50000, 6250, 256)
        H = 2 * D
        node_rep = jax.random.normal(ks[0], (N, D), dtype=jnp.float32)
        edge_attr = jax.random.normal(ks[1], (E, D), dtype=jnp.float32)
        edge_index = jax.random.randint(ks[2], (2, E), 0, N, dtype=jnp.int64)
        scale1 = 1.0 / np.sqrt(D)
        scale2 = 1.0 / np.sqrt(H)
        W1 = jax.random.uniform(ks[3], (D, H), jnp.float32, -scale1, scale1)
        W2 = jax.random.uniform(ks[4], (H, D), jnp.float32, -scale2, scale2)
        gamma1 = jnp.ones((H,), jnp.float32)
        beta1 = jnp.zeros((H,), jnp.float32)
        gamma2 = jnp.ones((D,), jnp.float32)
        beta2 = jnp.zeros((D,), jnp.float32)
        epsilon = jnp.zeros((1,), jnp.float32)
        return {'node_rep': node_rep, 'edge_attr': edge_attr, 'edge_index': edge_index, 'W1': W1, 'gamma1': gamma1, 'beta1': beta1, 'W2': W2, 'gamma2': gamma2, 'beta2': beta2, 'epsilon': epsilon}
    _L3_gnn_all = _L3_gnn_setup()
    _L3_gnn_in = {k: v for k, v in _L3_gnn_all.items() if k in ('W1', 'gamma1', 'beta1', 'W2', 'gamma2', 'beta2', 'epsilon')}
    del _L3_gnn_all
    return {'x': x, 'src': src, 'dst': dst, 'edge_attr_256': edge_attr_256, 'edge_type_240': edge_type_240, 'edge_weight': edge_weight, 'L0_gnn_ln_scale': _L0_gnn_in['ln_scale'], 'L0_gnn_ln_bias': _L0_gnn_in['ln_bias'], 'L0_gnn_conv_w': _L0_gnn_in['conv_w'], 'L0_gnn_conv_b': _L0_gnn_in['conv_b'], 'L0_gnn_post_w': _L0_gnn_in['post_w'], 'L0_gnn_post_b': _L0_gnn_in['post_b'], 'L1_gnn_node_lock': _L1_gnn_in['node_lock'], 'L1_gnn_W': _L1_gnn_in['W'], 'L1_gnn_b': _L1_gnn_in['b'], 'L2_gnn_basis1': _L2_gnn_in['basis1'], 'L2_gnn_comp1': _L2_gnn_in['comp1'], 'L2_gnn_loop_w1': _L2_gnn_in['loop_w1'], 'L2_gnn_bias1': _L2_gnn_in['bias1'], 'L2_gnn_basis2': _L2_gnn_in['basis2'], 'L2_gnn_comp2': _L2_gnn_in['comp2'], 'L2_gnn_loop_w2': _L2_gnn_in['loop_w2'], 'L2_gnn_bias2': _L2_gnn_in['bias2'], 'L2_gnn_ln_g': _L2_gnn_in['ln_g'], 'L2_gnn_ln_b': _L2_gnn_in['ln_b'], 'L2_gnn_current_time': _L2_gnn_in['current_time'], 'L3_gnn_W1': _L3_gnn_in['W1'], 'L3_gnn_gamma1': _L3_gnn_in['gamma1'], 'L3_gnn_beta1': _L3_gnn_in['beta1'], 'L3_gnn_W2': _L3_gnn_in['W2'], 'L3_gnn_gamma2': _L3_gnn_in['gamma2'], 'L3_gnn_beta2': _L3_gnn_in['beta2'], 'L3_gnn_epsilon': _L3_gnn_in['epsilon']}

def reference(x, src, dst, edge_attr_256, edge_type_240, edge_weight, L0_gnn_ln_scale, L0_gnn_ln_bias, L0_gnn_conv_w, L0_gnn_conv_b, L0_gnn_post_w, L0_gnn_post_b, L1_gnn_node_lock, L1_gnn_W, L1_gnn_b, L2_gnn_basis1, L2_gnn_comp1, L2_gnn_loop_w1, L2_gnn_bias1, L2_gnn_basis2, L2_gnn_comp2, L2_gnn_loop_w2, L2_gnn_bias2, L2_gnn_ln_g, L2_gnn_ln_b, L2_gnn_current_time, L3_gnn_W1, L3_gnn_gamma1, L3_gnn_beta1, L3_gnn_W2, L3_gnn_gamma2, L3_gnn_beta2, L3_gnn_epsilon):
    import jax
    import jax.numpy as jnp

    def _L0_gnn_ref(x, edge_weight, ln_scale, ln_bias, conv_w, conv_b, post_w, post_b, edge_index):
        import jax, jax.numpy as jnp
        import numpy as np
        N, D, E, L = (18870, 256, 9435, 4)
        EPS = 1e-05

        def _layer_norm(x, scale, bias):
            mu = jnp.mean(x, axis=-1, keepdims=True)
            var = jnp.mean(jnp.square(x - mu), axis=-1, keepdims=True)
            return (x - mu) * jax.lax.rsqrt(var + EPS) * scale + bias
        src, dst = (edge_index[0], edge_index[1])
        for i in range(L):
            xn = _layer_norm(x, ln_scale[i], ln_bias[i])
            h = xn @ conv_w[i]
            msg = h[src] * edge_weight[:, None]
            agg = jax.ops.segment_sum(msg, dst, num_segments=N)
            x = x + jax.nn.relu(agg + conv_b[i])
        return x @ post_w + post_b

    def _L1_gnn_ref(x, edge_index, edge_weight, node_lock, W, b):
        import jax, jax.numpy as jnp
        import numpy as np
        THR_A = 0.1
        THR_W = 0.1
        N, M, F_IN, F_OUT = (50000, 6250, 256, 256)
        n, f_in = x.shape
        norm_node_in = jnp.linalg.norm(x, axis=0)
        norm_all_in = jnp.linalg.norm(norm_node_in) / f_in
        thr_wi = THR_W * norm_all_in / norm_node_in
        W_pruned = jnp.where(jnp.abs(W) < thr_wi[None, :], 0.0, W)
        W_eff = jnp.where(norm_all_in > 1e-08, W_pruned, W)
        h = x @ W_eff.T
        src, dst = (edge_index[0], edge_index[1])
        locked = jnp.zeros((n,), dtype=bool).at[node_lock].set(True)
        lock = locked[dst] | (src == dst)
        msg = edge_weight[:, None] * h[src]
        norm_feat_msg = jnp.linalg.norm(msg, axis=1)
        norm_all_msg = jnp.sum(norm_feat_msg) / msg.shape[0]
        mask0 = (norm_feat_msg < THR_A * norm_all_msg) & ~lock
        msg = jnp.where(mask0[:, None], 0.0, msg)
        out = jax.ops.segment_sum(msg, dst, num_segments=n) + b
        return out

    def _L2_gnn_ref(entity_emb, basis1, comp1, loop_w1, bias1, basis2, comp2, loop_w2, bias2, ln_g, ln_b, etimes, current_time, src, dst, etypes):
        import jax, jax.numpy as jnp
        import numpy as np
        N = 50000
        R = 240
        D = 256
        B = 10
        E = 5000
        RATE = 0.1
        LN_EPS = 1e-05

        def _time_decay(etimes, current_time):
            td = jnp.maximum(current_time - etimes, 0.0)
            td = td / (td.max() + 1e-08)
            return jnp.exp(-RATE * td)[:, None]

        def _rgcn_layer(h, basis, comp, loop_w, bias, src, dst, etypes, enorm):
            hsrc = h[src]
            coef = comp[etypes]
            msg = jnp.zeros_like(hsrc)
            for b in range(basis.shape[0]):
                msg = msg + coef[:, b:b + 1] * (hsrc @ basis[b])
            msg = msg * enorm
            agg = jax.ops.segment_sum(msg, dst, num_segments=h.shape[0])
            return agg + bias + h @ loop_w
        enorm = _time_decay(etimes, current_time)
        h_init = entity_emb
        h = h_init
        h = jax.nn.relu(_rgcn_layer(h, basis1, comp1, loop_w1, bias1, src, dst, etypes, enorm))
        h = jax.nn.relu(_rgcn_layer(h, basis2, comp2, loop_w2, bias2, src, dst, etypes, enorm))
        h = h + h_init
        mu = h.mean(-1, keepdims=True)
        var = ((h - mu) ** 2).mean(-1, keepdims=True)
        return (h - mu) * jax.lax.rsqrt(var + LN_EPS) * ln_g + ln_b

    def _L3_gnn_ref(node_rep, edge_attr, edge_index, W1, gamma1, beta1, W2, gamma2, beta2, epsilon):
        import jax, jax.numpy as jnp
        import numpy as np
        BN_EPS = 1e-05

        def _batchnorm(x, gamma, beta):
            mu = jnp.mean(x, axis=0)
            var = jnp.var(x, axis=0)
            return gamma * (x - mu) * jax.lax.rsqrt(var + BN_EPS) + beta
        N = node_rep.shape[0]
        src, dst = (edge_index[0], edge_index[1])
        node2edge = node_rep[src] + node_rep[dst] + edge_attr
        node2edge = jax.nn.relu(node2edge)
        node_new = jax.ops.segment_sum(node2edge, src, num_segments=N) + jax.ops.segment_sum(node2edge, dst, num_segments=N)
        h = node_new + (1.0 + epsilon) * node_rep
        h = jax.nn.relu(_batchnorm(h @ W1, gamma1, beta1))
        h = jax.nn.relu(_batchnorm(h @ W2, gamma2, beta2))
        return h
    edge_index = jnp.stack([src, dst])
    h = jnp.maximum(_layernorm(x, axis=-1), 0.0)
    x = x + _L0_gnn_ref(h, edge_weight, L0_gnn_ln_scale, L0_gnn_ln_bias, L0_gnn_conv_w, L0_gnn_conv_b, L0_gnn_post_w, L0_gnn_post_b, edge_index)
    h = jnp.maximum(_layernorm(x, axis=-1), 0.0)
    x = x + _L1_gnn_ref(h, edge_index, edge_weight, L1_gnn_node_lock, L1_gnn_W, L1_gnn_b)
    h = jnp.maximum(_layernorm(x, axis=-1), 0.0)
    x = x + _L2_gnn_ref(h, L2_gnn_basis1, L2_gnn_comp1, L2_gnn_loop_w1, L2_gnn_bias1, L2_gnn_basis2, L2_gnn_comp2, L2_gnn_loop_w2, L2_gnn_bias2, L2_gnn_ln_g, L2_gnn_ln_b, edge_weight, L2_gnn_current_time, src, dst, edge_type_240)
    h = jnp.maximum(_layernorm(x, axis=-1), 0.0)
    x = x + _L3_gnn_ref(h, edge_attr_256, edge_index, L3_gnn_W1, L3_gnn_gamma1, L3_gnn_beta1, L3_gnn_W2, L3_gnn_gamma2, L3_gnn_beta2, L3_gnn_epsilon)
    return x

_drawn_inputs = setup_inputs


def setup_inputs(seed=0):
    import zlib

    import numpy as np

    out = dict(_drawn_inputs(seed))
    spreads = {'L0_gnn_ln_scale': (1.0, 0.2),
     'L0_gnn_ln_bias': (0.0, 0.277),
     'L0_gnn_conv_b': (0.0, 0.1),
     'L0_gnn_post_b': (0.0, 0.1),
     'L2_gnn_bias1': (0.0, 0.1),
     'L2_gnn_bias2': (0.0, 0.1),
     'L2_gnn_ln_g': (1.0, 0.2),
     'L2_gnn_ln_b': (0.0, 0.1),
     'L3_gnn_gamma1': (1.0, 0.2),
     'L3_gnn_beta1': (0.0, 0.328),
     'L3_gnn_gamma2': (1.0, 0.2),
     'L3_gnn_beta2': (0.0, 0.302)}
    factors = {'L1_gnn_b': 6.924}
    for name, (base, spread) in spreads.items():
        noise = np.random.default_rng([zlib.crc32(name.encode()), seed]).standard_normal(out[name].shape)
        drawn = base * np.exp(spread * noise) if base else spread * noise
        out[name] = jnp.asarray(drawn.astype(out[name].dtype))
    for name, factor in factors.items():
        out[name] = (out[name] * factor).astype(out[name].dtype)
    return out
```

```python
import numpy as np
import concourse.bass as bass
from concourse import mybir
from contextlib import ExitStack

F32, BF16, I32, U32 = mybir.dt.float32, mybir.dt.bfloat16, mybir.dt.int32, mybir.dt.uint32
ACT = mybir.ActivationFunctionType
ALU = mybir.AluOpType

P = 128
N, D, E = 18870, 256, 9435
NT = -(-N // P)
NP = NT * P
NC = -(-E // P)
EP = NC * P
KT = 4
KC = 2
NODE_STEPS = NT // KT
EDGE_STEPS = NC // KC
ZROW = EP
LAST_NODES = N - (NT - 1) * P
LAST_EDGES = E - (NC - 1) * P
PAD_KEY = NP - 1
NO_KEY = 1 << 20
LOCKS = 1000
LC = -(-LOCKS // P)
REC = 8
R_SRC, R_DST, R_W, R_TYPE, R_EID, R_RANKS, R_MAPS, R_LOCK = range(REC)
EPS = 1e-5


def run_steps(eng, n, stages, unroll=2):
    deep = max(lag for lag, _ in stages)
    head = deep + unroll + -deep % unroll
    tail = n - 1 - (n - 1 - head) % unroll
    for s in range(head):
        for lag, fn in stages:
            if s >= lag:
                fn(s - lag, (s - lag) % unroll)
    if tail > head:
        with eng.Fori(0, (tail - head) // unroll) as turn:
            for j in range(unroll):
                for lag, fn in stages:
                    fn(turn * unroll + (head + j - lag), (j - lag) % unroll)
    else:
        tail = head
    for s in range(tail, n + deep):
        for lag, fn in stages:
            if 0 <= s - lag < n:
                fn(s - lag, (s - lag) % unroll)


def last_step(s, n):
    return isinstance(s, int) and s == n - 1


def first(s, k):
    return isinstance(s, int) and s < k


def settle(eng, C, s):
    if not isinstance(s, int):
        eng.sem_inc(C.passed, 1)


def wait_apart(eng, C, *waits):
    for sem, value in waits:
        eng.wait_ge(sem, value)
    settle(eng, C, waits[-1][1])


def landed(s, r, n=1, ring=2):
    return (s - r) * (16 * n // ring) + 16 * n


class Mem:

    def __init__(self, nc, ctx, clear=True):
        self.nc, self.ctx, self.clear = nc, ctx, clear
        self.numbers = []
        if clear:
            ctx.callback(self.zero)

    def zero(self):
        numbers = sorted(self.numbers)
        while numbers:
            n = 1
            while n < len(numbers) and numbers[n] == numbers[0] + n:
                n += 1
            self.nc.sync.sem_clear(range(numbers[0], numbers[0] + n))
            numbers = numbers[n:]

    def sb(self, name, shape, dt=F32):
        return self.ctx.enter_context(self.nc.sbuf_tensor(name, shape, dt))

    def ps(self, name, shape, dt=F32):
        return self.ctx.enter_context(self.nc.psum_tensor(name, shape, dt))

    def sem(self, name):
        handle = self.ctx.enter_context(self.nc.semaphore(name))
        self.numbers.append(handle.num)
        return handle

    def dram(self, name, shape, dt=F32):
        return self.nc.dram_tensor(name, shape, dt).ap()


def make_constants(nc, C):
    with ExitStack() as ctx:
        s = Mem(nc, ctx).sem("const_made")
        t = Mem(nc, ctx).sem("const_cast")
        iota_i = Mem(nc, ctx).sb("iota_i", [P, NT], I32)
        part_i = Mem(nc, ctx).sb("part_i", [P, 1], I32)
        with nc.Block() as block:
            @block.gpsimd
            def _(pool):
                nc.gpsimd.memset(C.ones[:, :], 1.0).then_inc(s, 1)
                nc.gpsimd.memset(C.eps[:, :], EPS).then_inc(s, 1)
                nc.gpsimd.iota(iota_i[:, :], pattern=[[1, NT]], base=0, channel_multiplier=0).then_inc(s, 1)
                nc.gpsimd.iota(part_i[:, :], pattern=[[0, 1]], base=0, channel_multiplier=1).then_inc(s, 1)
                pool.wait_ge(s, 4)
                nc.gpsimd.memset(C.ident[:, :], 0.0).then_inc(s, 1)
                pool.wait_ge(s, 5)
                nc.gpsimd.affine_select(out=C.ident[:, :], in_=C.ident[:, :], compare_op=ALU.not_equal, fill=1.0,
                                        base=0, pattern=[[-1, P]], channel_multiplier=1).then_inc(s, 1)
                nc.gpsimd.affine_select(out=C.upper[:, :], in_=C.ones[:, :], compare_op=ALU.is_gt, fill=0.0,
                                        base=0, pattern=[[1, P]], channel_multiplier=-1).then_inc(s, 1)
                nc.gpsimd.affine_select(out=C.lower[:, :], in_=C.ones[:, :], compare_op=ALU.is_gt, fill=0.0,
                                        base=0, pattern=[[-1, P]], channel_multiplier=1).then_inc(s, 1)
                nc.gpsimd.affine_select(out=C.node_ok[:, :], in_=C.ones[:, 0:1], compare_op=ALU.is_gt, fill=0.0,
                                        base=LAST_NODES, pattern=[[0, 1]], channel_multiplier=-1).then_inc(s, 1)
                nc.gpsimd.affine_select(out=C.edge_ok[:, :], in_=C.ones[:, 0:1], compare_op=ALU.is_gt, fill=0.0,
                                        base=LAST_EDGES, pattern=[[0, 1]], channel_multiplier=-1).then_inc(s, 1)

            @block.vector
            def _(dve):
                dve.wait_ge(s, 4)
                nc.vector.tensor_copy(C.iota[:, :], iota_i[:, :]).then_inc(t, 1)
                nc.vector.tensor_copy(C.part[:, :], part_i[:, :]).then_inc(t, 1)
                dve.wait_ge(t, 1)
                nc.vector.tensor_scalar(C.chunk0[:, :], C.iota[:, :], float(P), None, ALU.mult).then_inc(t, 1)


def index_nodes(nc, C, cols_in, rec_d, rec_s):
    with ExitStack() as ctx:
        m = Mem(nc, ctx)
        NK = 2 * NC + LC
        keys = m.sb("keys", [P, NK], I32)
        parts_i = m.sb("parts_i", [P, 2, NK], I32)
        code = m.sb("code", [P, NK, 3])
        oh_lo = m.sb("oh_lo", [P, 2, KC, P], BF16)
        oh_hi = m.sb("oh_hi", [P, 2, KC, NT], BF16)
        count = [m.sb(f"count{k}", [P, NT]) for k in range(3)]
        scan = [[m.sb(f"scan{k}{j}", [P, NT]) for j in range(2)] for k in range(2)]
        found = m.sb("found", [P, NT])
        start = [m.sb(f"start{k}", [P, NT]) for k in range(2)]
        slot = [m.sb(f"slot{k}", [P, NT]) for k in range(2)]
        tab = m.sb("tab", [P, 2, 2, 2, NT])
        Hp, Sp = C.bank[0:3], C.bank[3:5]
        loaded, split, coded, counted = m.sem("keys_loaded"), m.sem("keys_split"), m.sem("codes_made"), m.sem("codes_counted")
        small, summed = m.sem("table_steps"), m.sem("table_sums")
        groups = [(0, NC, 0), (NC, NC, 1), (2 * NC, LC, 2)]
        with nc.Block() as block:
            @block.sync
            def _(sp):
                sp.dma_start(keys[:, :], cols_in["keys"]).then_inc(loaded, 16)

            @block.vector
            def _(dve):
                dve.wait_ge(loaded, 16)
                nc.vector.tensor_scalar(parts_i[:, 0, :], keys[:, :], P - 1, None, ALU.bitwise_and).then_inc(split, 1)
                nc.vector.tensor_scalar(parts_i[:, 1, :], keys[:, :], 7, None, ALU.arith_shift_right).then_inc(split, 1)
                dve.wait_ge(split, 2)
                nc.vector.tensor_copy(code[:, :, 0], keys[:, :]).then_inc(split, 1)
                nc.vector.tensor_copy(code[:, :, 1], parts_i[:, 0, :]).then_inc(split, 1)
                nc.vector.tensor_copy(code[:, :, 2], parts_i[:, 1, :]).then_inc(split, 1)
                dve.wait_ge(split, 5)
                done = 0
                for col, n, t in groups:
                    def codes(s, par, col=col, done=done):
                        if not first(s, 2):
                            dve.wait_ge(counted, s * KC + (done - KC))
                        elif done:
                            dve.wait_ge(counted, done)
                        for j in range(KC):
                            c = s * KC + (col + j)
                            nc.vector.tensor_scalar(oh_lo[:, par, j, :], C.iota[:, 0:P], code[:, bass.ds(c, 1), 1],
                                                    None, ALU.is_equal).then_inc(coded, 1)
                            nc.vector.tensor_scalar(oh_hi[:, par, j, :], C.iota[:, :], code[:, bass.ds(c, 1), 2],
                                                    None, ALU.is_equal).then_inc(coded, 1)
                    run_steps(dve, n // KC, [(0, codes)])
                    done += n
                dve.wait_ge(counted, done)
                for k in range(3):
                    nc.vector.tensor_copy(count[k][:, :], Hp[k][:, 0:NT]).then_inc(small, 1)

            @block.tensor
            def _(pe):
                done = 0
                for col, n, t in groups:
                    def tally(s, par, done=done, n=n, t=t):
                        for j in range(KC):
                            pe.wait_ge(coded, s * (2 * KC) + (2 * done + 2 * j + 2))
                            nc.tensor.matmul(Hp[t][:, 0:NT], oh_lo[:, par, j, :], oh_hi[:, par, j, :],
                                             start=first(s, 1) and j == 0,
                                             stop=isinstance(s, int) and s == n // KC - 1 and j == KC - 1
                                             ).then_inc(counted, 1)
                    run_steps(pe, n // KC, [(0, tally)])
                    done += n
        with nc.Block() as block:
            @block.tensor
            def _(pe):
                for k in range(2):
                    nc.tensor.matmul(Sp[k][:, 0:NT], C.upper[:, :], count[k][:, :], start=True, stop=True).then_inc(summed, 1)
                    nc.tensor.matmul(Sp[k][:, NT:2 * NT], C.ones[:, :], count[k][:, :], start=True, stop=True).then_inc(summed, 1)

            @block.vector
            def _(dve):
                n = [3]

                def link(ins):
                    ins.then_inc(small, 1)
                    n[0] += 1
                    dve.wait_ge(small, n[0])

                for k in range(2):
                    dve.wait_ge(summed, 2 * k + 2)
                    a, b = scan[k]
                    link(nc.vector.memset(a[:, :], 0.0))
                    link(nc.vector.tensor_copy(a[:, 1:NT], Sp[k][:, NT:2 * NT - 1]))
                    sh = 1
                    while sh < NT:
                        link(nc.vector.tensor_copy(b[:, 0:sh], a[:, 0:sh]))
                        link(nc.vector.tensor_tensor(b[:, sh:NT], a[:, sh:NT], a[:, 0:NT - sh], ALU.add))
                        a, b = b, a
                        sh *= 2
                    link(nc.vector.tensor_tensor(start[k][:, :], a[:, :], Sp[k][:, 0:NT], ALU.add))
                    link(nc.vector.tensor_scalar(found[:, :], count[k][:, :], 0.0, None, ALU.is_gt))
                    link(nc.vector.tensor_tensor(found[:, NT - 1:NT], found[:, NT - 1:NT], C.node_ok[:, :], ALU.mult))
                    link(nc.vector.tensor_tensor(slot[k][:, :], start[k][:, :], count[k][:, :], ALU.add))
                    link(nc.vector.tensor_scalar(slot[k][:, :], slot[k][:, :], -1.0 - ZROW, None, ALU.add))
                    link(nc.vector.tensor_tensor(slot[k][:, :], slot[k][:, :], found[:, :], ALU.mult))
                    link(nc.vector.tensor_scalar(slot[k][:, :], slot[k][:, :], float(ZROW), None, ALU.add))
                    link(nc.vector.tensor_copy(C.slot_of[k][:, :], slot[k][:, :]))
                for par in range(2):
                    link(nc.vector.tensor_scalar(tab[:, par, 0, 1, :], count[2][:, :], 0.0, None, ALU.is_gt))
                    link(nc.vector.tensor_copy(tab[:, par, 1, 1, :], slot[0][:, :]))
                for k in range(2):
                    link(nc.vector.tensor_copy(tab[:, 0, k, 0, :], start[k][:, :]))

        key = m.sb("key", [P, 2, 2, 3])
        hot = m.sb("hot", [P, 2, 2, P])
        lo1 = m.sb("lo1", [P, 2, 2, P], BF16)
        hi1 = m.sb("hi1", [P, 2, 2, NT], BF16)
        junk = m.sb("junk", [P, 3, NT])
        before = m.sb("before", [P, 2, 2, 4])
        rank = m.sb("rank", [P, 2, 2], U32)
        rec = m.sb("rec", [P, 2, REC], I32)
        recs = m.sb("recs", [P, NC, 4], I32)
        bc = [b[:, 0:2 * P].rearrange("p (f e) -> p f e", f=2) for b in C.bank[2:4]]
        got, run = C.bank[6:8], C.bank[0:2]
        keyed, shown, hotted, looked, noted = m.sem("key_copied"), m.sem("key_shown"), m.sem("hot_made"), m.sem("looked_up"), m.sem("slot_steps")
        upd, tabbed, packed, put, rld = m.sem("table_added"), m.sem("table_ready"), m.sem("record_packed"), [C.mem.sem(f"record_put{j}") for j in range(2)], m.sem("fields_loaded")
        coded2 = m.sem("codes_again")
        with nc.Block() as block:
            @block.sync
            def _(sp):
                sp.dma_start(recs[:, :, :], cols_in["fields"]).then_inc(rld, 16)

            @block.vector
            def _(dve):
                def prepare(s, par):
                    if not first(s, 2):
                        dve.wait_ge(upd, s * 2 + (-2))
                        dve.wait_ge(noted, s * 8 + (-8))
                    for k in range(2):
                        nc.vector.tensor_copy(key[:, par, k, :], code[:, bass.ds(s + k * NC, 1), :]).then_inc(keyed, 1)
                    for k in range(2):
                        dve.wait_ge(keyed, s * 2 + (k + 1))
                        nc.vector.tensor_scalar(lo1[:, par, k, :], C.iota[:, 0:P], key[:, par, k, 1:2], None,
                                                ALU.is_equal).then_inc(coded2, 1)
                        nc.vector.tensor_scalar(hi1[:, par, k, :], C.iota[:, :], key[:, par, k, 2:3], None,
                                                ALU.is_equal).then_inc(coded2, 1)

                def place(s, par):
                    for k in range(2):
                        dve.wait_ge(shown, s * 4 + (2 * k + 2))
                        nc.vector.tensor_scalar(hot[:, par, k, :], bc[k][:, 1, :], C.part[:, 0:1], None,
                                                ALU.is_equal).then_inc(hotted, 1)
                        nc.vector.scalar_tensor_tensor(out=junk[:, k, 0:P], in0=bc[k][:, 0, :],
                                                       scalar=key[:, par, k, 0:1], in1=C.lower[:, :],
                                                       op0=ALU.is_equal, op1=ALU.mult,
                                                       accum_out=before[:, par, k, 0:1]).then_inc(noted, 1)
                    for k in range(2):
                        dve.wait_ge(looked, s * 2 + (k + 1))
                        for f in range(2):
                            dve.wait_ge(noted, s * 8 + (2 + 3 * k + f))
                            nc.vector.scalar_tensor_tensor(out=junk[:, 2, :], in0=C.iota[:, :],
                                                           scalar=key[:, par, k, 2:3],
                                                           in1=got[k][:, f * NT:(f + 1) * NT],
                                                           op0=ALU.is_equal, op1=ALU.mult,
                                                           accum_out=before[:, par, k, 1 + f:2 + f]).then_inc(noted, 1)
                        dve.wait_ge(noted, s * 8 + (2 + 3 * k + 2))
                        if k == 0 and not first(s, 2):
                            dve.wait_ge(put[par], landed(s - 2, par, 2))
                        nc.vector.tensor_tensor(rank[:, par, k:k + 1], before[:, par, k, 0:1], before[:, par, k, 1:2],
                                                ALU.add).then_inc(noted, 1)
                    nc.vector.tensor_copy(rec[:, par, 0:4], recs[:, bass.ds(s, 1), :]).then_inc(packed, 1)
                    nc.vector.tensor_scalar(rec[:, par, R_EID:R_EID + 1], C.part[:, :], C.chunk0[:, bass.ds(s, 1)],
                                            None, ALU.add).then_inc(packed, 1)
                    nc.vector.tensor_tensor(rec[:, par, R_RANKS:R_RANKS + 1], before[:, par, 1, 0:1],
                                            before[:, par, 1, 1:2], ALU.add).then_inc(packed, 1)
                    nc.vector.tensor_copy(rec[:, par, R_MAPS:R_MAPS + 1], before[:, par, 1, 2:3]).then_inc(packed, 1)
                    nc.vector.tensor_copy(rec[:, par, R_LOCK:R_LOCK + 1], before[:, par, 0, 2:3]).then_inc(packed, 1)

                def table(s, par):
                    for k in range(2):
                        dve.wait_ge(upd, s * 2 + (k + 1))
                        if not first(s, 1):
                            dve.wait_ge(tabbed, s * 2)
                        nc.vector.tensor_tensor(tab[:, 1 - par, k, 0, :], tab[:, par, k, 0, :], run[k][:, 0:NT],
                                                ALU.add).then_inc(tabbed, 1)

                dve.wait_ge(rld, 16)
                run_steps(dve, NC, [(0, prepare), (0, place), (0, table)])

            @block.tensor
            def _(pe):
                def look(s, par):
                    for k in range(2):
                        pe.wait_ge(keyed, s * 2 + (k + 1))
                        if not first(s, 1):
                            pe.wait_ge(noted, s * 8)
                        for f in range(2):
                            nc.tensor.transpose(bc[k][:, f, :], key[:, par, k, f:f + 1].broadcast_to([P, P]),
                                                C.ident[:, :]).then_inc(shown, 1)
                    for k in range(2):
                        pe.wait_ge(hotted, s * 2 + (k + 1))
                        if not first(s, 1):
                            pe.wait_ge(tabbed, s * 2)
                        nc.tensor.matmul(got[k][:, 0:2 * NT], hot[:, par, k, :],
                                         tab[:, par, k, :, :].rearrange("p f t -> p (f t)"),
                                         start=True, stop=True).then_inc(looked, 1)
                    for k in range(2):
                        pe.wait_ge(coded2, s * 4 + (2 * k + 2))
                        nc.tensor.matmul(run[k][:, 0:NT], lo1[:, par, k, :], hi1[:, par, k, :],
                                         start=True, stop=True).then_inc(upd, 1)
                run_steps(pe, NC, [(0, look)])

            @block.gpsimd
            def _(pool):
                def scatter(s, par):
                    wait_apart(pool, C, (packed, s * 5 + 5), (noted, s * 8 + 8))
                    for k, table in enumerate((rec_d, rec_s)):
                        nc.gpsimd.indirect_dma_start(
                            out=table, out_offset=bass.IndirectOffsetOnAxis(ap=rank[:, par, k:k + 1], axis=0),
                            in_=rec[:, par, :], in_offset=None).then_inc(put[par], 16)
                run_steps(pool, NC, [(0, scatter)])
                for par in range(2):
                    pool.wait_ge(put[par], landed(NC - 2 + par, par, 2))


def rows(table, s, k):
    return table[bass.ds(s * (k * P), k * P), :].rearrange("(j p) d -> p j d", p=P)


def all_landed(eng, sems, n, k=1):
    for par in range(2):
        last = n - 1 - (n - 1 - par) % 2
        eng.wait_ge(sems[par], landed(last, par, k))


def spread(row, k):
    return row[:, :].rearrange("p (o d) -> p o d", o=1).broadcast_to([P, k, D])


class Norm:

    def __init__(self, m, C, name, K):
        self.C, self.K = C, K
        self.st = m.sb(f"{name}_st", [P, 2, K, 6])
        self.mv = m.sb(f"{name}_mv", [P, 2, K, 2])
        self.sd = m.sb(f"{name}_sd", [P, 2, K])
        self.scale = m.sb(f"{name}_scale", [P, 2, K])
        self.bias = m.sb(f"{name}_bias", [P, 2, K])
        self.sampled, self.averaged = m.sem(f"{name}_sampled"), m.sem(f"{name}_averaged")
        self.rooted, self.scaled, self.ready = m.sem(f"{name}_rooted"), m.sem(f"{name}_scaled"), m.sem(f"{name}_ready")

    def stats(self, nc, dve, s, par, tile):
        K = self.K
        settle(dve, self.C, s)
        for k in range(K):
            nc.vector.bn_stats(self.st[:, par, k, :], tile[:, k, :]).then_inc(self.sampled, 1)
        wait_apart(dve, self.C, (self.sampled, s * K + K))
        for k in range(K):
            ins = nc.vector.bn_aggr(self.mv[:, par, k, :], self.st[:, par, k, :])
        ins.then_inc(self.averaged, 1)

    def root(self, nc, act, s, par):
        act.wait_ge(self.averaged, s + 1)
        nc.scalar.activation(self.sd[:, par, :], self.mv[:, par, :, 1], ACT.Sqrt,
                             bias=self.C.eps[:, 0:1]).then_inc(self.rooted, 1)

    def finish(self, nc, dve, s, par):
        dve.wait_ge(self.rooted, s + 1)
        nc.vector.reciprocal(self.scale[:, par, :], self.sd[:, par, :]).then_inc(self.scaled, 1)
        dve.wait_ge(self.scaled, s + 1)
        nc.vector.scalar_tensor_tensor(out=self.bias[:, par, :], in0=self.mv[:, par, :, 0], scalar=-1.0,
                                       in1=self.scale[:, par, :], op0=ALU.mult, op1=ALU.mult).then_inc(self.ready, 1)

    def apply(self, nc, s, par, out, tile, func):
        for k in range(self.K):
            ins = nc.scalar.activation(out[:, k, :], tile[:, k, :], func, bias=self.bias[:, par, k:k + 1],
                                       scale=self.scale[:, par, k:k + 1])
        return ins


def sort_tables(nc, C, A, rec_d, rec_s):
    with ExitStack() as ctx:
        m = Mem(nc, ctx)
        keycol = m.sb("keycol", [P, 2, NC])
        kcol = m.sb("kcol", [P, 2, 2])
        shared = m.sb("shared", [P, 2, NC])
        row0 = m.sb("row0", [P, P])
        same_s = m.sb("same_s", [P, 2, P], BF16)
        skey = m.sb("skey", [P, NC], I32)
        last_key = m.sb("last_key", [P, 2])
        fix = m.sb("fix", [P, 2, 2])
        comp = m.sb("comp", [P, 2, 20])
        tidx = m.sb("tidx", [P, 2, 1], U32)
        decay = m.sb("decay", [P, NC]); dmax = m.sb("dmax", [P, 4]); now = m.sb("now", [P, 1])
        top = m.sb("top", [1, P])
        loaded, cast, kept, shown, made = (m.sem(x) for x in ("rec_loaded", "rec_cast", "key_kept", "keys_shown", "same_made"))
        ends, fixed, timed, expd, prod = (m.sem(x) for x in ("chunk_ends", "fix_steps", "decay_steps", "decay_exp", "coef_made"))
        idxed = m.sem("type_copied"); got = [C.mem.sem(f"comp_got{j}") for j in range(2)]
        peeked = m.sem("max_moved")
        with nc.Block() as block:
            @block.sync
            def _(sp):
                sp.dma_start(C.rec[:, :, :], rec_d.rearrange("(c p) k -> p c k", p=P)).then_inc(loaded, 16)
                sp.dma_start(skey[:, :], rec_s[:, R_SRC].rearrange("(c p) -> p c", p=P),
                             allow_slow_non_contiguous=True).then_inc(loaded, 16)
                sp.dma_start(now[:, :], A["now"].broadcast_to([P, 1])).then_inc(loaded, 16)

            @block.vector
            def _(dve):
                dve.wait_ge(loaded, 48)
                nc.vector.tensor_copy(keycol[:, 0, :], C.rec[:, :, R_DST]).then_inc(cast, 1)
                nc.vector.tensor_copy(keycol[:, 1, :], skey[:, :]).then_inc(cast, 1)
                nc.vector.tensor_copy(C.src_keys[:, :], skey[:, :]).then_inc(cast, 1)
                nc.vector.tensor_copy(C.weight[:, :], C.rec[:, :, R_W].bitcast(F32)).then_inc(cast, 1)
                nc.vector.memset(row0[:, :], 0.0).then_inc(cast, 1)
                dve.wait_ge(cast, 5)
                nc.vector.memset(row0[0:1, :], 1.0).then_inc(cast, 1)
                nc.vector.tensor_tensor(C.lock[:, :], C.rec[:, :, R_SRC], C.rec[:, :, R_DST], ALU.is_equal).then_inc(cast, 1)
                nc.vector.tensor_copy(decay[:, :], C.rec[:, :, R_LOCK]).then_inc(cast, 1)
                dve.wait_ge(cast, 8)
                nc.vector.tensor_tensor(C.lock[:, :], C.lock[:, :], decay[:, :], ALU.max).then_inc(cast, 1)
                dve.wait_ge(cast, 9)

                n = [0]

                def link(ins):
                    ins.then_inc(timed, 1)
                    n[0] += 1
                    dve.wait_ge(timed, n[0])

                link(nc.vector.tensor_scalar(decay[:, :], C.weight[:, :], now[:, 0:1], -1.0, ALU.subtract, ALU.mult))
                link(nc.vector.tensor_scalar(decay[:, :], decay[:, :], 0.0, None, ALU.max))
                link(nc.vector.tensor_tensor(decay[:, NC - 1:NC], decay[:, NC - 1:NC], C.edge_ok[:, :], ALU.mult))
                link(nc.vector.reduce_max(dmax[:, 0:1], decay[:, :], mybir.AxisListType.X))
                dve.wait_ge(peeked, 1)
                link(nc.vector.reduce_max(dmax[0:1, 1:2], C.bank[7][0:1, 0:P], mybir.AxisListType.X))
                link(nc.vector.tensor_scalar(dmax[0:1, 1:2], dmax[0:1, 1:2], 1e-8, None, ALU.add))
                link(nc.vector.tensor_scalar(top[:, :], C.ones[0:1, :], dmax[0:1, 1:2], None, ALU.mult))
                dve.wait_ge(peeked, 2)
                link(nc.vector.reciprocal(dmax[:, 2:3], C.bank[7][:, 128:129]))
                link(nc.vector.tensor_scalar(decay[:, :], decay[:, :], dmax[:, 2:3], -0.1, ALU.mult, ALU.mult))
                dve.wait_ge(expd, 1)

                def keep(s, par):
                    if not first(s, 2):
                        dve.wait_ge(made, s * 2 + (-2))
                    nc.vector.tensor_copy(kcol[:, par, :], keycol[:, :, bass.ds(s, 1)]).then_inc(kept, 1)

                def compare(s, par):
                    for k, same in enumerate((C.same_d[:, bass.ds(s * P, P)], same_s[:, par, :])):
                        dve.wait_ge(shown, s * 2 + (k + 1))
                        nc.vector.tensor_scalar(same, C.bank[2 * k + par][:, 0:P],
                                                kcol[:, par, k:k + 1], None, ALU.is_equal, ALU.add,
                                                accum_out=shared[:, k, bass.ds(s, 1)]).then_inc(made, 1)

                def weigh(s, par):
                    dve.wait_ge(got[par], landed(s, par))
                    nc.vector.tensor_scalar(C.coef[:, bass.ds(s, 1), :].rearrange("p o k -> p (o k)"), comp[:, par, :],
                                            C.decay[:, bass.ds(s, 1)], None, ALU.mult).then_inc(prod, 1)
                run_steps(dve, NC, [(1, compare), (1, weigh), (0, keep)])
                n = [0]

                def link2(ins):
                    ins.then_inc(fixed, 1)
                    n[0] += 1
                    dve.wait_ge(fixed, n[0])

                dve.wait_ge(ends, 1)
                for k in range(2):
                    link2(nc.vector.tensor_copy(last_key[0:NC, k:k + 1], C.bank[6][0:NC, 2 * k:2 * k + 1]))
                    link2(nc.vector.scalar_tensor_tensor(out=C.carry[k][0:NC, :], in0=C.bank[5][0:NC, k * NC:(k + 1) * NC],
                                                         scalar=last_key[0:NC, k:k + 1], in1=C.upper[0:NC, 0:NC],
                                                         op0=ALU.is_equal, op1=ALU.mult))
                    link2(nc.vector.tensor_scalar(fix[0:NC, k, 0:1], C.part[0:NC, :], float(P), -1.0, ALU.mult, ALU.add))
                    link2(nc.vector.tensor_tensor(C.fix_row[k][0:NC, :], fix[0:NC, k, 0:1], C.bank[6][0:NC, 2 * k + 1:2 * k + 2], ALU.add))

            @block.scalar
            def _(act):
                act.wait_ge(timed, 9)
                nc.scalar.activation(C.decay[:, :], decay[:, :], ACT.Exp).then_inc(expd, 1)

            @block.gpsimd
            def _(pool):
                pool.wait_ge(loaded, 48)

                def fetch(s, par):
                    if not first(s, 2):
                        pool.wait_ge(prod, s + (-1))
                    nc.gpsimd.tensor_copy(tidx[:, par, :], C.rec[:, bass.ds(s, 1), R_TYPE].bitcast(U32)).then_inc(idxed, 1)
                    wait_apart(pool, C, (idxed, s + 1))
                    nc.gpsimd.indirect_dma_start(out=comp[:, par, :], out_offset=None, in_=A["comp"],
                                                 in_offset=bass.IndirectOffsetOnAxis(ap=tidx[:, par, :], axis=0)
                                                 ).then_inc(got[par], 16)
                run_steps(pool, NC, [(0, fetch)])

            @block.tensor
            def _(pe):
                pe.wait_ge(timed, 4)
                nc.tensor.transpose(C.bank[7][0:1, 0:P], dmax[:, 0:1], C.ident[:, :]).then_inc(peeked, 1)
                pe.wait_ge(timed, 7)
                nc.tensor.matmul(C.bank[7][:, 128:129], top[:, :], C.ones[0:1, 0:1], start=True, stop=True).then_inc(peeked, 1)

                def show(s, par):
                    pe.wait_ge(kept, s + 1)
                    for k in range(2):
                        nc.tensor.transpose(C.bank[2 * k + par][:, 0:P], kcol[:, par, k:k + 1].broadcast_to([P, P]),
                                            C.ident[:, :]).then_inc(shown, 1)
                run_steps(pe, NC, [(0, show)])
                pe.wait_ge(made, 2 * NC)
                for k in range(2):
                    nc.tensor.matmul(C.bank[5][:, k * NC:(k + 1) * NC], row0[:, :], keycol[:, k, :], start=True, stop=True)
                    nc.tensor.matmul(C.bank[6][0:NC, 2 * k:2 * k + 1], keycol[:, k, :], C.ident[:, P - 1:P], start=True, stop=True)
                    ins = nc.tensor.matmul(C.bank[6][0:NC, 2 * k + 1:2 * k + 2], shared[:, k, :], C.ident[:, 0:1], start=True, stop=True)
                ins.then_inc(ends, 1)


def carry_over(nc, C, tag, k, table, bias):
    with ExitStack() as ctx:
        m = Mem(nc, ctx)
        tail = m.sb(f"{tag}_tail", [P, D])
        more = m.sb(f"{tag}_more", [P, D])
        read, plain, summed, copied, zero = (m.sem(f"{tag}_{x}") for x in ("tail_read", "tail_plain", "carry_summed", "carry_copied", "zrow_put"))
        added = C.mem.sem(f"{tag}_carry_added")
        with nc.Block() as block:
            @block.sync
            def _(sp):
                sp.dma_start(tail[0:NC, :], table[0:EP, :].rearrange("(c p) d -> p c d", p=P)[P - 1]).then_inc(read, 16)
                sp.dma_start(table[ZROW:ZROW + 1, :], bias[0:1, :]).then_inc(zero, 16)
                sp.wait_ge(zero, 16)

            @block.vector
            def _(dve):
                dve.wait_ge(read, 16)
                nc.vector.tensor_tensor(tail[0:NC, :], tail[0:NC, :], bias[0:NC, :], ALU.subtract).then_inc(plain, 1)
                dve.wait_ge(summed, 1)
                nc.vector.tensor_copy(more[0:NC, :], C.bank[0][0:NC, 0:D]).then_inc(copied, 1)

            @block.tensor
            def _(pe):
                pe.wait_ge(plain, 1)
                nc.tensor.matmul(C.bank[0][0:NC, 0:D], C.carry[k][0:NC, :], tail[0:NC, :], start=True, stop=True).then_inc(summed, 1)

            @block.gpsimd
            def _(pool):
                pool.wait_ge(copied, 1)
                nc.gpsimd.indirect_dma_start(out=table, out_offset=bass.IndirectOffsetOnAxis(ap=C.fix_row[k][0:NC, :], axis=0),
                                             in_=more[0:NC, :], in_offset=None, compute_op=ALU.add).then_inc(added, 16)
                pool.wait_ge(added, 16)


def load_all(nc, C, tag, pairs):
    with ExitStack() as ctx:
        s = Mem(nc, ctx).sem(f"{tag}_loaded")
        with nc.Block() as block:
            @block.sync
            def _(sp):
                for dst, src in pairs:
                    sp.dma_start(dst, src).then_inc(s, 16)
                sp.wait_ge(s, 16 * len(pairs))


def l0_layer(nc, C, A, i, table, prev, Y):
    with ExitStack() as ctx:
        m = Mem(nc, ctx)
        tag = f"l0_{i}"
        bias, lnb, lns = (m.sb(f"{tag}_{x}", [P, D]) for x in ("bias", "lnb", "lns"))
        W = m.sb(f"{tag}_W", [P, 2, D])
        load_all(nc, C, tag, [(bias[:, :], A["l0_cb"][i:i + 1, :].broadcast_to([P, D])),
                              (lnb[:, :], A["l0_lb"][i:i + 1, :].broadcast_to([P, D])),
                              (lns[:, :], A["l0_ls"][i:i + 1, :].broadcast_to([P, D])), (W[:, :, :], A["l0_w"][i].rearrange("(h p) d -> p h d", p=P))])
        idx = m.sb(f"{tag}_idx", [P, 2, KC], U32)
        G = m.sb(f"{tag}_G", [P, 2, KC, D])
        Z = m.sb(f"{tag}_Z", [P, 2, KC, D])
        seg = m.sb(f"{tag}_seg", [P, 2, KC, P])
        aggT = m.sb(f"{tag}_aggT", [P, 2, KC * 2, P])
        res = m.sb(f"{tag}_res", [P, 2, KC, D])
        norm = Norm(m, C, f"{tag}_n", KC)
        first_norm = Norm(m, C, f"{tag}_f", KC) if i == 0 else None
        scaled, idxed, updated, normed, biased, segged, mixed, copied, summed, evac = (
            m.sem(f"{tag}_{x}") for x in ("scaled", "idxed", "updated", "normed", "biased", "segged", "mixed", "copied", "summed", "evac"))
        got = [C.mem.sem(f"{tag}_got{j}") for j in range(2)]
        stored = [m.sem(f"{tag}_stored{j}") for j in range(2)]
        U = 1 if i else 3

        with nc.Block() as block:
            @block.gpsimd
            def _(pool):
                def gather(s, par):
                    if not first(s, 2):
                        pool.wait_ge(updated, s + (-1))
                    nc.gpsimd.tensor_copy(idx[:, par, :], C.rec[:, bass.ds(s * KC, KC), R_MAPS if i else R_SRC].bitcast(U32)
                                          ).then_inc(idxed, 1)
                    wait_apart(pool, C, (idxed, s + 1))
                    for j in range(KC):
                        nc.gpsimd.indirect_dma_start(out=G[:, par, j, :], out_offset=None, in_=prev if i else A["x"],
                                                     in_offset=bass.IndirectOffsetOnAxis(ap=idx[:, par, j:j + 1], axis=0)
                                                     ).then_inc(got[par], 16)

                def add_bias(s, par):
                    pool.wait_ge(scaled, s + 1)
                    nc.gpsimd.tensor_tensor(Z[:, par, :, :], Z[:, par, :, :], spread(lnb, KC), ALU.add).then_inc(biased, 1)
                run_steps(pool, EDGE_STEPS, [(U + 2, add_bias), (0, gather)])

            @block.sync
            def _(sp):
                def store(s, par):
                    wait_apart(sp, C, (evac, s + 1))
                    sp.dma_start(rows(table, s, KC), res[:, par, :, :]).then_inc(stored[par], 16)
                run_steps(sp, EDGE_STEPS, [(0, store)])
                all_landed(sp, stored, EDGE_STEPS)

            @block.vector
            def _(dve):
                def y(s):
                    return Y[:, bass.ds(s * KC, KC), :]

                def update(s, par):
                    dve.wait_ge(got[par], landed(s, par, KC))
                    nc.vector.scalar_tensor_tensor(out=y(s), in0=G[:, par, :, :], scalar=0.0, in1=y(s),
                                                   op0=ALU.max, op1=ALU.add).then_inc(updated, 1)

                def first_stats(s, par):
                    dve.wait_ge(got[par], landed(s, par, KC))
                    first_norm.stats(nc, dve, s, par, G[:, par, :, :])

                def stats(s, par):
                    dve.wait_ge(updated, s + 1)
                    norm.stats(nc, dve, s, par, y(s))

                def scale(s, par):
                    dve.wait_ge(normed, s + 1)
                    nc.vector.tensor_tensor(Z[:, par, :, :], Z[:, par, :, :], spread(lns, KC), ALU.mult).then_inc(scaled, 1)

                def evacuate(s, par):
                    dve.wait_ge(summed, s + 1)
                    if not first(s, 2):
                        dve.wait_ge(stored[par], landed(s - 2, par))
                    nc.vector.tensor_tensor(res[:, par, :, :], C.bank[2 + par][:, :].rearrange("p (j d) -> p j d", j=KC),
                                            spread(bias, KC), ALU.add).then_inc(evac, 1)
                fin = lambda s, par: norm.finish(nc, dve, s, par)
                head = [(1, update)] if i else [(2, lambda s, par: first_norm.finish(nc, dve, s, par)), (1, first_stats)]
                run_steps(dve, EDGE_STEPS, [(U + 4, evacuate), (U + 2, scale), (U + 1, fin)] + ([(U, stats)] + head if i == 0 else head + [(U, stats)]))

            @block.scalar
            def _(act):
                def first_rows(s, par):
                    act.wait_ge(first_norm.ready, s + 1)
                    first_norm.apply(nc, s, par, Y[:, bass.ds(s * KC, KC), :], G[:, par, :, :], ACT.Relu).then_inc(updated, 1)

                def normalise(s, par):
                    if not first(s, 2):
                        act.wait_ge(mixed, s + (-1))
                    for j in range(KC):
                        c = s * KC + j
                        ins = nc.scalar.activation(seg[:, par, j, :], C.same_d[:, bass.ds(c * P, P)], ACT.Copy,
                                                   scale=C.weight[:, bass.ds(c, 1)])
                    ins.then_inc(segged, 1)
                    act.wait_ge(norm.ready, s + 1)
                    norm.apply(nc, s, par, Z[:, par, :, :], Y[:, bass.ds(s * KC, KC), :], ACT.Identity).then_inc(normed, 1)

                def copy(s, par):
                    act.wait_ge(mixed, s + 1)
                    if not first(s, 2):
                        act.wait_ge(summed, s + (-1))
                    nc.scalar.activation(aggT[:, par, :, :], C.bank[par][:, :].rearrange("p (q e) -> p q e", q=2 * KC),
                                         ACT.Copy).then_inc(copied, 1)
                root = lambda s, par: norm.root(nc, act, s, par)
                froot = lambda s, par: first_norm.root(nc, act, s, par)
                run_steps(act, EDGE_STEPS, [(U + 3, copy), (U + 1, normalise), (U, root)] +
                          ([(2, first_rows), (1, froot)] if i == 0 else []))

            @block.tensor
            def _(pe):
                def mix(s, par):
                    pe.wait_ge(biased, s + 1)
                    pe.wait_ge(segged, s + 1)
                    if not first(s, 2):
                        pe.wait_ge(copied, s + (-1))
                    for j in range(KC):
                        for h in range(2):
                            q = 2 * j + h
                            ins = nc.tensor.matmul(C.bank[par][:, q * P:(q + 1) * P], Z[:, par, j, h * P:(h + 1) * P],
                                                   seg[:, par, j, :], start=True, stop=True)
                    ins.then_inc(mixed, 1)

                def convolve(s, par):
                    pe.wait_ge(copied, s + 1)
                    if not first(s, 2):
                        pe.wait_ge(evac, s + (-1))
                    for j in range(KC):
                        for h in range(2):
                            ins = nc.tensor.matmul(C.bank[2 + par][:, j * D:(j + 1) * D], aggT[:, par, 2 * j + h, :],
                                                   W[:, h, :], start=h == 0, stop=h == 1)
                    ins.then_inc(summed, 1)
                run_steps(pe, EDGE_STEPS, [(U + 4, convolve), (U + 3, mix)])


def l0_total(nc, C, tables, total, biases):
    n = EDGE_STEPS
    with ExitStack() as ctx:
        m = Mem(nc, ctx)
        T = m.sb("tot_T", [P, 4, 4, KC, D])
        R = m.sb("tot_R", [P, 4, KC, D])
        zr = m.sb("tot_z", [1, D])
        b = m.sb("tot_b", [1, 4, D])
        added, zsteps, bl, zput = m.sem("tot_added"), m.sem("tot_zsteps"), m.sem("tot_bl"), m.sem("tot_zput")
        read = [m.sem(f"tot_read{j}") for j in range(4)]
        stored = [m.sem(f"tot_stored{j}") for j in range(2)]
        with nc.Block() as block:
            @block.sync
            def _(sp):
                sp.dma_start(b[:, :, :], biases.rearrange("(o i) d -> o i d", o=1)).then_inc(bl, 16)

                def read_sums(s, r):
                    if not first(s, 4):
                        wait_apart(sp, C, (added, s * 4 + (-12)))
                    for i, table in enumerate(tables):
                        sp.dma_start(T[:, r, i, :, :], rows(table, s, KC)).then_inc(read[r], 16)

                def store(s, r):
                    wait_apart(sp, C, (added, s * 4 + 4))
                    sp.dma_start(rows(total, s, KC), R[:, r, :, :]).then_inc(stored[r % 2], 16)
                run_steps(sp, n, [(2, store), (0, read_sums)], 4)
                sp.wait_ge(zsteps, 5)
                sp.dma_start(total[ZROW:ZROW + 1, :], zr[:, :]).then_inc(zput, 16)
                sp.wait_ge(zput, 16)
                all_landed(sp, stored, n)

            @block.vector
            def _(dve):
                dve.wait_ge(bl, 16)
                nc.vector.memset(zr[:, :], 0.0).then_inc(zsteps, 1)
                for i in range(4):
                    dve.wait_ge(zsteps, i + 1)
                    nc.vector.scalar_tensor_tensor(out=zr[:, :], in0=b[:, i, :], scalar=0.0, in1=zr[:, :],
                                                   op0=ALU.max, op1=ALU.add).then_inc(zsteps, 1)

                def add(s, r):
                    dve.wait_ge(read[r], landed(s, r, 4, ring=4))
                    if not first(s, 2):
                        dve.wait_ge(stored[r % 2], landed(s - 2, r % 2))
                    out = R[:, r, :, :]
                    nc.vector.tensor_scalar(out, T[:, r, 0, :, :], 0.0, None, ALU.max).then_inc(added, 1)
                    for i in range(1, 4):
                        dve.wait_ge(added, s * 4 + i)
                        nc.vector.scalar_tensor_tensor(out=out, in0=T[:, r, i, :, :], scalar=0.0, in1=out,
                                                       op0=ALU.max, op1=ALU.add).then_inc(added, 1)
                run_steps(dve, n, [(0, add)], 4)


class NodeStores:

    def __init__(self, C, name, m):
        self.C = C
        self.done = [m.sem(f"{name}{j}") for j in range(2)]

    def put(self, sp, s, r, ready, table, tile):
        wait_apart(sp, self.C, (ready, s + 1))
        sp.dma_start(rows(table, s, KT), tile).then_inc(self.done[r % 2], 16)

    def free(self, eng, s, r):
        if not first(s, 2):
            eng.wait_ge(self.done[r % 2], landed(s - 2, r % 2))

    def finish(self, sp):
        all_landed(sp, self.done, NODE_STEPS)


def gather_sums(nc, pool, s, r, slots, table, G, got):
    for j in range(KT):
        nc.gpsimd.indirect_dma_start(out=G[:, r % 2, j, :], out_offset=None, in_=table,
                                     in_offset=bass.IndirectOffsetOnAxis(ap=slots[:, r % 2, j:j + 1], axis=0)
                                     ).then_inc(got[r % 2], 16)


def copy_slots(nc, C, pool, s, r, slots, slot_of, copied, per=1):
    nc.gpsimd.tensor_copy(slots[:, r % 2, :], slot_of[:, bass.ds(s * KT, KT)]).then_inc(copied, 1)
    wait_apart(pool, C, (copied, s * per + per))


def transpose_tiles(nc, C, banks, tile):
    for h in range(2):
        for k in range(KT):
            ins = nc.tensor.transpose(C.bank[banks + h][:, k * P:(k + 1) * P], tile[:, k, h * P:(h + 1) * P], C.ident[:, :])
    return ins


def project_tiles(nc, C, banks, xT, W):
    for k in range(KT):
        for h in range(2):
            ins = nc.tensor.matmul(C.bank[banks + k // 2][:, (k % 2) * D:(k % 2 + 1) * D], xT[:, h, k * P:(k + 1) * P],
                                   W[:, h, :], start=h == 0, stop=h == 1)
    return ins


def nodes_l0(nc, C, A, total, x1, h1):
    n = NODE_STEPS
    with ExitStack() as ctx:
        m = Mem(nc, ctx)
        W, b = m.sb("na_W", [P, 2, D]), m.sb("na_b", [P, D])
        load_all(nc, C, "na", [(W[:, :, :], A["l0_pw"].rearrange("(h p) d -> p h d", p=P)), (b[:, :], A["l0_pb"].broadcast_to([P, D]))])
        X = m.sb("na_X", [P, 4, KT, D])
        G = m.sb("na_G", [P, 2, KT, D])
        Y = m.sb("na_Y", [P, 2, KT, D])
        yT = m.sb("na_yT", [P, 2, 2, KT * P])
        X1 = m.sb("na_X1", [P, 2, KT, D])
        H1 = m.sb("na_H1", [P, 2, KT, D])
        SQ = m.sb("na_SQ", [P, 2, KT, D])
        slots = m.sb("na_slots", [P, 2, KT], U32)
        n1, n2 = Norm(m, C, "na_n1", KT), Norm(m, C, "na_n2", KT)
        normed, biased, added, turned, copied, projected, summed, squared, tallied, slotted, outnorm = (
            m.sem(f"na_{x}") for x in ("normed", "biased", "added", "turned", "copied", "projected", "summed", "squared", "tallied", "slotted", "outnorm"))
        xread = [m.sem(f"na_xread{j}") for j in range(4)]
        got = [C.mem.sem(f"na_got{j}") for j in range(2)]
        keep_x, keep_h = NodeStores(C, "na_keepx", m), NodeStores(C, "na_keeph", m)
        with nc.Block() as block:
            @block.sync
            def _(sp):
                def load(s, r):
                    if not first(s, 4):
                        wait_apart(sp, C, (summed, s + (-3)))
                    sp.dma_start(X[:, r, :, :], rows(A["x"], s, KT)).then_inc(xread[r], 16)
                run_steps(sp, n, [(4, lambda s, r: keep_x.put(sp, s, r, summed, x1, X1[:, r % 2, :, :])),
                                  (5, lambda s, r: keep_h.put(sp, s, r, outnorm, h1, H1[:, r % 2, :, :])), (0, load)], 4)
                keep_x.finish(sp)
                keep_h.finish(sp)

            @block.gpsimd
            def _(pool):
                def gather(s, r):
                    if not first(s, 2):
                        pool.wait_ge(added, s + (-1))
                    copy_slots(nc, C, pool, s, r, slots, C.slot_of[0], slotted)
                    gather_sums(nc, pool, s, r, slots, total, G, got)

                def add_bias(s, r):
                    pool.wait_ge(normed, s + 1)
                    nc.gpsimd.tensor_tensor(X[:, r, :, :], X[:, r, :, :], spread(b, KT), ALU.add).then_inc(biased, 1)
                run_steps(pool, n, [(2, add_bias), (0, gather)], 4)

            @block.vector
            def _(dve):
                def stats1(s, r):
                    dve.wait_ge(xread[r], landed(s, r, ring=4))
                    n1.stats(nc, dve, s, r % 2, X[:, r, :, :])

                def add_total(s, r):
                    dve.wait_ge(normed, s + 1)
                    dve.wait_ge(got[r % 2], landed(s, r % 2, KT))
                    y = Y[:, r % 2, :, :]
                    nc.vector.tensor_tensor(y, y, G[:, r % 2, :, :], ALU.add).then_inc(added, 1)

                def add_x(s, r):
                    par = r % 2
                    dve.wait_ge(projected, s + 1)
                    dve.wait_ge(biased, s + 1)
                    keep_x.free(dve, s, r)
                    if not first(s, 2):
                        dve.wait_ge(outnorm, s + (-1))
                    nc.vector.tensor_tensor(X1[:, par, :, :], C.banks(2 + 2 * par, 2, KT), X[:, r, :, :], ALU.add).then_inc(summed, 1)
                    dve.wait_ge(summed, s + 1)
                    n2.stats(nc, dve, s, par, X1[:, par, :, :])
                run_steps(dve, n, [(4, lambda s, r: n2.finish(nc, dve, s, r % 2)), (1, lambda s, r: n1.finish(nc, dve, s, r % 2)),
                                   (2, add_total), (0, stats1), (3, add_x)], 4)

            @block.scalar
            def _(act):
                def apply1(s, r):
                    if not first(s, 2):
                        act.wait_ge(turned, s + (-1))
                    act.wait_ge(n1.ready, s + 1)
                    n1.apply(nc, s, r % 2, Y[:, r % 2, :, :], X[:, r, :, :], ACT.Relu).then_inc(normed, 1)

                def apply2(s, r):
                    par = r % 2
                    keep_h.free(act, s, r)
                    if not first(s, 2):
                        act.wait_ge(tallied, s + (-1))
                    act.wait_ge(n2.ready, s + 1)
                    n2.apply(nc, s, par, H1[:, par, :, :], X1[:, par, :, :], ACT.Relu).then_inc(outnorm, 1)
                    act.wait_ge(outnorm, s + 1)
                    for k in range(KT):
                        pad = last_step(s, n) and k == KT - 1
                        ins = nc.scalar.activation(SQ[:, par, k, :], H1[:, par, k, :], ACT.Square,
                                                   scale=C.node_ok[:, 0:1] if pad else 1.0)
                    ins.then_inc(squared, 1)

                def copy(s, r):
                    if not first(s, 2):
                        act.wait_ge(projected, s + (-1))
                    act.wait_ge(turned, s + 1)
                    nc.scalar.activation(yT[:, r % 2, :, :], C.banks(0, 2, 2), ACT.Copy).then_inc(copied, 1)
                run_steps(act, n, [(4, apply2), (1, apply1), (0, lambda s, r: n1.root(nc, act, s, r % 2)), (2, copy),
                                   (3, lambda s, r: n2.root(nc, act, s, r % 2))], 4)

            @block.tensor
            def _(pe):
                def turn(s, r):
                    pe.wait_ge(added, s + 1)
                    if not first(s, 1):
                        pe.wait_ge(copied, s)
                    transpose_tiles(nc, C, 0, Y[:, r % 2, :, :]).then_inc(turned, 1)

                def project(s, r):
                    pe.wait_ge(copied, s + 1)
                    if not first(s, 2):
                        pe.wait_ge(summed, s + (-1))
                    project_tiles(nc, C, 2 + 2 * (r % 2), yT[:, r % 2, :, :], W).then_inc(projected, 1)

                def tally(s, r):
                    pe.wait_ge(squared, s + 1)
                    for k in range(KT):
                        for h in range(2):
                            ins = nc.tensor.matmul(C.bank[6 + h][:, 0:1], SQ[:, r % 2, k, h * P:(h + 1) * P], C.ones[:, 0:1],
                                                   start=first(s, 1) and k == 0, stop=last_step(s, n) and k == KT - 1)
                    ins.then_inc(tallied, 1)
                run_steps(pe, n, [(3, project), (5, tally), (2, turn)], 4)


def l1_weights(nc, C, A, Wt):
    with ExitStack() as ctx:
        m = Mem(nc, ctx)
        cs, nn, al = m.sb("lw_cs", [P, 2]), m.sb("lw_nn", [P, 2]), m.sb("lw_al", [P, 4])
        keep = m.sb("lw_keep", [P, 2, D])
        load_all(nc, C, "lw", [(Wt[:, :, :], A["l1_wt"].rearrange("(h p) d -> p h d", p=P))])
        v, a, t = m.sem("lw_v"), m.sem("lw_a"), m.sem("lw_t")
        with nc.Block() as block:
            @block.vector
            def _(dve):
                n = [0]

                def link(ins):
                    ins.then_inc(v, 1)
                    n[0] += 1
                    dve.wait_ge(v, n[0])

                link(nc.vector.tensor_copy(cs[:, 0:1], C.bank[6][:, 0:1]))
                link(nc.vector.tensor_copy(cs[:, 1:2], C.bank[7][:, 0:1]))
                dve.wait_ge(t, 2)
                link(nc.vector.tensor_copy(al[:, 0:1], C.bank[0][:, 0:1]))
                dve.wait_ge(a, 2)
                link(nc.vector.tensor_scalar(al[:, 1:2], al[:, 1:2], 1.0 / D, None, ALU.mult))
                link(nc.vector.tensor_scalar(al[:, 2:3], al[:, 1:2], 1e-8, None, ALU.is_gt))
                link(nc.vector.scalar_tensor_tensor(out=al[:, 3:4], in0=al[:, 1:2], scalar=0.1, in1=al[:, 2:3],
                                                    op0=ALU.mult, op1=ALU.mult))
                for h in range(2):
                    link(nc.vector.scalar_tensor_tensor(out=keep[:, h, :], in0=Wt[:, h, :], scalar=-1.0, in1=Wt[:, h, :],
                                                        op0=ALU.mult, op1=ALU.max))
                    link(nc.vector.tensor_scalar(keep[:, h, :], keep[:, h, :], nn[:, h:h + 1], al[:, 3:4], ALU.mult, ALU.is_ge))
                    link(nc.vector.tensor_tensor(Wt[:, h, :], Wt[:, h, :], keep[:, h, :], ALU.mult))

            @block.scalar
            def _(act):
                act.wait_ge(v, 2)
                nc.scalar.activation(nn[:, :], cs[:, :], ACT.Sqrt).then_inc(a, 1)
                act.wait_ge(v, 3)
                nc.scalar.activation(al[:, 1:2], al[:, 0:1], ACT.Sqrt).then_inc(a, 1)

            @block.tensor
            def _(pe):
                pe.wait_ge(v, 2)
                for h in range(2):
                    nc.tensor.matmul(C.bank[0][:, 0:1], C.ones[:, :], cs[:, h:h + 1], start=h == 0, stop=h == 1).then_inc(t, 1)


def l1_edges(nc, C, A, h1, table, bias, Wt):
    n = EDGE_STEPS
    with ExitStack() as ctx:
        m = Mem(nc, ctx)
        H = m.sb("l1_H", [P, NC, D])
        G = m.sb("l1_G", [P, 2, KC, D])
        gT = m.sb("l1_gT", [P, 2, KC * 2, P])
        idx = m.sb("l1_idx", [P, 2, KC], U32)
        junk = m.sb("l1_junk", [P, 2, D])
        ss = m.sb("l1_ss", [P, NC])
        idxed, turned, copied, projected, kept, squared = (m.sem(f"l1_{x}") for x in
                                                           ("idxed", "turned", "copied", "projected", "kept", "squared"))
        got = [C.mem.sem(f"l1_got{j}") for j in range(2)]
        with nc.Block() as block:
            @block.gpsimd
            def _(pool):
                def gather(s, par):
                    if not first(s, 2):
                        pool.wait_ge(turned, s + (-1))
                    nc.gpsimd.tensor_copy(idx[:, par, :], C.rec[:, bass.ds(s * KC, KC), R_SRC].bitcast(U32)).then_inc(idxed, 1)
                    wait_apart(pool, C, (idxed, s + 1))
                    for j in range(KC):
                        nc.gpsimd.indirect_dma_start(out=G[:, par, j, :], out_offset=None, in_=h1,
                                                     in_offset=bass.IndirectOffsetOnAxis(ap=idx[:, par, j:j + 1], axis=0)
                                                     ).then_inc(got[par], 16)
                run_steps(pool, n, [(0, gather)])

            @block.tensor
            def _(pe):
                def turn(s, par):
                    pe.wait_ge(got[par], landed(s, par, KC))
                    if not first(s, 2):
                        pe.wait_ge(copied, s + (-1))
                    for q in range(2 * KC):
                        ins = nc.tensor.transpose(C.bank[par][:, q * P:(q + 1) * P], G[:, par, q // 2, (q % 2) * P:(q % 2 + 1) * P], C.ident[:, :])
                    ins.then_inc(turned, 1)

                def project(s, par):
                    pe.wait_ge(copied, s + 1)
                    if not first(s, 2):
                        pe.wait_ge(kept, s + (-1))
                    for j in range(KC):
                        for h in range(2):
                            ins = nc.tensor.matmul(C.bank[2 + par][:, j * D:(j + 1) * D], gT[:, par, 2 * j + h, :], Wt[:, h, :],
                                                   start=h == 0, stop=h == 1)
                    ins.then_inc(projected, 1)
                run_steps(pe, n, [(1, project), (0, turn)])

            @block.vector
            def _(dve):
                def copy(s, par):
                    dve.wait_ge(turned, s + 1)
                    if not first(s, 2):
                        dve.wait_ge(projected, s + (-1))
                    nc.vector.tensor_copy(gT[:, par, :, :].rearrange("p q e -> p (q e)"), C.bank[par][:, :]).then_inc(copied, 1)
                run_steps(dve, n, [(0, copy)])

            @block.scalar
            def _(act):
                def keep(s, par):
                    act.wait_ge(projected, s + 1)
                    hv = H[:, bass.ds(s * KC, KC), :]
                    nc.scalar.activation(hv, C.bank[2 + par][:, :].rearrange("p (j d) -> p j d", j=KC), ACT.Copy).then_inc(kept, 1)
                    act.wait_ge(kept, s + 1)
                    if not first(s, 1):
                        act.wait_ge(squared, s)
                    for j in range(KC):
                        ins = nc.scalar.activation(junk[:, j, :], H[:, bass.ds(s * KC + j, 1), :].rearrange("p o d -> p (o d)"), ACT.Square,
                                                   accum_out=ss[:, bass.ds(s * KC + j, 1)])
                    ins.then_inc(squared, 1)
                run_steps(act, n, [(0, keep)])

        nm, some, w2, tot, thr = m.sb("l1_nm", [P, NC]), m.sb("l1_some", [P, NC]), m.sb("l1_w2", [P, NC]), m.sb("l1_tot", [P, 1]), m.sb("l1_thr", [P, 1])
        v, a, t = m.sem("l1_v"), m.sem("l1_a"), m.sem("l1_t")
        with nc.Block() as block:
            @block.vector
            def _(dve):
                k = [0]

                def link(ins):
                    ins.then_inc(v, 1)
                    k[0] += 1
                    dve.wait_ge(v, k[0])

                link(nc.vector.tensor_tensor(w2[:, :], C.weight[:, :], C.weight[:, :], ALU.mult))
                link(nc.vector.tensor_tensor(ss[:, :], ss[:, :], w2[:, :], ALU.mult))
                link(nc.vector.tensor_scalar(some[:, :], ss[:, :], 2.0 ** -110, None, ALU.is_gt))
                link(nc.vector.tensor_scalar(ss[:, :], ss[:, :], 2.0 ** -110, None, ALU.max))
                dve.wait_ge(a, 1)
                link(nc.vector.tensor_tensor(nm[:, :], nm[:, :], some[:, :], ALU.mult))
                link(nc.vector.tensor_copy(w2[:, :], nm[:, :]))
                link(nc.vector.tensor_tensor(w2[:, NC - 1:NC], nm[:, NC - 1:NC], C.edge_ok[:, :], ALU.mult))
                link(nc.vector.reduce_sum(tot[:, :], w2[:, :], mybir.AxisListType.X))
                dve.wait_ge(t, 1)
                link(nc.vector.tensor_scalar(thr[:, :], C.bank[4][:, 0:1], 1.0 / E, 0.1, ALU.mult, ALU.mult))
                link(nc.vector.tensor_scalar(nm[:, :], nm[:, :], thr[:, 0:1], None, ALU.is_ge))
                link(nc.vector.tensor_tensor(nm[:, :], nm[:, :], C.lock[:, :], ALU.max))
                link(nc.vector.tensor_tensor(nm[:, :], nm[:, :], C.weight[:, :], ALU.mult))

            @block.scalar
            def _(act):
                act.wait_ge(v, 4)
                nc.scalar.activation(nm[:, :], ss[:, :], ACT.Sqrt).then_inc(a, 1)

            @block.tensor
            def _(pe):
                pe.wait_ge(v, 8)
                nc.tensor.matmul(C.bank[4][:, 0:1], C.ones[:, :], tot[:, :], start=True, stop=True).then_inc(t, 1)

        sum_edges(nc, C, "l1s", table, bias, C.same_d, nm, resident=H)
        carry_over(nc, C, "l1", 0, table, bias)


def sum_edges(nc, C, tag, table, bias, same, weight, resident):
    n = EDGE_STEPS
    with ExitStack() as ctx:
        m = Mem(nc, ctx)
        seg = m.sb(f"{tag}_seg", [P, 2, KC, P])
        res = m.sb(f"{tag}_res", [P, 2, KC, D])
        segged, summed, evac = m.sem(f"{tag}_segged"), m.sem(f"{tag}_summed"), m.sem(f"{tag}_evac")
        stored = [m.sem(f"{tag}_stored{j}") for j in range(2)]
        with nc.Block() as block:
            @block.scalar
            def _(act):
                def weigh(s, par):
                    if not first(s, 2):
                        act.wait_ge(summed, s + (-1))
                    for j in range(KC):
                        c = s * KC + j
                        ins = nc.scalar.activation(seg[:, par, j, :], same[:, bass.ds(c * P, P)], ACT.Copy, scale=weight[:, bass.ds(c, 1)])
                    ins.then_inc(segged, 1)
                run_steps(act, n, [(0, weigh)])

            @block.tensor
            def _(pe):
                def total(s, par):
                    pe.wait_ge(segged, s + 1)
                    if not first(s, 2):
                        pe.wait_ge(evac, s + (-1))
                    for j in range(KC):
                        ins = nc.tensor.matmul(C.bank[par][:, j * D:(j + 1) * D], seg[:, par, j, :],
                                               resident[:, bass.ds(s * KC + j, 1), :].rearrange("p o d -> p (o d)"), start=True, stop=True)
                    ins.then_inc(summed, 1)
                run_steps(pe, n, [(0, total)])

            @block.vector
            def _(dve):
                def evacuate(s, par):
                    dve.wait_ge(summed, s + 1)
                    if not first(s, 2):
                        dve.wait_ge(stored[par], landed(s - 2, par))
                    nc.vector.tensor_tensor(res[:, par, :, :], C.bank[par][:, :].rearrange("p (j d) -> p j d", j=KC),
                                            spread(bias, KC), ALU.add).then_inc(evac, 1)
                run_steps(dve, n, [(0, evacuate)])

            @block.sync
            def _(sp):
                def store(s, par):
                    wait_apart(sp, C, (evac, s + 1))
                    sp.dma_start(rows(table, s, KC), res[:, par, :, :]).then_inc(stored[par], 16)
                run_steps(sp, n, [(0, store)])
                all_landed(sp, stored, n)


def nodes_l1(nc, C, x1, table, x2, e0):
    n = NODE_STEPS
    with ExitStack() as ctx:
        m = Mem(nc, ctx)
        X, G, H = (m.sb(f"nb_{x}", [P, 2, KT, D]) for x in "XGH")
        X2 = m.sb("nb_X2", [P, 2, KT, D])
        slots = m.sb("nb_slots", [P, 2, KT], U32)
        norm = Norm(m, C, "nb_n", KT)
        summed, normed, slotted = m.sem("nb_summed"), m.sem("nb_normed"), m.sem("nb_slotted")
        xread = [m.sem(f"nb_xread{j}") for j in range(2)]
        got = [C.mem.sem(f"nb_got{j}") for j in range(2)]
        keep_x, keep_h = NodeStores(C, "nb_keepx", m), NodeStores(C, "nb_keeph", m)
        with nc.Block() as block:
            @block.sync
            def _(sp):
                def load(s, r):
                    if not first(s, 2):
                        wait_apart(sp, C, (summed, s + (-1)))
                    sp.dma_start(X[:, r, :, :], rows(x1, s, KT)).then_inc(xread[r], 16)
                run_steps(sp, n, [(0, load), (1, lambda s, r: keep_x.put(sp, s, r, summed, x2, X2[:, r, :, :])),
                                  (2, lambda s, r: keep_h.put(sp, s, r, normed, e0, H[:, r, :, :]))])
                keep_x.finish(sp)
                keep_h.finish(sp)

            @block.gpsimd
            def _(pool):
                def gather(s, r):
                    if not first(s, 2):
                        pool.wait_ge(summed, s + (-1))
                    copy_slots(nc, C, pool, s, r, slots, C.slot_of[0], slotted)
                    gather_sums(nc, pool, s, r, slots, table, G, got)
                run_steps(pool, n, [(0, gather)])

            @block.vector
            def _(dve):
                def add(s, r):
                    dve.wait_ge(xread[r], landed(s, r))
                    dve.wait_ge(got[r], landed(s, r, KT))
                    keep_x.free(dve, s, r)
                    if not first(s, 2):
                        dve.wait_ge(normed, s + (-1))
                    nc.vector.tensor_tensor(X2[:, r, :, :], X[:, r, :, :], G[:, r, :, :], ALU.add).then_inc(summed, 1)
                    dve.wait_ge(summed, s + 1)
                    norm.stats(nc, dve, s, r, X2[:, r, :, :])
                run_steps(dve, n, [(0, add), (1, lambda s, r: norm.finish(nc, dve, s, r))])

            @block.scalar
            def _(act):
                def apply(s, r):
                    keep_h.free(act, s, r)
                    act.wait_ge(norm.ready, s + 1)
                    norm.apply(nc, s, r, H[:, r, :, :], X2[:, r, :, :], ACT.Relu).then_inc(normed, 1)
                run_steps(act, n, [(0, lambda s, r: norm.root(nc, act, s, r)), (1, apply)])


def l2_edges(nc, C, A, layer, hin, table, bias):
    n = EDGE_STEPS
    NB = 10
    tag = f"l2e{layer}"
    with ExitStack() as ctx:
        m = Mem(nc, ctx)
        B = m.sb(f"{tag}_B", [P, 2, NB, D])
        load_all(nc, C, tag, [(B[:, h, :, :], A[f"l2_basis{layer}"][:, h * P:(h + 1) * P, :].rearrange("b p d -> p b d")) for h in range(2)])
        G = m.sb(f"{tag}_G", [P, 2, KC, D])
        gT = m.sb(f"{tag}_gT", [P, 2, KC * 2, P])
        M = m.sb(f"{tag}_M", [P, 2, KC, D])
        seg = m.sb(f"{tag}_seg", [P, 2, KC, P])
        res = m.sb(f"{tag}_res", [P, 2, KC, D])
        idx = m.sb(f"{tag}_idx", [P, 2, KC], U32)
        idxed, turned, copied, projected, weighed, segged, summed, evac = (
            m.sem(f"{tag}_{x}") for x in ("idxed", "turned", "copied", "projected", "weighed", "segged", "summed", "evac"))
        got = [C.mem.sem(f"{tag}_got{j}") for j in range(2)]
        stored = [m.sem(f"{tag}_stored{j}") for j in range(2)]
        PAIRS = NB // 2
        with nc.Block() as block:
            @block.gpsimd
            def _(pool):
                def gather(s, par):
                    if not first(s, 2):
                        pool.wait_ge(turned, s + (-1))
                    nc.gpsimd.tensor_copy(idx[:, par, :], C.rec[:, bass.ds(s * KC, KC), R_SRC].bitcast(U32)).then_inc(idxed, 1)
                    wait_apart(pool, C, (idxed, s + 1))
                    for j in range(KC):
                        nc.gpsimd.indirect_dma_start(out=G[:, par, j, :], out_offset=None, in_=hin,
                                                     in_offset=bass.IndirectOffsetOnAxis(ap=idx[:, par, j:j + 1], axis=0)
                                                     ).then_inc(got[par], 16)
                run_steps(pool, n, [(0, gather)])

            @block.tensor
            def _(pe):
                def turn(s, par):
                    pe.wait_ge(got[par], landed(s, par, KC))
                    if not first(s, 1):
                        pe.wait_ge(copied, s)
                    for q in range(2 * KC):
                        ins = nc.tensor.transpose(C.bank[0][:, q * P:(q + 1) * P], G[:, par, q // 2, (q % 2) * P:(q % 2 + 1) * P], C.ident[:, :])
                    ins.then_inc(turned, 1)

                def project(s, par):
                    pe.wait_ge(copied, s + 1)
                    for j in range(KC):
                        for p in range(PAIRS):
                            i = j * PAIRS + p
                            if not (first(s, 1) and i < 4):
                                pe.wait_ge(weighed, s * (KC * NB) + 2 * (i - 3))
                            for h in range(2):
                                ins = nc.tensor.matmul(C.bank[1 + (i + 2 * par) % 4][:, :], gT[:, par, 2 * j + h, :],
                                                       B[:, h, 2 * p:2 * p + 2, :].rearrange("p b d -> p (b d)"), start=h == 0, stop=h == 1)
                            ins.then_inc(projected, 1)

                def total(s, par):
                    pe.wait_ge(segged, s + 1)
                    pe.wait_ge(weighed, s * (KC * NB) + KC * NB)
                    if not first(s, 2):
                        pe.wait_ge(evac, s + (-1))
                    for j in range(KC):
                        ins = nc.tensor.matmul(C.bank[5 + par][:, j * D:(j + 1) * D], seg[:, par, j, :], M[:, par, j, :], start=True, stop=True)
                    ins.then_inc(summed, 1)
                run_steps(pe, n, [(0, turn), (2, total), (1, project)])

            @block.scalar
            def _(act):
                def copy(s, par):
                    act.wait_ge(turned, s + 1)
                    if not first(s, 2):
                        act.wait_ge(projected, s * (KC * PAIRS) + (-KC * PAIRS))
                    nc.scalar.activation(gT[:, par, :, :].rearrange("p q e -> p (q e)"), C.bank[0][:, :], ACT.Copy).then_inc(copied, 1)

                def widen(s, par):
                    if not first(s, 2):
                        act.wait_ge(summed, s + (-1))
                    for j in range(KC):
                        ins = nc.scalar.activation(seg[:, par, j, :], C.same_d[:, bass.ds((s * KC + j) * P, P)], ACT.Copy)
                    ins.then_inc(segged, 1)
                run_steps(act, n, [(0, copy), (1, widen)])

            @block.vector
            def _(dve):
                def weigh(s, par):
                    if not first(s, 2):
                        dve.wait_ge(summed, s + (-1))
                    for j in range(KC):
                        for p in range(PAIRS):
                            i = j * PAIRS + p
                            dve.wait_ge(projected, s * (KC * PAIRS) + (i + 1))
                            for b in range(2):
                                k = 2 * p + b
                                bank = C.bank[1 + (i + 2 * par) % 4][:, b * D:(b + 1) * D]
                                c = C.coef[:, bass.ds(s * KC + j, 1), (layer - 1) * NB + k]
                                out = M[:, par, j, :]
                                if k == 0:
                                    ins = nc.vector.tensor_scalar(out, bank, c, None, ALU.mult)
                                else:
                                    dve.wait_ge(weighed, s * (KC * NB) + (j * NB + k))
                                    ins = nc.vector.scalar_tensor_tensor(out=out, in0=bank, scalar=c, in1=out, op0=ALU.mult, op1=ALU.add)
                                ins.then_inc(weighed, 1)

                def evacuate(s, par):
                    dve.wait_ge(summed, s + 1)
                    if not first(s, 2):
                        dve.wait_ge(stored[par], landed(s - 2, par))
                    nc.vector.tensor_tensor(res[:, par, :, :], C.bank[5 + par][:, :].rearrange("p (j d) -> p j d", j=KC),
                                            spread(bias, KC), ALU.add).then_inc(evac, 1)
                run_steps(dve, n, [(2, evacuate), (0, weigh)])

            @block.sync
            def _(sp):
                def store(s, par):
                    wait_apart(sp, C, (evac, s + 1))
                    sp.dma_start(rows(table, s, KC), res[:, par, :, :]).then_inc(stored[par], 16)
                run_steps(sp, n, [(0, store)])
                all_landed(sp, stored, n)
        carry_over(nc, C, f"l2c{layer}", 0, table, bias)


def nodes_l2a(nc, C, A, e0, table, h2):
    n = NODE_STEPS
    with ExitStack() as ctx:
        m = Mem(nc, ctx)
        W = m.sb("nc_W", [P, 2, D])
        load_all(nc, C, "nc", [(W[:, :, :], A["l2_lw1"].rearrange("(h p) d -> p h d", p=P))])
        X, G, H = (m.sb(f"nc_{x}", [P, 2, KT, D]) for x in "XGH")
        xT = m.sb("nc_xT", [P, 2, 2, KT * P])
        slots = m.sb("nc_slots", [P, 2, KT], U32)
        turned, copied, projected, summed, relued, slotted = (m.sem(f"nc_{x}") for x in ("turned", "copied", "projected", "summed", "relued", "slotted"))
        xread = [m.sem(f"nc_xread{j}") for j in range(2)]
        got = [C.mem.sem(f"nc_got{j}") for j in range(2)]
        keep = NodeStores(C, "nc_keep", m)
        with nc.Block() as block:
            @block.sync
            def _(sp):
                def load(s, r):
                    if not first(s, 2):
                        wait_apart(sp, C, (turned, s + (-1)))
                    sp.dma_start(X[:, r, :, :], rows(e0, s, KT)).then_inc(xread[r], 16)
                run_steps(sp, n, [(0, load), (2, lambda s, r: keep.put(sp, s, r, relued, h2, H[:, r, :, :]))])
                keep.finish(sp)

            @block.gpsimd
            def _(pool):
                def gather(s, r):
                    if not first(s, 2):
                        pool.wait_ge(relued, s + (-1))
                    copy_slots(nc, C, pool, s, r, slots, C.slot_of[0], slotted)
                    gather_sums(nc, pool, s, r, slots, table, G, got)
                run_steps(pool, n, [(0, gather)])

            @block.tensor
            def _(pe):
                def turn(s, r):
                    pe.wait_ge(xread[r], landed(s, r))
                    if not first(s, 2):
                        pe.wait_ge(copied, s + (-1))
                    transpose_tiles(nc, C, 2 * r, X[:, r, :, :]).then_inc(turned, 1)

                def project(s, r):
                    pe.wait_ge(copied, s + 1)
                    if not first(s, 2):
                        pe.wait_ge(summed, s + (-1))
                    project_tiles(nc, C, 4 + 2 * r, xT[:, r, :, :], W).then_inc(projected, 1)
                run_steps(pe, n, [(0, turn), (1, project)])

            @block.scalar
            def _(act):
                def copy(s, r):
                    act.wait_ge(turned, s + 1)
                    if not first(s, 2):
                        act.wait_ge(projected, s + (-1))
                    nc.scalar.activation(xT[:, r, :, :], C.banks(2 * r, 2, 2), ACT.Copy).then_inc(copied, 1)

                def relu(s, r):
                    act.wait_ge(summed, s + 1)
                    keep.free(act, s, r)
                    nc.scalar.activation(H[:, r, :, :], G[:, r, :, :], ACT.Relu).then_inc(relued, 1)
                run_steps(act, n, [(0, copy), (1, relu)])

            @block.vector
            def _(dve):
                def add(s, r):
                    dve.wait_ge(projected, s + 1)
                    dve.wait_ge(got[r], landed(s, r, KT))
                    nc.vector.tensor_tensor(G[:, r, :, :], C.banks(4 + 2 * r, 2, KT), G[:, r, :, :], ALU.add).then_inc(summed, 1)
                run_steps(dve, n, [(0, add)])


def nodes_l2b(nc, C, A, h2, e0, x2, table, x3, h3):
    n = NODE_STEPS
    with ExitStack() as ctx:
        m = Mem(nc, ctx)
        W, g, b = m.sb("nd_W", [P, 2, D]), m.sb("nd_g", [P, D]), m.sb("nd_b", [P, D])
        load_all(nc, C, "nd", [(W[:, :, :], A["l2_lw2"].rearrange("(h p) d -> p h d", p=P)),
                               (g[:, :], A["l2_g"].broadcast_to([P, D])), (b[:, :], A["l2_b"].broadcast_to([P, D]))])
        H, G, U, Z, X3, H3 = (m.sb(f"nd_{x}", [P, 2, KT, D]) for x in ("H", "G", "U", "Z", "X3", "H3"))
        X, E0 = m.sb("nd_X", [P, 4, KT, D]), m.sb("nd_E0", [P, 4, KT, D])
        hT = m.sb("nd_hT", [P, 2, 2, KT * P])
        slots = m.sb("nd_slots", [P, 2, KT], U32)
        n1, n2 = Norm(m, C, "nd_n1", KT), Norm(m, C, "nd_n2", KT)
        turned, copied, projected, summed, biased, normed, scaled, added, normed2, slotted, mixed = (
            m.sem(f"nd_{x}") for x in ("turned", "copied", "projected", "summed", "biased", "normed", "scaled", "added", "normed2", "slotted", "mixed"))
        hread = [m.sem(f"nd_hread{j}") for j in range(2)]
        xread = [m.sem(f"nd_xread{j}") for j in range(4)]
        eread = [m.sem(f"nd_eread{j}") for j in range(4)]
        got = [C.mem.sem(f"nd_got{j}") for j in range(2)]
        keep_x, keep_h = NodeStores(C, "nd_keepx", m), NodeStores(C, "nd_keeph", m)
        with nc.Block() as block:
            @block.sync
            def _(sp):
                def load(s, r):
                    if not first(s, 2):
                        wait_apart(sp, C, (turned, s + (-1)))
                    sp.dma_start(H[:, r % 2, :, :], rows(h2, s, KT)).then_inc(hread[r % 2], 16)
                    if not first(s, 4):
                        wait_apart(sp, C, (mixed, s + (-3)))
                    sp.dma_start(E0[:, r, :, :], rows(e0, s, KT)).then_inc(eread[r], 16)
                    if not first(s, 4):
                        wait_apart(sp, C, (added, s + (-3)))
                    sp.dma_start(X[:, r, :, :], rows(x2, s, KT)).then_inc(xread[r], 16)
                run_steps(sp, n, [(4, lambda s, r: keep_x.put(sp, s, r, added, x3, X3[:, r % 2, :, :])),
                                  (5, lambda s, r: keep_h.put(sp, s, r, normed2, h3, H3[:, r % 2, :, :])), (0, load)], 4)
                keep_x.finish(sp)
                keep_h.finish(sp)

            @block.gpsimd
            def _(pool):
                def gather(s, r):
                    if not first(s, 2):
                        pool.wait_ge(summed, s + (-1))
                    copy_slots(nc, C, pool, s, r, slots, C.slot_of[0], slotted)
                    gather_sums(nc, pool, s, r, slots, table, G, got)

                def add_bias(s, r):
                    pool.wait_ge(xread[r], landed(s, r, ring=4))
                    nc.gpsimd.tensor_tensor(X[:, r, :, :], X[:, r, :, :], spread(b, KT), ALU.add).then_inc(biased, 1)
                run_steps(pool, n, [(0, gather), (0, add_bias)], 4)

            @block.tensor
            def _(pe):
                def turn(s, r):
                    pe.wait_ge(hread[r % 2], landed(s, r % 2))
                    if not first(s, 2):
                        pe.wait_ge(copied, s + (-1))
                    transpose_tiles(nc, C, 2 * (r % 2), H[:, r % 2, :, :]).then_inc(turned, 1)

                def project(s, r):
                    pe.wait_ge(copied, s + 1)
                    if not first(s, 2):
                        pe.wait_ge(summed, s + (-1))
                    project_tiles(nc, C, 4 + 2 * (r % 2), hT[:, r % 2, :, :], W).then_inc(projected, 1)
                run_steps(pe, n, [(0, turn), (1, project)], 4)

            @block.scalar
            def _(act):
                def copy(s, r):
                    par = r % 2
                    act.wait_ge(turned, s + 1)
                    if not first(s, 2):
                        act.wait_ge(projected, s + (-1))
                    nc.scalar.activation(hT[:, par, :, :], C.banks(2 * par, 2, 2), ACT.Copy).then_inc(copied, 1)

                def apply1(s, r):
                    act.wait_ge(n1.ready, s + 1)
                    if not first(s, 2):
                        act.wait_ge(added, s + (-1))
                    n1.apply(nc, s, r % 2, Z[:, r % 2, :, :], U[:, r % 2, :, :], ACT.Identity).then_inc(normed, 1)

                def apply2(s, r):
                    keep_h.free(act, s, r)
                    act.wait_ge(n2.ready, s + 1)
                    n2.apply(nc, s, r % 2, H3[:, r % 2, :, :], X3[:, r % 2, :, :], ACT.Relu).then_inc(normed2, 1)
                run_steps(act, n, [(4, apply2), (2, apply1), (0, copy), (1, lambda s, r: n1.root(nc, act, s, r % 2)),
                                   (3, lambda s, r: n2.root(nc, act, s, r % 2))], 4)

            @block.vector
            def _(dve):
                def mix(s, r):
                    par = r % 2
                    dve.wait_ge(projected, s + 1)
                    dve.wait_ge(got[par], landed(s, par, KT))
                    if not first(s, 2):
                        dve.wait_ge(normed, s + (-1))
                    nc.vector.tensor_tensor(U[:, par, :, :], C.banks(4 + 2 * par, 2, KT), G[:, par, :, :], ALU.add).then_inc(summed, 1)
                    dve.wait_ge(summed, s + 1)
                    dve.wait_ge(eread[r], landed(s, r, ring=4))
                    nc.vector.scalar_tensor_tensor(out=U[:, par, :, :], in0=U[:, par, :, :], scalar=0.0, in1=E0[:, r, :, :],
                                                   op0=ALU.max, op1=ALU.add).then_inc(mixed, 1)
                    dve.wait_ge(mixed, s + 1)
                    n1.stats(nc, dve, s, par, U[:, par, :, :])

                def add(s, r):
                    par = r % 2
                    dve.wait_ge(normed, s + 1)
                    nc.vector.tensor_tensor(Z[:, par, :, :], Z[:, par, :, :], spread(g, KT), ALU.mult).then_inc(scaled, 1)
                    dve.wait_ge(scaled, s + 1)
                    dve.wait_ge(biased, s + 1)
                    keep_x.free(dve, s, r)
                    if not first(s, 2):
                        dve.wait_ge(normed2, s + (-1))
                    nc.vector.tensor_tensor(X3[:, par, :, :], Z[:, par, :, :], X[:, r, :, :], ALU.add).then_inc(added, 1)
                    dve.wait_ge(added, s + 1)
                    n2.stats(nc, dve, s, par, X3[:, par, :, :])
                run_steps(dve, n, [(4, lambda s, r: n2.finish(nc, dve, s, r % 2)), (2, lambda s, r: n1.finish(nc, dve, s, r % 2)),
                                   (3, add), (1, mix)], 4)


def l3_edges(nc, C, A, h3, by_src, table_d, table_s, zero):
    n = EDGE_STEPS
    with ExitStack() as ctx:
        m = Mem(nc, ctx)
        G = m.sb("l3_G", [P, 2, 3, KC, D])
        M = m.sb("l3_M", [P, 2, KC, D])
        res = m.sb("l3_res", [P, 2, KC, D])
        seg = m.sb("l3_seg", [P, 2, KC, P])
        idx = m.sb("l3_idx", [P, 2, 4, KC], U32)
        FIELDS = (R_SRC, R_DST, R_EID, R_RANKS)
        idxed, summed0, added, relued, segged, summed, evac = (m.sem(f"l3_{x}") for x in
                                                               ("idxed", "summed0", "added", "relued", "segged", "summed", "evac"))
        got = [C.mem.sem(f"l3_got{j}") for j in range(2)]
        put = [C.mem.sem(f"l3_put{j}") for j in range(2)]
        stored = [m.sem(f"l3_stored{j}") for j in range(2)]
        with nc.Block() as block:
            @block.gpsimd
            def _(pool):
                def gather(s, par):
                    if not first(s, 2):
                        pool.wait_ge(added, s + (-1))
                        pool.wait_ge(put[par], landed(s - 2, par, KC))
                    for f, field in enumerate(FIELDS):
                        nc.gpsimd.tensor_copy(idx[:, par, f, :], C.rec[:, bass.ds(s * KC, KC), field].bitcast(U32)).then_inc(idxed, 1)
                    wait_apart(pool, C, (idxed, s * 4 + 4))
                    for f, t in enumerate((h3, h3, A["attr"])):
                        for j in range(KC):
                            nc.gpsimd.indirect_dma_start(out=G[:, par, f, j, :], out_offset=None, in_=t,
                                                         in_offset=bass.IndirectOffsetOnAxis(ap=idx[:, par, f, j:j + 1], axis=0)
                                                         ).then_inc(got[par], 16)

                def scatter(s, par):
                    wait_apart(pool, C, (relued, s + 1))
                    for j in range(KC):
                        nc.gpsimd.indirect_dma_start(out=by_src, out_offset=bass.IndirectOffsetOnAxis(ap=idx[:, par, 3, j:j + 1], axis=0),
                                                     in_=M[:, par, j, :], in_offset=None).then_inc(put[par], 16)
                run_steps(pool, n, [(0, gather), (1, scatter)])
                all_landed(pool, put, n, KC)

            @block.vector
            def _(dve):
                def add(s, par):
                    dve.wait_ge(got[par], landed(s, par, 3 * KC))
                    g = [G[:, par, f, :, :] for f in range(3)]
                    nc.vector.tensor_tensor(g[0], g[0], g[1], ALU.add).then_inc(summed0, 1)
                    dve.wait_ge(summed0, s + 1)
                    if not first(s, 2):
                        dve.wait_ge(relued, s + (-1))
                        dve.wait_ge(put[par], landed(s - 2, par, KC))
                        dve.wait_ge(summed, s + (-1))
                    nc.vector.tensor_tensor(M[:, par, :, :], g[0], g[2], ALU.add).then_inc(added, 1)

                def evacuate(s, par):
                    dve.wait_ge(summed, s + 1)
                    if not first(s, 2):
                        dve.wait_ge(stored[par], landed(s - 2, par))
                    nc.vector.tensor_copy(res[:, par, :, :], C.bank[par][:, :].rearrange("p (j d) -> p j d", j=KC)).then_inc(evac, 1)
                run_steps(dve, n, [(1, evacuate), (0, add)])

            @block.scalar
            def _(act):
                def relu(s, par):
                    act.wait_ge(added, s + 1)
                    nc.scalar.activation(M[:, par, :, :], M[:, par, :, :], ACT.Relu).then_inc(relued, 1)
                    for j in range(KC):
                        ins = nc.scalar.activation(seg[:, par, j, :], C.same_d[:, bass.ds((s * KC + j) * P, P)], ACT.Copy)
                    ins.then_inc(segged, 1)
                run_steps(act, n, [(0, relu)])

            @block.tensor
            def _(pe):
                def total(s, par):
                    pe.wait_ge(segged, s + 1)
                    if not first(s, 2):
                        pe.wait_ge(evac, s + (-1))
                    for j in range(KC):
                        ins = nc.tensor.matmul(C.bank[par][:, j * D:(j + 1) * D], seg[:, par, j, :], M[:, par, j, :], start=True, stop=True)
                    ins.then_inc(summed, 1)
                run_steps(pe, n, [(0, total)])

            @block.sync
            def _(sp):
                def store(s, par):
                    wait_apart(sp, C, (evac, s + 1))
                    sp.dma_start(rows(table_d, s, KC), res[:, par, :, :]).then_inc(stored[par], 16)
                run_steps(sp, n, [(0, store)])
                all_landed(sp, stored, n)
        carry_over(nc, C, "l3c", 0, table_d, zero)

    with ExitStack() as ctx:
        m = Mem(nc, ctx)
        M = m.sb("l3s_M", [P, 2, KC, D])
        res = m.sb("l3s_res", [P, 2, KC, D])
        key = m.sb("l3s_key", [P, 2, KC])
        seg = m.sb("l3s_seg", [P, 2, KC, P])
        kept, shown, segged, summed, evac = (m.sem(f"l3s_{x}") for x in ("kept", "shown", "segged", "summed", "evac"))
        read = [m.sem(f"l3s_read{j}") for j in range(2)]
        stored = [m.sem(f"l3s_stored{j}") for j in range(2)]
        with nc.Block() as block:
            @block.sync
            def _(sp):
                def load(s, par):
                    if not first(s, 2):
                        wait_apart(sp, C, (summed, s + (-1)))
                    sp.dma_start(M[:, par, :, :], rows(by_src, s, KC)).then_inc(read[par], 16)

                def store(s, par):
                    wait_apart(sp, C, (evac, s + 1))
                    sp.dma_start(rows(table_s, s, KC), res[:, par, :, :]).then_inc(stored[par], 16)
                run_steps(sp, n, [(0, load), (1, store)])
                all_landed(sp, stored, n)

            @block.vector
            def _(dve):
                def keep(s, par):
                    if not first(s, 2):
                        dve.wait_ge(shown, s + (-1))
                    nc.vector.tensor_copy(key[:, par, :], C.src_keys[:, bass.ds(s * KC, KC)]).then_inc(kept, 1)

                def compare(s, par):
                    dve.wait_ge(shown, s + 1)
                    if not first(s, 2):
                        dve.wait_ge(summed, s + (-1))
                    for j in range(KC):
                        ins = nc.vector.tensor_scalar(seg[:, par, j, :], C.bank[2 + par][:, j * P:(j + 1) * P], key[:, par, j:j + 1], None, ALU.is_equal)
                    ins.then_inc(segged, 1)

                def evacuate(s, par):
                    dve.wait_ge(summed, s + 1)
                    if not first(s, 2):
                        dve.wait_ge(stored[par], landed(s - 2, par))
                    nc.vector.tensor_copy(res[:, par, :, :], C.bank[par][:, :].rearrange("p (j d) -> p j d", j=KC)).then_inc(evac, 1)
                run_steps(dve, n, [(2, evacuate), (1, compare), (0, keep)])

            @block.tensor
            def _(pe):
                def show(s, par):
                    pe.wait_ge(kept, s + 1)
                    if not first(s, 2):
                        pe.wait_ge(segged, s + (-1))
                    for j in range(KC):
                        ins = nc.tensor.transpose(C.bank[2 + par][:, j * P:(j + 1) * P], key[:, par, j:j + 1].broadcast_to([P, P]), C.ident[:, :])
                    ins.then_inc(shown, 1)

                def total(s, par):
                    pe.wait_ge(segged, s + 1)
                    pe.wait_ge(read[par], landed(s, par))
                    if not first(s, 2):
                        pe.wait_ge(evac, s + (-1))
                    for j in range(KC):
                        ins = nc.tensor.matmul(C.bank[par][:, j * D:(j + 1) * D], seg[:, par, j, :], M[:, par, j, :], start=True, stop=True)
                    ins.then_inc(summed, 1)
                run_steps(pe, n, [(1, total), (0, show)])
        carry_over(nc, C, "l3sc", 1, table_s, zero)


def nodes_l3(nc, C, A, h3, x3, table_d, table_s, out):
    n = NODE_STEPS
    KP = KT * P
    with ExitStack() as ctx:
        m = Mem(nc, ctx)
        W1, W2 = m.sb("ne_W1", [P, 2, 2 * D]), m.sb("ne_W2", [P, 4, D])
        g1, b1, g2, b2 = (m.sb(f"ne_{x}", [P, k]) for x, k in (("g1", 4), ("b1", 4), ("g2", 2), ("b2", 2)))
        eps1 = m.sb("ne_eps", [P, 1])
        load_all(nc, C, "ne", [(W1[:, :, :], A["l3_w1"].rearrange("(h p) d -> p h d", p=P)), (W2[:, :, :], A["l3_w2"].rearrange("(h p) d -> p h d", p=P)),
                               (g1[:, :], A["l3_g1"]), (b1[:, :], A["l3_b1"]), (g2[:, :], A["l3_g2"]), (b2[:, :], A["l3_b2"]),
                               (eps1[:, :], A["l3_eps"].broadcast_to([P, 1]))])
        T = m.sb("ne_T", [P, n, 2, KP])
        scale1, bias1, scale2, bias2 = (m.sb(f"ne_{x}", [P, k]) for x, k in (("sc1", 4), ("bi1", 4), ("sc2", 2), ("bi2", 2)))
        with ExitStack() as inner:
            m = Mem(nc, inner)
            H3 = m.sb("ne_H3", [P, 2, KT, D])
            Gd, Gs = m.sb("ne_Gd", [P, 2, KT, D]), m.sb("ne_Gs", [P, 2, KT, D])
            H = m.sb("ne_H", [P, 2, KT, D + 1])
            slots_d, slots_s = m.sb("ne_slotsd", [P, 2, KT], U32), m.sb("ne_slotss", [P, 2, KT], U32)
            prep, part, built, grammed, turned, copied, slotted, masked = (m.sem(f"ne_{x}") for x in
                                                                ("prep", "part", "built", "grammed", "turned", "copied", "slotted", "masked"))
            hread = [m.sem(f"ne_hread{j}") for j in range(2)]
            got = [C.mem.sem(f"ne_got{j}") for j in range(2)]
            with nc.Block() as block:
                @block.sync
                def _(sp):
                    def load(s, r):
                        if not first(s, 2):
                            wait_apart(sp, C, (part, s + (-1)))
                        sp.dma_start(H3[:, r, :, :], rows(h3, s, KT)).then_inc(hread[r], 16)
                    run_steps(sp, n, [(0, load)])

                @block.gpsimd
                def _(pool):
                    def gather(s, r):
                        if not first(s, 2):
                            pool.wait_ge(built, s + (-1))
                        nc.gpsimd.tensor_copy(slots_d[:, r, :], C.slot_of[0][:, bass.ds(s * KT, KT)]).then_inc(slotted, 1)
                        copy_slots(nc, C, pool, s, r, slots_s, C.slot_of[1], slotted, 2)
                        gather_sums(nc, pool, s, r, slots_d, table_d, Gd, got)
                        gather_sums(nc, pool, s, r, slots_s, table_s, Gs, got)
                    run_steps(pool, n, [(0, gather)])

                @block.vector
                def _(dve):
                    nc.vector.tensor_scalar(eps1[:, :], eps1[:, :], 1.0, None, ALU.add).then_inc(prep, 1)
                    nc.vector.memset(H[:, 0, :, D:D + 1], 1.0).then_inc(prep, 1)
                    nc.vector.memset(H[:, 1, :, D:D + 1], 1.0).then_inc(prep, 1)
                    dve.wait_ge(prep, 3)

                    def make(s, r):
                        dve.wait_ge(hread[r], landed(s, r))
                        dve.wait_ge(got[r], landed(s, r, 2 * KT))
                        nc.vector.scalar_tensor_tensor(out=Gd[:, r, :, :], in0=H3[:, r, :, :], scalar=eps1[:, 0:1], in1=Gd[:, r, :, :],
                                                       op0=ALU.mult, op1=ALU.add).then_inc(part, 1)
                        dve.wait_ge(part, s + 1)
                        if not first(s, 2):
                            dve.wait_ge(turned, s + (-1))
                        ins = nc.vector.tensor_tensor(H[:, r, :, 0:D], Gd[:, r, :, :], Gs[:, r, :, :], ALU.add)
                        if last_step(s, n):
                            ins.then_inc(masked, 1)
                            dve.wait_ge(masked, 1)
                            ins = nc.vector.tensor_scalar(H[:, r, KT - 1, :], H[:, r, KT - 1, :], C.node_ok[:, 0:1], None, ALU.mult)
                        ins.then_inc(built, 1)
                    run_steps(dve, n, [(0, make)])

                @block.tensor
                def _(pe):
                    pe.wait_ge(prep, 3)

                    def work(s, r):
                        pe.wait_ge(built, s + 1)
                        for k in range(KT):
                            for h in range(2):
                                nc.tensor.matmul(C.bank[h][:, 0:D + 1], H[:, r, k, h * P:(h + 1) * P], H[:, r, k, :],
                                                 start=first(s, 1) and k == 0, stop=last_step(s, n) and k == KT - 1)
                        if not first(s, 2):
                            pe.wait_ge(copied, s + (-1))
                        transpose_tiles(nc, C, 2 + 2 * r, H[:, r, :, :]).then_inc(turned, 1)
                    run_steps(pe, n, [(0, work)])

                @block.scalar
                def _(act):
                    def copy(s, r):
                        act.wait_ge(turned, s + 1)
                        nc.scalar.activation(T[:, bass.ds(s, 1), :, :].rearrange("p o h e -> p (o h) e"), C.banks(2 + 2 * r, 2, 2), ACT.Copy).then_inc(copied, 1)
                    run_steps(act, n, [(0, copy)])

            gram, prod, mean, ex2, tmp = m.sb("ne_gram", [P, 2, D + 1]), m.sb("ne_prod", [P, 2, 2 * D]), m.sb("ne_mean", [P, 4]), m.sb("ne_ex2", [P, 4]), m.sb("ne_tmp", [P, 4])
            v, t, a = m.sem("ne_v"), m.sem("ne_t"), m.sem("ne_a")
            with nc.Block() as block:
                @block.vector
                def _(dve):
                    k = [0]

                    def link(ins):
                        ins.then_inc(v, 1)
                        k[0] += 1
                        dve.wait_ge(v, k[0])

                    for h in range(2):
                        link(nc.vector.tensor_copy(gram[:, h, :], C.bank[h][:, 0:D + 1]))
                    dve.wait_ge(t, 1)
                    for h in range(2):
                        link(nc.vector.tensor_tensor(prod[:, h, :], C.bank[2 + h][:, :], W1[:, h, :], ALU.mult))
                    dve.wait_ge(t, 2)
                    link(nc.vector.tensor_scalar(mean[:, :], C.bank[4][:, 0:4], 1.0 / N, None, ALU.mult))
                    link(nc.vector.tensor_scalar(ex2[:, :], C.bank[5][:, 0:4], 1.0 / N, None, ALU.mult))
                    link(nc.vector.tensor_tensor(tmp[:, :], mean[:, :], mean[:, :], ALU.mult))
                    link(nc.vector.tensor_tensor(ex2[:, :], ex2[:, :], tmp[:, :], ALU.subtract))
                    link(nc.vector.tensor_scalar(ex2[:, :], ex2[:, :], 0.0, None, ALU.max))
                    dve.wait_ge(a, 1)
                    link(nc.vector.reciprocal(scale1[:, :], tmp[:, :]))
                    link(nc.vector.tensor_tensor(scale1[:, :], scale1[:, :], g1[:, :], ALU.mult))
                    link(nc.vector.tensor_tensor(tmp[:, :], scale1[:, :], mean[:, :], ALU.mult))
                    link(nc.vector.tensor_tensor(bias1[:, :], b1[:, :], tmp[:, :], ALU.subtract))

                @block.scalar
                def _(act):
                    act.wait_ge(v, 9)
                    nc.scalar.activation(tmp[:, :], ex2[:, :], ACT.Sqrt, bias=C.eps[:, 0:1]).then_inc(a, 1)

                @block.tensor
                def _(pe):
                    pe.wait_ge(v, 2)
                    for q in range(2):
                        for h in range(2):
                            ins = nc.tensor.matmul(C.bank[2 + q][:, :], gram[:, h, q * P:(q + 1) * P], W1[:, h, :], start=h == 0, stop=h == 1)
                    ins.then_inc(t, 1)
                    for o in range(4):
                        for h in range(2):
                            nc.tensor.matmul(C.bank[4][:, o:o + 1], W1[:, h, o * P:(o + 1) * P], gram[:, h, D:D + 1], start=h == 0, stop=h == 1)
                    pe.wait_ge(v, 4)
                    for o in range(4):
                        for h in range(2):
                            ins = nc.tensor.matmul(C.bank[5][:, o:o + 1], prod[:, h, o * P:(o + 1) * P], C.ones[:, 0:1], start=h == 0, stop=h == 1)
                    ins.then_inc(t, 1)

        with ExitStack() as inner:
            m = Mem(nc, inner)
            R1 = m.sb("nf_R1", [P, 2, 4, KP])
            st = m.sb("nf_st", [P, 2, n, 6])
            one, relued, two, kept, sampled = (m.sem(f"nf_{x}") for x in ("one", "relued", "two", "kept", "sampled"))
            with nc.Block() as block:
                @block.tensor
                def _(pe):
                    def layer1(s, r):
                        for o in range(4):
                            if not first(s, 1):
                                pe.wait_ge(relued, s * 4 + (o - 3))
                            for h in range(2):
                                ins = nc.tensor.matmul(C.bank[o][:, :], W1[:, h, o * P:(o + 1) * P],
                                                       T[:, bass.ds(s, 1), h, :].rearrange("p o e -> p (o e)"), start=h == 0, stop=h == 1)
                            ins.then_inc(one, 1)

                    def layer2(s, r):
                        pe.wait_ge(relued, s * 4 + 4)
                        if not first(s, 2):
                            pe.wait_ge(kept, s * 2 + (-2))
                        for q in range(2):
                            for o in range(4):
                                ins = nc.tensor.matmul(C.bank[4 + 2 * r + q][:, :], W2[:, o, q * P:(q + 1) * P], R1[:, r, o, :], start=o == 0, stop=o == 3)
                            ins.then_inc(two, 1)
                    run_steps(pe, n, [(0, layer1), (1, layer2)])

                @block.scalar
                def _(act):
                    def relu(s, r):
                        if not first(s, 2):
                            act.wait_ge(two, s * 2 + (-2))
                        for o in range(4):
                            act.wait_ge(one, s * 4 + (o + 1))
                            nc.scalar.activation(R1[:, r, o, :], C.bank[o][:, :], ACT.Relu, bias=bias1[:, o:o + 1], scale=scale1[:, o:o + 1]).then_inc(relued, 1)
                    run_steps(act, n, [(0, relu)])

                @block.vector
                def _(dve):
                    def keep(s, r):
                        for q in range(2):
                            dve.wait_ge(two, s * 2 + (q + 1))
                            nc.vector.tensor_copy(T[:, bass.ds(s, 1), q, :].rearrange("p o e -> p (o e)"), C.bank[4 + 2 * r + q][:, :]).then_inc(kept, 1)
                        for q in range(2):
                            wait_apart(dve, C, (kept, s * 2 + (q + 1)))
                            w = KP - P + LAST_NODES if last_step(s, n) else KP
                            nc.vector.bn_stats(st[:, q, bass.ds(s, 1), :].rearrange("p o k -> p (o k)"),
                                               T[:, bass.ds(s, 1), q, 0:w].rearrange("p o e -> p (o e)")).then_inc(sampled, 1)
                    run_steps(dve, n, [(0, keep)])

            mv, sd, tmp = m.sb("nf_mv", [P, 2, 2]), m.sb("nf_sd", [P, 2]), m.sb("nf_tmp", [P, 2])
            v, a = m.sem("nf_v"), m.sem("nf_a")
            with nc.Block() as block:
                @block.vector
                def _(dve):
                    for q in range(2):
                        nc.vector.bn_aggr(mv[:, q, :], st[:, q, :, :]).then_inc(v, 1)
                    dve.wait_ge(a, 1)
                    nc.vector.reciprocal(scale2[:, :], sd[:, :]).then_inc(v, 1)
                    dve.wait_ge(v, 3)
                    nc.vector.tensor_tensor(scale2[:, :], scale2[:, :], g2[:, :], ALU.mult).then_inc(v, 1)
                    dve.wait_ge(v, 4)
                    nc.vector.tensor_tensor(tmp[:, :], scale2[:, :], mv[:, :, 0], ALU.mult).then_inc(v, 1)
                    dve.wait_ge(v, 5)
                    nc.vector.tensor_tensor(bias2[:, :], b2[:, :], tmp[:, :], ALU.subtract).then_inc(v, 1)

                @block.scalar
                def _(act):
                    act.wait_ge(v, 2)
                    nc.scalar.activation(sd[:, :], mv[:, :, 1], ACT.Sqrt, bias=C.eps[:, 0:1]).then_inc(a, 1)

        m = Mem(nc, ctx)
        R2 = m.sb("ng_R2", [P, 2, 2, KP])
        X, O = m.sb("ng_X", [P, 2, KT, D]), m.sb("ng_O", [P, 2, KT, D])
        relued, turned, added = (m.sem(f"ng_{x}") for x in ("relued", "turned", "added"))
        xread = [m.sem(f"ng_xread{j}") for j in range(2)]
        stored = [m.sem(f"ng_stored{j}") for j in range(2)]
        tail_put = m.sem("ng_tail")
        with nc.Block() as block:
            @block.sync
            def _(sp):
                def load(s, r):
                    if not first(s, 2):
                        wait_apart(sp, C, (added, s + (-1)))
                    sp.dma_start(X[:, r, :, :], rows(x3, s, KT)).then_inc(xread[r], 16)

                def store(s, r):
                    wait_apart(sp, C, (added, s + 1))
                    if last_step(s, n):
                        full = s * KT * P
                        sp.dma_start(out[full:full + (KT - 1) * P, :].rearrange("(j p) d -> p j d", p=P), O[:, r, 0:KT - 1, :]).then_inc(stored[r], 16)
                        sp.dma_start(out[full + (KT - 1) * P:N, :], O[0:LAST_NODES, r, KT - 1, :]).then_inc(tail_put, 16)
                    else:
                        sp.dma_start(rows(out, s, KT), O[:, r, :, :]).then_inc(stored[r], 16)
                run_steps(sp, n, [(0, load), (1, store)])
                all_landed(sp, stored, n)
                sp.wait_ge(tail_put, 16)

            @block.scalar
            def _(act):
                def relu(s, r):
                    if not first(s, 2):
                        act.wait_ge(turned, s + (-1))
                    for q in range(2):
                        ins = nc.scalar.activation(R2[:, r, q, :], T[:, bass.ds(s, 1), q, :].rearrange("p o e -> p (o e)"), ACT.Relu,
                                                   bias=bias2[:, q:q + 1], scale=scale2[:, q:q + 1])
                    ins.then_inc(relued, 1)
                run_steps(act, n, [(0, relu)])

            @block.tensor
            def _(pe):
                def turn(s, r):
                    pe.wait_ge(relued, s + 1)
                    if not first(s, 2):
                        pe.wait_ge(added, s + (-1))
                    for k in range(KT):
                        for q in range(2):
                            ins = nc.tensor.transpose(C.bank[2 * r + k // 2][:, (k % 2) * D + q * P:(k % 2) * D + (q + 1) * P],
                                                      R2[:, r, q, k * P:(k + 1) * P], C.ident[:, :])
                    ins.then_inc(turned, 1)
                run_steps(pe, n, [(0, turn)])

            @block.vector
            def _(dve):
                def add(s, r):
                    dve.wait_ge(turned, s + 1)
                    dve.wait_ge(xread[r], landed(s, r))
                    if not first(s, 2):
                        dve.wait_ge(stored[r], landed(s - 2, r))
                    nc.vector.tensor_tensor(O[:, r, :, :], C.banks(2 * r, 2, KT), X[:, r, :, :], ALU.add).then_inc(added, 1)
                run_steps(dve, n, [(0, add)])


class Constants:
    pass


def build(nc, A, out):
    with ExitStack() as ctx:
        m = Mem(nc, ctx, clear=False)
        C = Constants()
        psum = m.ps("psum", [P, 8, 512])
        C.bank = [psum[:, k, :] for k in range(8)]
        C.banks = lambda k, nb, parts: psum[:, k:k + nb, :].rearrange("p b e -> p (b e)").rearrange("p (j d) -> p j d", j=parts)
        C.ones, C.ident, C.upper, C.lower = (m.sb(x, [P, P]) for x in ("ones", "ident", "upper", "lower"))
        C.eps, C.part, C.node_ok, C.edge_ok = (m.sb(x, [P, 1]) for x in ("eps", "part", "node_ok", "edge_ok"))
        C.iota, C.chunk0 = m.sb("iota", [P, NT]), m.sb("chunk0", [P, NT])
        C.slot_of = [m.sb(f"slot_of{k}", [P, NT], U32) for k in range(2)]
        edges = ctx.enter_context(ExitStack())
        me = Mem(nc, edges)
        C.rec = me.sb("sorted_rec", [P, NC, REC], I32)
        C.weight, C.lock, C.decay, C.src_keys = (me.sb(x, [P, NC]) for x in ("weight", "lock", "decay_f", "src_keys"))
        C.coef = me.sb("coef", [P, NC, 20])
        C.same_d = me.sb("same_d", [P, EP], BF16)
        C.carry = [me.sb(f"carry{k}", [P, NC]) for k in range(2)]
        C.fix_row = [me.sb(f"fix_row{k}", [P, 1], U32) for k in range(2)]
        C.passed = m.sem("passed")
        C.mem = m
        rec_d, rec_s = m.dram("rec_d", [EP, REC], I32), m.dram("rec_s", [EP, REC], I32)
        tables = [m.dram(f"sums{k}", [ZROW + 1, D]) for k in range(10)]
        by_src = m.dram("by_src", [EP, D])
        x1, h1, x2, e0, h2, x3, h3 = (m.dram(x, [NP, D]) for x in ("x1", "h1", "x2", "e0", "h2", "x3", "h3"))

        make_constants(nc, C)
        index_nodes(nc, C, A, rec_d, rec_s)
        sort_tables(nc, C, A, rec_d, rec_s)

        biases = me.sb("layer_bias", [P, 5, D])
        load_all(nc, C, "bias", [(biases[:, 0, :], A["l1_b"].broadcast_to([P, D])), (biases[:, 1, :], A["l2_bias1"].broadcast_to([P, D])),
                                 (biases[:, 2, :], A["l2_bias2"].broadcast_to([P, D]))])
        zs = m.sem("zero_made")
        with nc.Block() as block:
            @block.vector
            def _(dve):
                nc.vector.memset(biases[:, 3, :], 0.0).then_inc(zs, 1)

        with ExitStack() as l0:
            ml = Mem(nc, l0)
            Y, cb = ml.sb("Y", [P, NC, D]), ml.sb("cb", [P, D])
            for i in range(4):
                l0_layer(nc, C, A, i, tables[i], tables[i - 1] if i else None, Y)
                load_all(nc, C, f"cb{i}", [(cb[:, :], A["l0_cb"][i:i + 1, :].broadcast_to([P, D]))])
                carry_over(nc, C, f"l0c{i}", 0, tables[i], cb)
        l0_total(nc, C, tables[0:4], tables[4], A["l0_cb"])
        nodes_l0(nc, C, A, tables[4], x1, h1)
        with ExitStack() as l1:
            Wt = Mem(nc, l1).sb("Wt", [P, 2, D])
            l1_weights(nc, C, A, Wt)
            l1_edges(nc, C, A, h1, tables[5], biases[:, 0, :], Wt)
        nodes_l1(nc, C, x1, tables[5], x2, e0)
        l2_edges(nc, C, A, 1, e0, tables[6], biases[:, 1, :])
        nodes_l2a(nc, C, A, e0, tables[6], h2)
        l2_edges(nc, C, A, 2, h2, tables[7], biases[:, 2, :])
        nodes_l2b(nc, C, A, h2, e0, x2, tables[7], x3, h3)
        l3_edges(nc, C, A, h3, by_src, tables[8], tables[9], biases[:, 3, :])
        edges.close()
        nodes_l3(nc, C, A, h3, x3, tables[8], tables[9], out)


def lay(inputs):
    import numpy as _np
    get = lambda k: _np.asarray(inputs[k])
    src, dst, typ, w, lock = (get(k) for k in ("src", "dst", "edge_type_240", "edge_weight", "L1_gnn_node_lock"))

    def filled(a, fill, n):
        return _np.concatenate([a, _np.full((n - len(a),) + a.shape[1:], fill, a.dtype)])

    def cols(a, fill, n):
        return filled(a, fill, n).reshape(-1, P).T

    def by_part(v):
        return v.reshape(-1, P).T
    out = {
        "keys": _np.concatenate([cols(dst, PAD_KEY, EP), cols(src, PAD_KEY, EP), cols(lock, NO_KEY, LC * P)], axis=1),
        "fields": _np.stack([cols(src, PAD_KEY, EP), cols(dst, PAD_KEY, EP), cols(w, 0, EP).view(_np.int32), cols(typ, 0, EP)], axis=2),
        "x": filled(get("x"), 0, NP), "attr": filled(get("edge_attr_256"), 0, EP),
        "comp": _np.concatenate([get("L2_gnn_comp1"), get("L2_gnn_comp2")], axis=1),
        "now": get("L2_gnn_current_time").reshape(1, 1),
        "l0_cb": get("L0_gnn_conv_b"), "l0_lb": get("L0_gnn_ln_bias"),
        "l0_ls": get("L0_gnn_ln_scale"), "l0_w": get("L0_gnn_conv_w"),
        "l0_pw": get("L0_gnn_post_w"), "l0_pb": get("L0_gnn_post_b").reshape(1, D),
        "l1_wt": get("L1_gnn_W").T, "l1_b": get("L1_gnn_b").reshape(1, D),
        "l2_basis1": get("L2_gnn_basis1"), "l2_basis2": get("L2_gnn_basis2"),
        "l2_bias1": get("L2_gnn_bias1").reshape(1, D), "l2_bias2": get("L2_gnn_bias2").reshape(1, D),
        "l2_lw1": get("L2_gnn_loop_w1"), "l2_lw2": get("L2_gnn_loop_w2"),
        "l2_g": get("L2_gnn_ln_g").reshape(1, D), "l2_b": get("L2_gnn_ln_b").reshape(1, D),
        "l3_w1": get("L3_gnn_W1"), "l3_w2": get("L3_gnn_W2"), "l3_eps": get("L3_gnn_epsilon").reshape(1, 1),
        "l3_g1": by_part(get("L3_gnn_gamma1")), "l3_b1": by_part(get("L3_gnn_beta1")),
        "l3_g2": by_part(get("L3_gnn_gamma2")), "l3_b2": by_part(get("L3_gnn_beta2")),
    }
    return {"in_" + k: _np.ascontiguousarray(a) for k, a in out.items()}


def kernel(**inputs):
    import concourse.bacc as _bacc
    from concourse import mybir as _mybir
    from concourse.bass_utils import run_bass_kernel_spmd as _run
    nc = _bacc.Bacc("TRN2", target_bir_lowering=False, num_devices=1)
    arrays = lay(inputs)
    A = {k[3:]: nc.dram_tensor(k, a.shape, _mybir.dt.from_np(a.dtype), kind="ExternalInput").ap() for k, a in arrays.items()}
    out = nc.dram_tensor("out", (N, D), _mybir.dt.float32, kind="ExternalOutput").ap()
    build(nc, A, out)
    r = _run(nc, [arrays], core_ids=[0])
    return r.results[0]["out"]
```

```python
import numpy as np
import concourse.bass as bass
from concourse import mybir
from contextlib import ExitStack

F32, F32R, BF16, I32, U32 = mybir.dt.float32, mybir.dt.float32r, mybir.dt.bfloat16, mybir.dt.int32, mybir.dt.uint32
ACT = mybir.ActivationFunctionType
ALU = mybir.AluOpType

P = 128
N, D, E = 18870, 256, 9435
NT = -(-N // P)
NP = NT * P
NC = -(-E // P)
EP = NC * P
KT = 4
KC = 2
NODE_STEPS = NT // KT
EDGE_STEPS = NC // KC
ZROW = EP
LAST_NODES = N - (NT - 1) * P
LAST_EDGES = E - (NC - 1) * P
PAD_KEY = NP - 1
NO_KEY = 1 << 20
LOCKS = 1000
LC = -(-LOCKS // P)
REC = 8
R_SRC, R_DST, R_W, R_TYPE, R_EID, R_RANKS, R_MAPS, R_LOCK = range(REC)
EPS = 1e-5


def run_steps(eng, n, stages, unroll=2):
    deep = max(lag for lag, _ in stages)
    head = deep + unroll + -deep % unroll
    tail = n - 1 - (n - 1 - head) % unroll
    for s in range(head):
        for lag, fn in stages:
            if s >= lag:
                fn(s - lag, (s - lag) % unroll)
    if tail > head:
        with eng.Fori(0, (tail - head) // unroll) as turn:
            for j in range(unroll):
                for lag, fn in stages:
                    fn(turn * unroll + (head + j - lag), (j - lag) % unroll)
    else:
        tail = head
    for s in range(tail, n + deep):
        for lag, fn in stages:
            if 0 <= s - lag < n:
                fn(s - lag, (s - lag) % unroll)


def last_step(s, n):
    return isinstance(s, int) and s == n - 1


def first(s, k):
    return isinstance(s, int) and s < k


def settle(eng, C, s):
    if not isinstance(s, int):
        eng.sem_inc(C.passed, 1)


def wait_apart(eng, C, *waits):
    for sem, value in waits:
        eng.wait_ge(sem, value)
    settle(eng, C, waits[-1][1])


def landed(s, r, n=1, ring=2):
    return (s - r) * (16 * n // ring) + 16 * n


class Mem:

    def __init__(self, nc, ctx, clear=True):
        self.nc, self.ctx, self.clear = nc, ctx, clear
        self.numbers = []
        if clear:
            ctx.callback(self.zero)

    def zero(self):
        numbers = sorted(self.numbers)
        while numbers:
            n = 1
            while n < len(numbers) and numbers[n] == numbers[0] + n:
                n += 1
            self.nc.sync.sem_clear(range(numbers[0], numbers[0] + n))
            numbers = numbers[n:]

    def sb(self, name, shape, dt=F32):
        return self.ctx.enter_context(self.nc.sbuf_tensor(name, shape, dt))

    def ps(self, name, shape, dt=F32):
        return self.ctx.enter_context(self.nc.psum_tensor(name, shape, dt))

    def sem(self, name):
        handle = self.ctx.enter_context(self.nc.semaphore(name))
        self.numbers.append(handle.num)
        return handle

    def dram(self, name, shape, dt=F32):
        return self.nc.dram_tensor(name, shape, dt).ap()


def make_constants(nc, C):
    with ExitStack() as ctx:
        s = Mem(nc, ctx).sem("const_made")
        t = Mem(nc, ctx).sem("const_cast")
        iota_i = Mem(nc, ctx).sb("iota_i", [P, NT], I32)
        part_i = Mem(nc, ctx).sb("part_i", [P, 1], I32)
        with nc.Block() as block:
            @block.gpsimd
            def _(pool):
                nc.gpsimd.memset(C.ones[:, :], 1.0).then_inc(s, 1)
                nc.gpsimd.memset(C.eps[:, :], EPS).then_inc(s, 1)
                nc.gpsimd.iota(iota_i[:, :], pattern=[[1, NT]], base=0, channel_multiplier=0).then_inc(s, 1)
                nc.gpsimd.iota(part_i[:, :], pattern=[[0, 1]], base=0, channel_multiplier=1).then_inc(s, 1)
                pool.wait_ge(s, 4)
                nc.gpsimd.memset(C.ident[:, :], 0.0).then_inc(s, 1)
                pool.wait_ge(s, 5)
                nc.gpsimd.affine_select(out=C.ident[:, :], in_=C.ident[:, :], compare_op=ALU.not_equal, fill=1.0,
                                        base=0, pattern=[[-1, P]], channel_multiplier=1).then_inc(s, 1)
                nc.gpsimd.affine_select(out=C.upper[:, :], in_=C.ones[:, :], compare_op=ALU.is_gt, fill=0.0,
                                        base=0, pattern=[[1, P]], channel_multiplier=-1).then_inc(s, 1)
                nc.gpsimd.affine_select(out=C.lower[:, :], in_=C.ones[:, :], compare_op=ALU.is_gt, fill=0.0,
                                        base=0, pattern=[[-1, P]], channel_multiplier=1).then_inc(s, 1)
                nc.gpsimd.affine_select(out=C.node_ok[:, :], in_=C.ones[:, 0:1], compare_op=ALU.is_gt, fill=0.0,
                                        base=LAST_NODES, pattern=[[0, 1]], channel_multiplier=-1).then_inc(s, 1)
                nc.gpsimd.affine_select(out=C.edge_ok[:, :], in_=C.ones[:, 0:1], compare_op=ALU.is_gt, fill=0.0,
                                        base=LAST_EDGES, pattern=[[0, 1]], channel_multiplier=-1).then_inc(s, 1)

            @block.vector
            def _(dve):
                dve.wait_ge(s, 4)
                nc.vector.tensor_copy(C.iota[:, :], iota_i[:, :]).then_inc(t, 1)
                nc.vector.tensor_copy(C.part[:, :], part_i[:, :]).then_inc(t, 1)
                dve.wait_ge(t, 1)
                nc.vector.tensor_scalar(C.chunk0[:, :], C.iota[:, :], float(P), None, ALU.mult).then_inc(t, 1)


def index_nodes(nc, C, cols_in, rec_d, rec_s):
    with ExitStack() as ctx:
        m = Mem(nc, ctx)
        NK = 2 * NC + LC
        keys = m.sb("keys", [P, NK], I32)
        parts_i = m.sb("parts_i", [P, 2, NK], I32)
        code = m.sb("code", [P, NK, 3])
        oh_lo = m.sb("oh_lo", [P, 2, KC, P], BF16)
        oh_hi = m.sb("oh_hi", [P, 2, KC, NT], BF16)
        count = [m.sb(f"count{k}", [P, NT]) for k in range(3)]
        scan = [[m.sb(f"scan{k}{j}", [P, NT]) for j in range(2)] for k in range(2)]
        found = m.sb("found", [P, NT])
        start = [m.sb(f"start{k}", [P, NT]) for k in range(2)]
        slot = [m.sb(f"slot{k}", [P, NT]) for k in range(2)]
        tab = m.sb("tab", [P, 2, 2, 2, NT])
        Hp, Sp = C.bank[0:3], C.bank[3:5]
        loaded, split, coded, counted = m.sem("keys_loaded"), m.sem("keys_split"), m.sem("codes_made"), m.sem("codes_counted")
        small, summed = m.sem("table_steps"), m.sem("table_sums")
        groups = [(0, NC, 0), (NC, NC, 1), (2 * NC, LC, 2)]
        with nc.Block() as block:
            @block.sync
            def _(sp):
                sp.dma_start(keys[:, :], cols_in["keys"]).then_inc(loaded, 16)

            @block.vector
            def _(dve):
                dve.wait_ge(loaded, 16)
                nc.vector.tensor_scalar(parts_i[:, 0, :], keys[:, :], P - 1, None, ALU.bitwise_and).then_inc(split, 1)
                nc.vector.tensor_scalar(parts_i[:, 1, :], keys[:, :], 7, None, ALU.arith_shift_right).then_inc(split, 1)
                dve.wait_ge(split, 2)
                nc.vector.tensor_copy(code[:, :, 0], keys[:, :]).then_inc(split, 1)
                nc.vector.tensor_copy(code[:, :, 1], parts_i[:, 0, :]).then_inc(split, 1)
                nc.vector.tensor_copy(code[:, :, 2], parts_i[:, 1, :]).then_inc(split, 1)
                dve.wait_ge(split, 5)
                done = 0
                for col, n, t in groups:
                    def codes(s, par, col=col, done=done):
                        if not first(s, 2):
                            dve.wait_ge(counted, s * KC + (done - KC))
                        elif done:
                            dve.wait_ge(counted, done)
                        for j in range(KC):
                            c = s * KC + (col + j)
                            nc.vector.tensor_scalar(oh_lo[:, par, j, :], C.iota[:, 0:P], code[:, bass.ds(c, 1), 1],
                                                    None, ALU.is_equal).then_inc(coded, 1)
                            nc.vector.tensor_scalar(oh_hi[:, par, j, :], C.iota[:, :], code[:, bass.ds(c, 1), 2],
                                                    None, ALU.is_equal).then_inc(coded, 1)
                    run_steps(dve, n // KC, [(0, codes)])
                    done += n
                dve.wait_ge(counted, done)
                for k in range(3):
                    nc.vector.tensor_copy(count[k][:, :], Hp[k][:, 0:NT]).then_inc(small, 1)

            @block.tensor
            def _(pe):
                done = 0
                for col, n, t in groups:
                    def tally(s, par, done=done, n=n, t=t):
                        for j in range(KC):
                            pe.wait_ge(coded, s * (2 * KC) + (2 * done + 2 * j + 2))
                            nc.tensor.matmul(Hp[t][:, 0:NT], oh_lo[:, par, j, :], oh_hi[:, par, j, :],
                                             start=first(s, 1) and j == 0,
                                             stop=isinstance(s, int) and s == n // KC - 1 and j == KC - 1
                                             ).then_inc(counted, 1)
                    run_steps(pe, n // KC, [(0, tally)])
                    done += n
        with nc.Block() as block:
            @block.tensor
            def _(pe):
                for k in range(2):
                    nc.tensor.matmul(Sp[k][:, 0:NT], C.upper[:, :], count[k][:, :], start=True, stop=True).then_inc(summed, 1)
                    nc.tensor.matmul(Sp[k][:, NT:2 * NT], C.ones[:, :], count[k][:, :], start=True, stop=True).then_inc(summed, 1)

            @block.vector
            def _(dve):
                n = [3]

                def link(ins):
                    ins.then_inc(small, 1)
                    n[0] += 1
                    dve.wait_ge(small, n[0])

                for k in range(2):
                    dve.wait_ge(summed, 2 * k + 2)
                    a, b = scan[k]
                    link(nc.vector.memset(a[:, :], 0.0))
                    link(nc.vector.tensor_copy(a[:, 1:NT], Sp[k][:, NT:2 * NT - 1]))
                    sh = 1
                    while sh < NT:
                        link(nc.vector.tensor_copy(b[:, 0:sh], a[:, 0:sh]))
                        link(nc.vector.tensor_tensor(b[:, sh:NT], a[:, sh:NT], a[:, 0:NT - sh], ALU.add))
                        a, b = b, a
                        sh *= 2
                    link(nc.vector.tensor_tensor(start[k][:, :], a[:, :], Sp[k][:, 0:NT], ALU.add))
                    link(nc.vector.tensor_scalar(found[:, :], count[k][:, :], 0.0, None, ALU.is_gt))
                    link(nc.vector.tensor_tensor(found[:, NT - 1:NT], found[:, NT - 1:NT], C.node_ok[:, :], ALU.mult))
                    link(nc.vector.tensor_tensor(slot[k][:, :], start[k][:, :], count[k][:, :], ALU.add))
                    link(nc.vector.tensor_scalar(slot[k][:, :], slot[k][:, :], -1.0 - ZROW, None, ALU.add))
                    link(nc.vector.tensor_tensor(slot[k][:, :], slot[k][:, :], found[:, :], ALU.mult))
                    link(nc.vector.tensor_scalar(slot[k][:, :], slot[k][:, :], float(ZROW), None, ALU.add))
                    link(nc.vector.tensor_copy(C.slot_of[k][:, :], slot[k][:, :]))
                for par in range(2):
                    link(nc.vector.tensor_scalar(tab[:, par, 0, 1, :], count[2][:, :], 0.0, None, ALU.is_gt))
                    link(nc.vector.tensor_copy(tab[:, par, 1, 1, :], slot[0][:, :]))
                for k in range(2):
                    link(nc.vector.tensor_copy(tab[:, 0, k, 0, :], start[k][:, :]))

        key = m.sb("key", [P, 2, 2, 3])
        hot = m.sb("hot", [P, 2, 2, P])
        lo1 = m.sb("lo1", [P, 2, 2, P], BF16)
        hi1 = m.sb("hi1", [P, 2, 2, NT], BF16)
        junk_in = m.sb("junk_in", [P, 2, P])
        junk_table = m.sb("junk_table", [P, 4, NT])
        before = m.sb("before", [P, 2, 2, 3])
        rank = m.sb("rank", [P, 2, 2], U32)
        rec = m.sb("rec", [P, 2, REC], I32)
        recs = m.sb("recs", [P, NC, 4], I32)
        run = [b[:, 0:2 * NT].rearrange("p (k t) -> p k t", k=2) for b in C.bank[0:2]]
        bc = [b[:, :].rearrange("p (k f e) -> p k f e", k=2, f=2) for b in C.bank[2:4]]
        got = [C.bank[4:6], C.bank[6:8]]
        keyed, shown, hotted, noted = m.sem("key_copied"), m.sem("keys_shown"), m.sem("hot_made"), m.sem("counted_in_chunk")
        coded_d, coded2, upd, tabbed = m.sem("codes_by_dst"), m.sem("codes_by_src"), m.sem("table_added"), m.sem("table_ready")
        looked, found_at, moved, packed = m.sem("looked_up"), m.sem("found_in_table"), m.sem("fields_moved"), m.sem("record_packed")

        def one_hot(eng, par, k):
            eng.tensor_scalar(lo1[:, par, k, :], C.iota[:, 0:P], key[:, par, k, 1:2], None, ALU.is_equal)
            return eng.tensor_scalar(hi1[:, par, k, :], C.iota[:, :], key[:, par, k, 2:3], None, ALU.is_equal)

        put, rld = [C.mem.sem(f"record_put{j}") for j in range(2)], m.sem("fields_loaded")
        with nc.Block() as block:
            @block.sync
            def _(sp):
                sp.dma_start(recs[:, :, :], cols_in["fields"]).then_inc(rld, 16)

            @block.vector
            def _(dve):
                def prepare(s, par):
                    if not first(s, 2):
                        dve.wait_ge(found_at, s * 4 + (-4))
                        dve.wait_ge(shown, s + (-1))
                        dve.wait_ge(coded2, s + (-1))
                        dve.wait_ge(upd, s + (-1))
                    nc.vector.tensor_copy(key[:, par, :, :], code[:, 0:2 * NC, :].rearrange("p (k c) f -> p k c f", k=2)[:, :, bass.ds(s, 1), :]
                                          .rearrange("p k o f -> p k (o f)")).then_inc(keyed, 1)
                    dve.wait_ge(keyed, s + 1)
                    one_hot(nc.vector, par, 0).then_inc(coded_d, 1)

                def count_in_chunk(s, par):
                    dve.wait_ge(shown, s + 1)
                    if not first(s, 2):
                        dve.wait_ge(looked, s + (-1))
                        dve.wait_ge(packed, s + (-1))
                    for k in range(2):
                        ins = nc.vector.tensor_scalar(hot[:, par, k, :], bc[par][:, k, 1, :], C.part[:, 0:1], None, ALU.is_equal)
                    ins.then_inc(hotted, 1)
                    for k in range(2):
                        if not first(s, 1):
                            dve.wait_ge(noted, s * 2 + (k - 1))
                        nc.vector.scalar_tensor_tensor(out=junk_in[:, k, :], in0=bc[par][:, k, 0, :],
                                                       scalar=key[:, par, k, 0:1], in1=C.lower[:, :],
                                                       op0=ALU.is_equal, op1=ALU.mult,
                                                       accum_out=before[:, par, k, 0:1]).then_inc(noted, 1)

                def table(s, par):
                    dve.wait_ge(upd, s + 1)
                    if not first(s, 1):
                        dve.wait_ge(tabbed, s)
                        dve.wait_ge(looked, s)
                    nc.vector.tensor_tensor(tab[:, 1 - par, :, 0, :], tab[:, par, :, 0, :], run[par], ALU.add).then_inc(tabbed, 1)

                def find(s, par):
                    dve.wait_ge(looked, s + 1)
                    for k in range(2):
                        for f in range(2):
                            if not first(s, 1):
                                dve.wait_ge(found_at, s * 4 + (2 * k + f - 3))
                            nc.vector.scalar_tensor_tensor(out=junk_table[:, 2 * k + f, :], in0=C.iota[:, :],
                                                           scalar=key[:, par, k, 2:3],
                                                           in1=got[par][k][:, f * NT:(f + 1) * NT],
                                                           op0=ALU.is_equal, op1=ALU.mult,
                                                           accum_out=before[:, par, k, 1 + f:2 + f]).then_inc(found_at, 1)
                    if not first(s, 2):
                        dve.wait_ge(put[par], landed(s - 2, par, 2))
                    nc.vector.tensor_copy(rec[:, par, 0:4], recs[:, bass.ds(s, 1), :]).then_inc(moved, 1)

                dve.wait_ge(rld, 16)
                run_steps(dve, NC, [(2, find), (1, count_in_chunk), (1, table), (0, prepare)])

            @block.scalar
            def _(act):
                def pack(s, par):
                    act.wait_ge(found_at, s * 4 + 4)
                    if not first(s, 2):
                        act.wait_ge(put[par], landed(s - 2, par, 2))
                    for k in range(2):
                        nc.scalar.activation(rank[:, par, k:k + 1], before[:, par, k, 0:1], ACT.Identity, bias=before[:, par, k, 1:2])
                    nc.scalar.activation(rec[:, par, R_EID:R_EID + 1], C.part[:, :], ACT.Identity, bias=C.chunk0[:, bass.ds(s, 1)])
                    nc.scalar.activation(rec[:, par, R_RANKS:R_RANKS + 1], before[:, par, 1, 0:1], ACT.Identity, bias=before[:, par, 1, 1:2])
                    nc.scalar.activation(rec[:, par, R_MAPS:R_MAPS + 1], before[:, par, 1, 2:3], ACT.Copy)
                    nc.scalar.activation(rec[:, par, R_LOCK:R_LOCK + 1], before[:, par, 0, 2:3], ACT.Copy).then_inc(packed, 1)
                run_steps(act, NC, [(2, pack)])

            @block.tensor
            def _(pe):
                def update(s, par):
                    pe.wait_ge(coded_d, s + 1)
                    pe.wait_ge(coded2, s + 1)
                    if not first(s, 2):
                        pe.wait_ge(tabbed, s + (-1))
                    for k in range(2):
                        ins = nc.tensor.matmul(run[par][:, k, :], lo1[:, par, k, :], hi1[:, par, k, :], start=True, stop=True)
                    ins.then_inc(upd, 1)

                def look(s, par):
                    pe.wait_ge(hotted, s + 1)
                    if not first(s, 1):
                        pe.wait_ge(tabbed, s)
                    if not first(s, 2):
                        pe.wait_ge(found_at, s * 4 + (-4))
                    for k in range(2):
                        ins = nc.tensor.matmul(got[par][k][:, 0:2 * NT], hot[:, par, k, :],
                                               tab[:, par, k, :, :].rearrange("p f t -> p (f t)"), start=True, stop=True)
                    ins.then_inc(looked, 1)

                def show(s, par):
                    pe.wait_ge(keyed, s + 1)
                    if not first(s, 2):
                        pe.wait_ge(noted, s * 2 + (-2))
                    for k in range(2):
                        for f in range(2):
                            ins = nc.tensor.transpose(bc[par][:, k, f, :], key[:, par, k, f:f + 1].broadcast_to([P, P]), C.ident[:, :])
                    ins.then_inc(shown, 1)
                run_steps(pe, NC, [(1, update), (1, look), (0, show)])

            @block.gpsimd
            def _(pool):
                def scatter(s, par):
                    wait_apart(pool, C, (moved, s + 1), (packed, s + 1))
                    for k, table in enumerate((rec_d, rec_s)):
                        nc.gpsimd.indirect_dma_start(
                            out=table, out_offset=bass.IndirectOffsetOnAxis(ap=rank[:, par, k:k + 1], axis=0),
                            in_=rec[:, par, :], in_offset=None).then_inc(put[par], 16)

                def codes(s, par):
                    wait_apart(pool, C, (keyed, s + 1), *([] if first(s, 2) else [(upd, s + (-1))]))
                    one_hot(nc.gpsimd, par, 1).then_inc(coded2, 1)
                run_steps(pool, NC, [(3, scatter), (0, codes)])
                for par in range(2):
                    pool.wait_ge(put[par], landed(NC - 2 + par, par, 2))




def rows(table, s, k):
    return table[bass.ds(s * (k * P), k * P), :].rearrange("(j p) d -> p j d", p=P)


def all_landed(eng, sems, n, k=1):
    for par in range(2):
        last = n - 1 - (n - 1 - par) % 2
        eng.wait_ge(sems[par], landed(last, par, k))


def spread(row, k):
    return row[:, :].rearrange("p (o d) -> p o d", o=1).broadcast_to([P, k, D])


class Norm:

    def __init__(self, m, C, name, K):
        self.C, self.K = C, K
        self.st = m.sb(f"{name}_st", [P, 2, K, 6])
        self.mv = m.sb(f"{name}_mv", [P, 2, K, 2])
        self.sd = m.sb(f"{name}_sd", [P, 2, K])
        self.scale = m.sb(f"{name}_scale", [P, 2, K])
        self.bias = m.sb(f"{name}_bias", [P, 2, K])
        self.sampled, self.averaged = m.sem(f"{name}_sampled"), m.sem(f"{name}_averaged")
        self.rooted, self.scaled, self.ready = m.sem(f"{name}_rooted"), m.sem(f"{name}_scaled"), m.sem(f"{name}_ready")

    def stats(self, nc, dve, s, par, tile):
        K = self.K
        settle(dve, self.C, s)
        for k in range(K):
            nc.vector.bn_stats(self.st[:, par, k, :], tile[:, k, :]).then_inc(self.sampled, 1)
        wait_apart(dve, self.C, (self.sampled, s * K + K))
        for k in range(K):
            ins = nc.vector.bn_aggr(self.mv[:, par, k, :], self.st[:, par, k, :])
        ins.then_inc(self.averaged, 1)

    def root(self, nc, act, s, par):
        act.wait_ge(self.averaged, s + 1)
        nc.scalar.activation(self.sd[:, par, :], self.mv[:, par, :, 1], ACT.Sqrt,
                             bias=self.C.eps[:, 0:1]).then_inc(self.rooted, 1)

    def finish(self, nc, dve, s, par):
        dve.wait_ge(self.rooted, s + 1)
        nc.vector.reciprocal(self.scale[:, par, :], self.sd[:, par, :]).then_inc(self.scaled, 1)
        dve.wait_ge(self.scaled, s + 1)
        nc.vector.scalar_tensor_tensor(out=self.bias[:, par, :], in0=self.mv[:, par, :, 0], scalar=-1.0,
                                       in1=self.scale[:, par, :], op0=ALU.mult, op1=ALU.mult).then_inc(self.ready, 1)

    def apply(self, nc, s, par, out, tile, func):
        for k in range(self.K):
            ins = nc.scalar.activation(out[:, k, :], tile[:, k, :], func, bias=self.bias[:, par, k:k + 1],
                                       scale=self.scale[:, par, k:k + 1])
        return ins


def sort_tables(nc, C, A, rec_d, rec_s):
    with ExitStack() as ctx:
        m = Mem(nc, ctx)
        keycol = m.sb("keycol", [P, 2, NC])
        kcol = m.sb("kcol", [P, 2, 2])
        shared = m.sb("shared", [P, 2, NC])
        row0 = m.sb("row0", [P, P])
        same_s = m.sb("same_s", [P, 2, P], BF16)
        skey = m.sb("skey", [P, NC], I32)
        last_key = m.sb("last_key", [P, 2])
        fix = m.sb("fix", [P, 2, 2])
        decay = m.sb("decay", [P, NC]); dmax = m.sb("dmax", [P, 4]); now = m.sb("now", [P, 1])
        top = m.sb("top", [1, P])
        loaded, cast, kept, shown, made = (m.sem(x) for x in ("rec_loaded", "rec_cast", "key_kept", "keys_shown", "same_made"))
        ends, fixed, timed, expd = (m.sem(x) for x in ("chunk_ends", "fix_steps", "decay_steps", "decay_exp"))
        peeked = m.sem("max_moved")
        with nc.Block() as block:
            @block.sync
            def _(sp):
                sp.dma_start(C.rec[:, :, :], rec_d.rearrange("(c p) k -> p c k", p=P)).then_inc(loaded, 16)
                sp.dma_start(skey[:, :], rec_s[:, R_SRC].rearrange("(c p) -> p c", p=P),
                             allow_slow_non_contiguous=True).then_inc(loaded, 16)
                sp.dma_start(now[:, :], A["now"].broadcast_to([P, 1])).then_inc(loaded, 16)

            @block.vector
            def _(dve):
                dve.wait_ge(loaded, 48)
                nc.vector.tensor_copy(keycol[:, 0, :], C.rec[:, :, R_DST]).then_inc(cast, 1)
                nc.vector.tensor_copy(keycol[:, 1, :], skey[:, :]).then_inc(cast, 1)
                nc.vector.tensor_copy(C.src_keys[:, :], skey[:, :]).then_inc(cast, 1)
                nc.vector.tensor_copy(C.weight[:, :], C.rec[:, :, R_W].bitcast(F32)).then_inc(cast, 1)
                nc.vector.memset(row0[:, :], 0.0).then_inc(cast, 1)
                dve.wait_ge(cast, 5)
                nc.vector.memset(row0[0:1, :], 1.0).then_inc(cast, 1)
                nc.vector.tensor_tensor(C.lock[:, :], C.rec[:, :, R_SRC], C.rec[:, :, R_DST], ALU.is_equal).then_inc(cast, 1)
                nc.vector.tensor_copy(decay[:, :], C.rec[:, :, R_LOCK]).then_inc(cast, 1)
                dve.wait_ge(cast, 8)
                nc.vector.tensor_tensor(C.lock[:, :], C.lock[:, :], decay[:, :], ALU.max).then_inc(cast, 1)
                dve.wait_ge(cast, 9)

                n = [0]

                def link(ins):
                    ins.then_inc(timed, 1)
                    n[0] += 1
                    dve.wait_ge(timed, n[0])

                link(nc.vector.tensor_scalar(decay[:, :], C.weight[:, :], now[:, 0:1], -1.0, ALU.subtract, ALU.mult))
                link(nc.vector.tensor_scalar(decay[:, :], decay[:, :], 0.0, None, ALU.max))
                link(nc.vector.tensor_tensor(decay[:, NC - 1:NC], decay[:, NC - 1:NC], C.edge_ok[:, :], ALU.mult))
                link(nc.vector.reduce_max(dmax[:, 0:1], decay[:, :], mybir.AxisListType.X))
                dve.wait_ge(peeked, 1)
                link(nc.vector.reduce_max(dmax[0:1, 1:2], C.bank[7][0:1, 0:P], mybir.AxisListType.X))
                link(nc.vector.tensor_scalar(dmax[0:1, 1:2], dmax[0:1, 1:2], 1e-8, None, ALU.add))
                link(nc.vector.tensor_scalar(top[:, :], C.ones[0:1, :], dmax[0:1, 1:2], None, ALU.mult))
                dve.wait_ge(peeked, 2)
                link(nc.vector.reciprocal(dmax[:, 2:3], C.bank[7][:, 128:129]))
                link(nc.vector.tensor_scalar(decay[:, :], decay[:, :], dmax[:, 2:3], -0.1, ALU.mult, ALU.mult))
                dve.wait_ge(expd, 1)

                def keep(s, par):
                    if not first(s, 2):
                        dve.wait_ge(made, s * 2 + (-2))
                    nc.vector.tensor_copy(kcol[:, par, :], keycol[:, :, bass.ds(s, 1)]).then_inc(kept, 1)

                def compare(s, par):
                    for k, same in enumerate((C.same_d[:, bass.ds(s * P, P)], same_s[:, par, :])):
                        dve.wait_ge(shown, s * 2 + (k + 1))
                        nc.vector.tensor_scalar(same, C.bank[2 * k + par][:, 0:P],
                                                kcol[:, par, k:k + 1], None, ALU.is_equal, ALU.add,
                                                accum_out=shared[:, k, bass.ds(s, 1)]).then_inc(made, 1)

                run_steps(dve, NC, [(2, compare), (0, keep)])
                n = [0]

                def link2(ins):
                    ins.then_inc(fixed, 1)
                    n[0] += 1
                    dve.wait_ge(fixed, n[0])

                dve.wait_ge(ends, 1)
                for k in range(2):
                    link2(nc.vector.tensor_copy(last_key[0:NC, k:k + 1], C.bank[6][0:NC, 2 * k:2 * k + 1]))
                    link2(nc.vector.scalar_tensor_tensor(out=C.carry[k][0:NC, :], in0=C.bank[5][0:NC, k * NC:(k + 1) * NC],
                                                         scalar=last_key[0:NC, k:k + 1], in1=C.upper[0:NC, 0:NC],
                                                         op0=ALU.is_equal, op1=ALU.mult))
                    link2(nc.vector.tensor_scalar(fix[0:NC, k, 0:1], C.part[0:NC, :], float(P), -1.0, ALU.mult, ALU.add))
                    link2(nc.vector.tensor_tensor(C.fix_row[k][0:NC, :], fix[0:NC, k, 0:1], C.bank[6][0:NC, 2 * k + 1:2 * k + 2], ALU.add))

            @block.scalar
            def _(act):
                act.wait_ge(timed, 9)
                nc.scalar.activation(C.decay[:, :], decay[:, :], ACT.Exp).then_inc(expd, 1)

            @block.tensor
            def _(pe):
                pe.wait_ge(timed, 4)
                nc.tensor.transpose(C.bank[7][0:1, 0:P], dmax[:, 0:1], C.ident[:, :]).then_inc(peeked, 1)
                pe.wait_ge(timed, 7)
                nc.tensor.matmul(C.bank[7][:, 128:129], top[:, :], C.ones[0:1, 0:1], start=True, stop=True).then_inc(peeked, 1)

                def show(s, par):
                    pe.wait_ge(kept, s + 1)
                    for k in range(2):
                        nc.tensor.transpose(C.bank[2 * k + par][:, 0:P], kcol[:, par, k:k + 1].broadcast_to([P, P]),
                                            C.ident[:, :]).then_inc(shown, 1)
                run_steps(pe, NC, [(0, show)])
                pe.wait_ge(made, 2 * NC)
                for k in range(2):
                    nc.tensor.matmul(C.bank[5][:, k * NC:(k + 1) * NC], row0[:, :], keycol[:, k, :], start=True, stop=True)
                    nc.tensor.matmul(C.bank[6][0:NC, 2 * k:2 * k + 1], keycol[:, k, :], C.ident[:, P - 1:P], start=True, stop=True)
                    ins = nc.tensor.matmul(C.bank[6][0:NC, 2 * k + 1:2 * k + 2], shared[:, k, :], C.ident[:, 0:1], start=True, stop=True)
                ins.then_inc(ends, 1)


def carry_over(nc, C, tag, k, table, bias):
    with ExitStack() as ctx:
        m = Mem(nc, ctx)
        tail = m.sb(f"{tag}_tail", [P, D])
        more = m.sb(f"{tag}_more", [P, D])
        read, plain, summed, copied, zero = (m.sem(f"{tag}_{x}") for x in ("tail_read", "tail_plain", "carry_summed", "carry_copied", "zrow_put"))
        added = C.mem.sem(f"{tag}_carry_added")
        with nc.Block() as block:
            @block.sync
            def _(sp):
                sp.dma_start(tail[0:NC, :], table[0:EP, :].rearrange("(c p) d -> p c d", p=P)[P - 1]).then_inc(read, 16)
                sp.dma_start(table[ZROW:ZROW + 1, :], bias[0:1, :]).then_inc(zero, 16)
                sp.wait_ge(zero, 16)

            @block.vector
            def _(dve):
                dve.wait_ge(read, 16)
                nc.vector.tensor_tensor(tail[0:NC, :], tail[0:NC, :], bias[0:NC, :], ALU.subtract).then_inc(plain, 1)
                dve.wait_ge(summed, 1)
                nc.vector.tensor_copy(more[0:NC, :], C.bank[0][0:NC, 0:D]).then_inc(copied, 1)

            @block.tensor
            def _(pe):
                pe.wait_ge(plain, 1)
                nc.tensor.matmul(C.bank[0][0:NC, 0:D], C.carry[k][0:NC, :], tail[0:NC, :], start=True, stop=True).then_inc(summed, 1)

            @block.gpsimd
            def _(pool):
                pool.wait_ge(copied, 1)
                nc.gpsimd.indirect_dma_start(out=table, out_offset=bass.IndirectOffsetOnAxis(ap=C.fix_row[k][0:NC, :], axis=0),
                                             in_=more[0:NC, :], in_offset=None, compute_op=ALU.add).then_inc(added, 16)
                pool.wait_ge(added, 16)


def load_all(nc, C, tag, pairs):
    with ExitStack() as ctx:
        s = Mem(nc, ctx).sem(f"{tag}_loaded")
        with nc.Block() as block:
            @block.sync
            def _(sp):
                for dst, src in pairs:
                    sp.dma_start(dst, src).then_inc(s, 16)
                sp.wait_ge(s, 16 * len(pairs))


def l0_layer(nc, C, A, i, table, prev, Y, R, bias):
    with ExitStack() as ctx:
        m = Mem(nc, ctx)
        tag = f"l0_{i}"
        lnb, lns = (m.sb(f"{tag}_{x}", [P, D]) for x in ("lnb", "lns"))
        W = m.sb(f"{tag}_W", [P, 2, D])
        load_all(nc, C, tag, [(bias[:, :], A["l0_cb"][i:i + 1, :].broadcast_to([P, D])),
                              (lnb[:, :], A["l0_lb"][i:i + 1, :].broadcast_to([P, D])),
                              (lns[:, :], A["l0_ls"][i:i + 1, :].broadcast_to([P, D])), (W[:, :, :], A["l0_w"][i].rearrange("(h p) d -> p h d", p=P))])
        idx = m.sb(f"{tag}_idx", [P, 2, KC], U32)
        G = m.sb(f"{tag}_G", [P, 2, KC, D])
        Z = m.sb(f"{tag}_Z", [P, 2, KC, D])
        seg = m.sb(f"{tag}_seg", [P, 2, KC, P])
        aggT = m.sb(f"{tag}_aggT", [P, 2, KC * 2, P])
        res = m.sb(f"{tag}_res", [P, 2, KC, D])
        norm = Norm(m, C, f"{tag}_n", KC)
        first_norm = Norm(m, C, f"{tag}_f", KC) if i == 0 else None
        scaled, idxed, updated, normed, biased, segged, mixed, copied, summed, evac = (
            m.sem(f"{tag}_{x}") for x in ("scaled", "idxed", "updated", "normed", "biased", "segged", "mixed", "copied", "summed", "evac"))
        got = [C.mem.sem(f"{tag}_got{j}") for j in range(2)]
        stored = [m.sem(f"{tag}_stored{j}") for j in range(2)]
        U = 1 if i else 3
        if i:
            T = m.sb(f"{tag}_T", [P, 2, KC, D])
            gained = m.sem(f"{tag}_gained")
            tread = [m.sem(f"{tag}_tread{j}") for j in range(2)]

        with nc.Block() as block:
            @block.gpsimd
            def _(pool):
                def gather(s, par):
                    if not first(s, 2):
                        pool.wait_ge(updated, s + (-1))
                    nc.gpsimd.tensor_copy(idx[:, par, :], C.rec[:, bass.ds(s * KC, KC), R_MAPS if i else R_SRC].bitcast(U32)
                                          ).then_inc(idxed, 1)
                    wait_apart(pool, C, (idxed, s + 1))
                    for j in range(KC):
                        nc.gpsimd.indirect_dma_start(out=G[:, par, j, :], out_offset=None, in_=prev if i else A["x"],
                                                     in_offset=bass.IndirectOffsetOnAxis(ap=idx[:, par, j:j + 1], axis=0)
                                                     ).then_inc(got[par], 16)

                def add_bias(s, par):
                    pool.wait_ge(scaled, s + 1)
                    nc.gpsimd.tensor_tensor(Z[:, par, :, :], Z[:, par, :, :], spread(lnb, KC), ALU.add).then_inc(biased, 1)
                run_steps(pool, EDGE_STEPS, [(0, gather), (U + 2, add_bias)] if i else [(U + 2, add_bias), (0, gather)])

            @block.sync
            def _(sp):
                def store(s, par):
                    wait_apart(sp, C, (evac, s + 1))
                    sp.dma_start(rows(table, s, KC), res[:, par, :, :]).then_inc(stored[par], 16)

                def read_sums(s, par):
                    if not first(s, 2):
                        wait_apart(sp, C, (gained, s + (-1)))
                    sp.dma_start(T[:, par, :, :], rows(prev, s, KC)).then_inc(tread[par], 16)
                run_steps(sp, EDGE_STEPS, [(0, read_sums), (U + 4, store)] if i else [(0, store)])
                all_landed(sp, stored, EDGE_STEPS)

            @block.vector
            def _(dve):
                def gain(s, par):
                    dve.wait_ge(tread[par], landed(s, par))
                    total = R[:, bass.ds(s * KC, KC), :]
                    if i == 1:
                        ins = nc.vector.tensor_scalar(total, T[:, par, :, :], 0.0, None, ALU.max)
                    else:
                        ins = nc.vector.scalar_tensor_tensor(out=total, in0=T[:, par, :, :], scalar=0.0, in1=total,
                                                             op0=ALU.max, op1=ALU.add)
                    ins.then_inc(gained, 1)

                def y(s):
                    return Y[:, bass.ds(s * KC, KC), :]

                def update(s, par):
                    dve.wait_ge(got[par], landed(s, par, KC))
                    nc.vector.scalar_tensor_tensor(out=y(s), in0=G[:, par, :, :], scalar=0.0, in1=y(s),
                                                   op0=ALU.max, op1=ALU.add).then_inc(updated, 1)

                def first_stats(s, par):
                    dve.wait_ge(got[par], landed(s, par, KC))
                    first_norm.stats(nc, dve, s, par, G[:, par, :, :])

                def stats(s, par):
                    dve.wait_ge(updated, s + 1)
                    norm.stats(nc, dve, s, par, y(s))

                def scale(s, par):
                    dve.wait_ge(normed, s + 1)
                    nc.vector.tensor_tensor(Z[:, par, :, :], Z[:, par, :, :], spread(lns, KC), ALU.mult).then_inc(scaled, 1)

                def evacuate(s, par):
                    dve.wait_ge(summed, s + 1)
                    if not first(s, 2):
                        dve.wait_ge(stored[par], landed(s - 2, par))
                    nc.vector.tensor_tensor(res[:, par, :, :], C.bank[2 + par][:, :].rearrange("p (j d) -> p j d", j=KC),
                                            spread(bias, KC), ALU.add).then_inc(evac, 1)
                fin = lambda s, par: norm.finish(nc, dve, s, par)
                first_fin = [] if i else [(2, lambda s, par: first_norm.finish(nc, dve, s, par))]
                head = [(1, update)] if i else [(1, first_stats)]
                run_steps(dve, EDGE_STEPS, first_fin + [(U + 4, evacuate), (U + 2, scale), (U + 1, fin)] + ([(U, stats)] + head if i == 0 else head + [(U, stats), (2, gain)]))

            @block.scalar
            def _(act):
                def first_rows(s, par):
                    act.wait_ge(first_norm.ready, s + 1)
                    first_norm.apply(nc, s, par, Y[:, bass.ds(s * KC, KC), :], G[:, par, :, :], ACT.Relu).then_inc(updated, 1)

                def normalise(s, par):
                    if not first(s, 2):
                        act.wait_ge(mixed, s + (-1))
                    for j in range(KC):
                        c = s * KC + j
                        ins = nc.scalar.activation(seg[:, par, j, :], C.same_d[:, bass.ds(c * P, P)], ACT.Copy,
                                                   scale=C.weight[:, bass.ds(c, 1)])
                    ins.then_inc(segged, 1)
                    act.wait_ge(norm.ready, s + 1)
                    norm.apply(nc, s, par, Z[:, par, :, :], Y[:, bass.ds(s * KC, KC), :], ACT.Identity).then_inc(normed, 1)

                def copy(s, par):
                    act.wait_ge(mixed, s + 1)
                    if not first(s, 2):
                        act.wait_ge(summed, s + (-1))
                    nc.scalar.activation(aggT[:, par, :, :], C.bank[par][:, :].rearrange("p (q e) -> p q e", q=2 * KC),
                                         ACT.Copy).then_inc(copied, 1)
                root = lambda s, par: norm.root(nc, act, s, par)
                froot = lambda s, par: first_norm.root(nc, act, s, par)
                run_steps(act, EDGE_STEPS, ([(2, first_rows)] if i == 0 else []) + [(U + 3, copy), (U + 1, normalise), (U, root)] +
                          ([(1, froot)] if i == 0 else []))

            @block.tensor
            def _(pe):
                def mix(s, par):
                    pe.wait_ge(biased, s + 1)
                    pe.wait_ge(segged, s + 1)
                    if not first(s, 2):
                        pe.wait_ge(copied, s + (-1))
                    for j in range(KC):
                        for h in range(2):
                            q = 2 * j + h
                            ins = nc.tensor.matmul(C.bank[par][:, q * P:(q + 1) * P], Z[:, par, j, h * P:(h + 1) * P],
                                                   seg[:, par, j, :], start=True, stop=True)
                    ins.then_inc(mixed, 1)

                def convolve(s, par):
                    pe.wait_ge(copied, s + 1)
                    if not first(s, 2):
                        pe.wait_ge(evac, s + (-1))
                    for j in range(KC):
                        for h in range(2):
                            ins = nc.tensor.matmul(C.bank[2 + par][:, j * D:(j + 1) * D], aggT[:, par, 2 * j + h, :],
                                                   W[:, h, :], start=h == 0, stop=h == 1)
                    ins.then_inc(summed, 1)
                run_steps(pe, EDGE_STEPS, [(U + 4, convolve), (U + 3, mix)])


def l0_total(nc, C, last, total, biases, earlier):
    n = EDGE_STEPS
    with ExitStack() as ctx:
        m = Mem(nc, ctx)
        T, R = m.sb("tot_T", [P, 4, KC, D]), m.sb("tot_R", [P, 4, KC, D])
        zr = m.sb("tot_z", [1, D])
        b = m.sb("tot_b", [1, 4, D])
        added, zsteps, bl, zput = m.sem("tot_added"), m.sem("tot_zsteps"), m.sem("tot_bl"), m.sem("tot_zput")
        read = [m.sem(f"tot_read{j}") for j in range(4)]
        stored = [m.sem(f"tot_stored{j}") for j in range(2)]
        with nc.Block() as block:
            @block.sync
            def _(sp):
                sp.dma_start(b[:, :, :], biases.rearrange("(o i) d -> o i d", o=1)).then_inc(bl, 16)

                def read_sums(s, r):
                    if not first(s, 4):
                        wait_apart(sp, C, (added, s + (-3)))
                    sp.dma_start(T[:, r, :, :], rows(last, s, KC)).then_inc(read[r], 16)

                def store(s, r):
                    wait_apart(sp, C, (added, s + 1))
                    sp.dma_start(rows(total, s, KC), R[:, r, :, :]).then_inc(stored[r % 2], 16)
                run_steps(sp, n, [(0, read_sums), (2, store)], 4)
                sp.wait_ge(zsteps, 5)
                sp.dma_start(total[ZROW:ZROW + 1, :], zr[:, :]).then_inc(zput, 16)
                sp.wait_ge(zput, 16)
                all_landed(sp, stored, n)

            @block.vector
            def _(dve):
                dve.wait_ge(bl, 16)
                nc.vector.memset(zr[:, :], 0.0).then_inc(zsteps, 1)
                for i in range(4):
                    dve.wait_ge(zsteps, i + 1)
                    nc.vector.scalar_tensor_tensor(out=zr[:, :], in0=b[:, i, :], scalar=0.0, in1=zr[:, :],
                                                   op0=ALU.max, op1=ALU.add).then_inc(zsteps, 1)

                def add(s, r):
                    dve.wait_ge(read[r], landed(s, r, ring=4))
                    if not first(s, 2):
                        dve.wait_ge(stored[r % 2], landed(s - 2, r % 2))
                    nc.vector.scalar_tensor_tensor(out=R[:, r, :, :], in0=T[:, r, :, :], scalar=0.0, in1=earlier[:, bass.ds(s * KC, KC), :],
                                                   op0=ALU.max, op1=ALU.add).then_inc(added, 1)
                run_steps(dve, n, [(0, add)], 4)


PART_PRODUCTS = [(h, x, y) for h in range(2) for x, y in ((0, 0), (0, 1), (1, 0))]


def split_in_two(nc, m, tag, triples):
    s = m.sem(f"{tag}_parted")
    with nc.Block() as block:
        @block.vector
        def _(dve):
            for i, (src, high, low) in enumerate(triples):
                nc.vector.tensor_copy(high, src).then_inc(s, 1)
                dve.wait_ge(s, 2 * i + 1)
                nc.vector.tensor_tensor(low, src, high, ALU.subtract).then_inc(s, 1)


class NodeStores:

    def __init__(self, C, name, m):
        self.C = C
        self.done = [m.sem(f"{name}{j}") for j in range(2)]

    def put(self, sp, s, r, ready, table, tile):
        wait_apart(sp, self.C, (ready, s + 1))
        sp.dma_start(rows(table, s, KT), tile).then_inc(self.done[r % 2], 16)

    def free(self, eng, s, r):
        if not first(s, 2):
            eng.wait_ge(self.done[r % 2], landed(s - 2, r % 2))

    def finish(self, sp):
        all_landed(sp, self.done, NODE_STEPS)


def gather_sums(nc, pool, s, r, slots, table, G, got):
    r = r % len(got)
    """Each node's sum: the row of its last edge's slot (ZROW where it has none)."""
    for j in range(KT):
        nc.gpsimd.indirect_dma_start(out=G[:, r, j, :], out_offset=None, in_=table,
                                     in_offset=bass.IndirectOffsetOnAxis(ap=slots[:, r, j:j + 1], axis=0)
                                     ).then_inc(got[r], 16)


def copy_slots(nc, C, pool, s, r, slots, slot_of, copied, per=1, ring=2):
    nc.gpsimd.tensor_copy(slots[:, r % ring, :], slot_of[:, bass.ds(s * KT, KT)]).then_inc(copied, 1)
    wait_apart(pool, C, (copied, s * per + per))


def transpose_tiles(nc, C, banks, tile):
    for h in range(2):
        for k in range(KT):
            ins = nc.tensor.transpose(C.bank[banks + h][:, k * P:(k + 1) * P], tile[:, k, h * P:(h + 1) * P], C.ident[:, :])
    return ins


def project_tiles(nc, C, banks, xT, W):
    for k in range(KT):
        for h in range(2):
            ins = nc.tensor.matmul(C.bank[banks + k // 2][:, (k % 2) * D:(k % 2 + 1) * D], xT[:, h, k * P:(k + 1) * P],
                                   W[:, h, :], start=h == 0, stop=h == 1)
    return ins


def nodes_l0(nc, C, A, total, x1, h1):
    n = NODE_STEPS
    with ExitStack() as ctx:
        m = Mem(nc, ctx)
        W, b = m.sb("na_W", [P, 2, D]), m.sb("na_b", [P, D])
        load_all(nc, C, "na", [(W[:, :, :], A["l0_pw"].rearrange("(h p) d -> p h d", p=P)), (b[:, :], A["l0_pb"].broadcast_to([P, D]))])
        X = m.sb("na_X", [P, 4, KT, D])
        G = m.sb("na_G", [P, 4, KT, D])
        Y = m.sb("na_Y", [P, 2, KT, D])
        yT = m.sb("na_yT", [P, 2, 2, KT * P])
        XB = m.sb("na_XB", [P, 2, KT, D])
        X1 = m.sb("na_X1", [P, 2, KT, D])
        H1 = m.sb("na_H1", [P, 2, KT, D])
        SQ = m.sb("na_SQ", [P, 2, KT, D])
        slots = m.sb("na_slots", [P, 4, KT], U32)
        n1, n2 = Norm(m, C, "na_n1", KT), Norm(m, C, "na_n2", KT)
        normed, biased, added, turned, copied, projected, summed, squared, tallied, slotted, outnorm = (
            m.sem(f"na_{x}") for x in ("normed", "biased", "added", "turned", "copied", "projected", "summed", "squared", "tallied", "slotted", "outnorm"))
        xread = [m.sem(f"na_xread{j}") for j in range(4)]
        got = [C.mem.sem(f"na_got{j}") for j in range(4)]
        keep_x, keep_h = NodeStores(C, "na_keepx", m), NodeStores(C, "na_keeph", m)
        with nc.Block() as block:
            @block.sync
            def _(sp):
                def load(s, r):
                    if not first(s, 4):
                        wait_apart(sp, C, (biased, s + (-3)))
                    sp.dma_start(X[:, r, :, :], rows(A["x"], s, KT)).then_inc(xread[r], 16)
                run_steps(sp, n, [(0, load), (4, lambda s, r: keep_x.put(sp, s, r, summed, x1, X1[:, r % 2, :, :])),
                                  (5, lambda s, r: keep_h.put(sp, s, r, outnorm, h1, H1[:, r % 2, :, :]))], 4)
                keep_x.finish(sp)
                keep_h.finish(sp)

            @block.gpsimd
            def _(pool):
                def gather(s, r):
                    if not first(s, 4):
                        pool.wait_ge(added, s + (-3))
                    copy_slots(nc, C, pool, s, r, slots, C.slot_of[0], slotted, ring=4)
                    gather_sums(nc, pool, s, r, slots, total, G, got)

                def add_bias(s, r):
                    pool.wait_ge(normed, s + 1)
                    if not first(s, 2):
                        pool.wait_ge(summed, s + (-1))
                    nc.gpsimd.tensor_tensor(XB[:, r % 2, :, :], X[:, r, :, :], spread(b, KT), ALU.add).then_inc(biased, 1)
                run_steps(pool, n, [(2, add_bias), (0, gather)], 4)

            @block.vector
            def _(dve):
                def stats1(s, r):
                    dve.wait_ge(xread[r], landed(s, r, ring=4))
                    n1.stats(nc, dve, s, r % 2, X[:, r, :, :])

                def add_total(s, r):
                    dve.wait_ge(normed, s + 1)
                    dve.wait_ge(got[r], landed(s, r, KT, ring=4))
                    y = Y[:, r % 2, :, :]
                    nc.vector.tensor_tensor(y, y, G[:, r, :, :], ALU.add).then_inc(added, 1)

                def add_x(s, r):
                    par = r % 2
                    dve.wait_ge(projected, s + 1)
                    dve.wait_ge(biased, s + 1)
                    keep_x.free(dve, s, r)
                    if not first(s, 2):
                        dve.wait_ge(outnorm, s + (-1))
                    nc.vector.tensor_tensor(X1[:, par, :, :], C.banks(2 + 2 * par, 2, KT), XB[:, par, :, :], ALU.add).then_inc(summed, 1)
                    dve.wait_ge(summed, s + 1)
                    n2.stats(nc, dve, s, par, X1[:, par, :, :])
                run_steps(dve, n, [(4, lambda s, r: n2.finish(nc, dve, s, r % 2)), (1, lambda s, r: n1.finish(nc, dve, s, r % 2)),
                                   (2, add_total), (0, stats1), (3, add_x)], 4)

            @block.scalar
            def _(act):
                def apply1(s, r):
                    if not first(s, 2):
                        act.wait_ge(turned, s + (-1))
                    act.wait_ge(n1.ready, s + 1)
                    n1.apply(nc, s, r % 2, Y[:, r % 2, :, :], X[:, r, :, :], ACT.Relu).then_inc(normed, 1)

                def apply2(s, r):
                    par = r % 2
                    keep_h.free(act, s, r)
                    if not first(s, 2):
                        act.wait_ge(tallied, s + (-1))
                    act.wait_ge(n2.ready, s + 1)
                    n2.apply(nc, s, par, H1[:, par, :, :], X1[:, par, :, :], ACT.Relu).then_inc(outnorm, 1)
                    act.wait_ge(outnorm, s + 1)
                    for k in range(KT):
                        pad = last_step(s, n) and k == KT - 1
                        ins = nc.scalar.activation(SQ[:, par, k, :], H1[:, par, k, :], ACT.Square,
                                                   scale=C.node_ok[:, 0:1] if pad else 1.0)
                    ins.then_inc(squared, 1)

                def copy(s, r):
                    if not first(s, 2):
                        act.wait_ge(projected, s + (-1))
                    act.wait_ge(turned, s + 1)
                    nc.scalar.activation(yT[:, r % 2, :, :], C.banks(0, 2, 2), ACT.Copy).then_inc(copied, 1)
                run_steps(act, n, [(4, apply2), (1, apply1), (2, copy), (3, lambda s, r: n2.root(nc, act, s, r % 2)),
                                   (0, lambda s, r: n1.root(nc, act, s, r % 2))], 4)

            @block.tensor
            def _(pe):
                def turn(s, r):
                    pe.wait_ge(added, s + 1)
                    if not first(s, 1):
                        pe.wait_ge(copied, s)
                    transpose_tiles(nc, C, 0, Y[:, r % 2, :, :]).then_inc(turned, 1)

                def project(s, r):
                    pe.wait_ge(copied, s + 1)
                    if not first(s, 2):
                        pe.wait_ge(summed, s + (-1))
                    project_tiles(nc, C, 2 + 2 * (r % 2), yT[:, r % 2, :, :], W).then_inc(projected, 1)

                def tally(s, r):
                    pe.wait_ge(squared, s + 1)
                    for k in range(KT):
                        for h in range(2):
                            ins = nc.tensor.matmul(C.bank[6 + h][:, 0:1], SQ[:, r % 2, k, h * P:(h + 1) * P], C.ones[:, 0:1],
                                                   start=first(s, 1) and k == 0, stop=last_step(s, n) and k == KT - 1)
                    ins.then_inc(tallied, 1)
                run_steps(pe, n, [(3, project), (2, turn), (5, tally)], 4)


def l1_weights(nc, C, A, Wt):
    with ExitStack() as ctx:
        m = Mem(nc, ctx)
        cs, nn, al = m.sb("lw_cs", [P, 2]), m.sb("lw_nn", [P, 2]), m.sb("lw_al", [P, 4])
        keep = m.sb("lw_keep", [P, 2, D])
        load_all(nc, C, "lw", [(Wt[:, :, :], A["l1_wt"].rearrange("(h p) d -> p h d", p=P))])
        v, a, t = m.sem("lw_v"), m.sem("lw_a"), m.sem("lw_t")
        with nc.Block() as block:
            @block.vector
            def _(dve):
                n = [0]

                def link(ins):
                    ins.then_inc(v, 1)
                    n[0] += 1
                    dve.wait_ge(v, n[0])

                link(nc.vector.tensor_copy(cs[:, 0:1], C.bank[6][:, 0:1]))
                link(nc.vector.tensor_copy(cs[:, 1:2], C.bank[7][:, 0:1]))
                dve.wait_ge(t, 2)
                link(nc.vector.tensor_copy(al[:, 0:1], C.bank[0][:, 0:1]))
                dve.wait_ge(a, 2)
                link(nc.vector.tensor_scalar(al[:, 1:2], al[:, 1:2], 1.0 / D, None, ALU.mult))
                link(nc.vector.tensor_scalar(al[:, 2:3], al[:, 1:2], 1e-8, None, ALU.is_gt))
                link(nc.vector.scalar_tensor_tensor(out=al[:, 3:4], in0=al[:, 1:2], scalar=0.1, in1=al[:, 2:3],
                                                    op0=ALU.mult, op1=ALU.mult))
                for h in range(2):
                    link(nc.vector.scalar_tensor_tensor(out=keep[:, h, :], in0=Wt[:, h, :], scalar=-1.0, in1=Wt[:, h, :],
                                                        op0=ALU.mult, op1=ALU.max))
                    link(nc.vector.tensor_scalar(keep[:, h, :], keep[:, h, :], nn[:, h:h + 1], al[:, 3:4], ALU.mult, ALU.is_ge))
                    link(nc.vector.tensor_tensor(Wt[:, h, :], Wt[:, h, :], keep[:, h, :], ALU.mult))

            @block.scalar
            def _(act):
                act.wait_ge(v, 2)
                nc.scalar.activation(nn[:, :], cs[:, :], ACT.Sqrt).then_inc(a, 1)
                act.wait_ge(v, 3)
                nc.scalar.activation(al[:, 1:2], al[:, 0:1], ACT.Sqrt).then_inc(a, 1)

            @block.tensor
            def _(pe):
                pe.wait_ge(v, 2)
                for h in range(2):
                    nc.tensor.matmul(C.bank[0][:, 0:1], C.ones[:, :], cs[:, h:h + 1], start=h == 0, stop=h == 1).then_inc(t, 1)


def l1_edges(nc, C, A, h1, table, bias, Wt):
    n = EDGE_STEPS
    with ExitStack() as ctx:
        m = Mem(nc, ctx)
        H = m.sb("l1_H", [P, NC, D])
        G = m.sb("l1_G", [P, 2, KC, D])
        gT = m.sb("l1_gT", [P, 2, KC * 2, P])
        idx = m.sb("l1_idx", [P, 2, KC], U32)
        junk = m.sb("l1_junk", [P, 2, D])
        ss = m.sb("l1_ss", [P, NC])
        idxed, turned, copied, projected, kept, squared = (m.sem(f"l1_{x}") for x in
                                                           ("idxed", "turned", "copied", "projected", "kept", "squared"))
        got = [C.mem.sem(f"l1_got{j}") for j in range(2)]
        with nc.Block() as block:
            @block.gpsimd
            def _(pool):
                def gather(s, par):
                    if not first(s, 2):
                        pool.wait_ge(turned, s + (-1))
                    nc.gpsimd.tensor_copy(idx[:, par, :], C.rec[:, bass.ds(s * KC, KC), R_SRC].bitcast(U32)).then_inc(idxed, 1)
                    wait_apart(pool, C, (idxed, s + 1))
                    for j in range(KC):
                        nc.gpsimd.indirect_dma_start(out=G[:, par, j, :], out_offset=None, in_=h1,
                                                     in_offset=bass.IndirectOffsetOnAxis(ap=idx[:, par, j:j + 1], axis=0)
                                                     ).then_inc(got[par], 16)
                run_steps(pool, n, [(0, gather)])

            @block.tensor
            def _(pe):
                def turn(s, par):
                    pe.wait_ge(got[par], landed(s, par, KC))
                    if not first(s, 2):
                        pe.wait_ge(copied, s + (-1))
                    for q in range(2 * KC):
                        ins = nc.tensor.transpose(C.bank[par][:, q * P:(q + 1) * P], G[:, par, q // 2, (q % 2) * P:(q % 2 + 1) * P], C.ident[:, :])
                    ins.then_inc(turned, 1)

                def project(s, par):
                    pe.wait_ge(copied, s + 1)
                    if not first(s, 2):
                        pe.wait_ge(kept, s + (-1))
                    for j in range(KC):
                        for h in range(2):
                            ins = nc.tensor.matmul(C.bank[2 + par][:, j * D:(j + 1) * D], gT[:, par, 2 * j + h, :], Wt[:, h, :],
                                                   start=h == 0, stop=h == 1)
                    ins.then_inc(projected, 1)
                run_steps(pe, n, [(1, project), (0, turn)])

            @block.vector
            def _(dve):
                def copy(s, par):
                    dve.wait_ge(turned, s + 1)
                    if not first(s, 2):
                        dve.wait_ge(projected, s + (-1))
                    nc.vector.tensor_copy(gT[:, par, :, :].rearrange("p q e -> p (q e)"), C.bank[par][:, :]).then_inc(copied, 1)
                run_steps(dve, n, [(0, copy)])

            @block.scalar
            def _(act):
                def keep(s, par):
                    act.wait_ge(projected, s + 1)
                    hv = H[:, bass.ds(s * KC, KC), :]
                    nc.scalar.activation(hv, C.bank[2 + par][:, :].rearrange("p (j d) -> p j d", j=KC), ACT.Copy).then_inc(kept, 1)
                    act.wait_ge(kept, s + 1)
                    if not first(s, 1):
                        act.wait_ge(squared, s)
                    for j in range(KC):
                        ins = nc.scalar.activation(junk[:, j, :], H[:, bass.ds(s * KC + j, 1), :].rearrange("p o d -> p (o d)"), ACT.Square,
                                                   accum_out=ss[:, bass.ds(s * KC + j, 1)])
                    ins.then_inc(squared, 1)
                run_steps(act, n, [(0, keep)])

        nm, some, w2, tot, thr = m.sb("l1_nm", [P, NC]), m.sb("l1_some", [P, NC]), m.sb("l1_w2", [P, NC]), m.sb("l1_tot", [P, 1]), m.sb("l1_thr", [P, 1])
        v, a, t = m.sem("l1_v"), m.sem("l1_a"), m.sem("l1_t")
        with nc.Block() as block:
            @block.vector
            def _(dve):
                k = [0]

                def link(ins):
                    ins.then_inc(v, 1)
                    k[0] += 1
                    dve.wait_ge(v, k[0])

                link(nc.vector.tensor_tensor(w2[:, :], C.weight[:, :], C.weight[:, :], ALU.mult))
                link(nc.vector.tensor_tensor(ss[:, :], ss[:, :], w2[:, :], ALU.mult))
                link(nc.vector.tensor_scalar(some[:, :], ss[:, :], 2.0 ** -110, None, ALU.is_gt))
                link(nc.vector.tensor_scalar(ss[:, :], ss[:, :], 2.0 ** -110, None, ALU.max))
                dve.wait_ge(a, 1)
                link(nc.vector.tensor_tensor(nm[:, :], nm[:, :], some[:, :], ALU.mult))
                link(nc.vector.tensor_copy(w2[:, :], nm[:, :]))
                link(nc.vector.tensor_tensor(w2[:, NC - 1:NC], nm[:, NC - 1:NC], C.edge_ok[:, :], ALU.mult))
                link(nc.vector.reduce_sum(tot[:, :], w2[:, :], mybir.AxisListType.X))
                dve.wait_ge(t, 1)
                link(nc.vector.tensor_scalar(thr[:, :], C.bank[4][:, 0:1], 1.0 / E, 0.1, ALU.mult, ALU.mult))
                link(nc.vector.tensor_scalar(nm[:, :], nm[:, :], thr[:, 0:1], None, ALU.is_ge))
                link(nc.vector.tensor_tensor(nm[:, :], nm[:, :], C.lock[:, :], ALU.max))
                link(nc.vector.tensor_tensor(nm[:, :], nm[:, :], C.weight[:, :], ALU.mult))

            @block.scalar
            def _(act):
                act.wait_ge(v, 4)
                nc.scalar.activation(nm[:, :], ss[:, :], ACT.Sqrt).then_inc(a, 1)

            @block.tensor
            def _(pe):
                pe.wait_ge(v, 8)
                nc.tensor.matmul(C.bank[4][:, 0:1], C.ones[:, :], tot[:, :], start=True, stop=True).then_inc(t, 1)

        sum_edges(nc, C, A, "l1s", table, bias, C.same_d, nm, resident=H)
        carry_over(nc, C, "l1", 0, table, bias)


def sum_edges(nc, C, A, tag, table, bias, same, weight, resident):
    n = EDGE_STEPS
    with ExitStack() as ctx:
        m = Mem(nc, ctx)
        seg = m.sb(f"{tag}_seg", [P, 2, KC, P])
        res = m.sb(f"{tag}_res", [P, 2, KC, D])
        segged, summed, evac = m.sem(f"{tag}_segged"), m.sem(f"{tag}_summed"), m.sem(f"{tag}_evac")
        stored = [m.sem(f"{tag}_stored{j}") for j in range(2)]
        comp = m.sb("comp", [P, 2, KC, 20])
        types = m.sb("types", [P, 2, KC], U32)
        typed, prod = m.sem("types_copied"), m.sem("coef_made")
        comp_got = [C.mem.sem(f"comp_got{j}") for j in range(2)]
        with nc.Block() as block:
            @block.gpsimd
            def _(pool):
                def fetch(s, par):
                    if not first(s, 2):
                        pool.wait_ge(prod, s + (-1))
                    nc.gpsimd.tensor_copy(types[:, par, :], C.rec[:, bass.ds(s * KC, KC), R_TYPE].bitcast(U32)).then_inc(typed, 1)
                    wait_apart(pool, C, (typed, s + 1))
                    for j in range(KC):
                        nc.gpsimd.indirect_dma_start(out=comp[:, par, j, :], out_offset=None, in_=A["comp"],
                                                     in_offset=bass.IndirectOffsetOnAxis(ap=types[:, par, j:j + 1], axis=0)
                                                     ).then_inc(comp_got[par], 16)
                run_steps(pool, n, [(0, fetch)])

            @block.scalar
            def _(act):
                def weigh(s, par):
                    if not first(s, 2):
                        act.wait_ge(summed, s + (-1))
                    for j in range(KC):
                        c = s * KC + j
                        ins = nc.scalar.activation(seg[:, par, j, :], same[:, bass.ds(c * P, P)], ACT.Copy, scale=weight[:, bass.ds(c, 1)])
                    ins.then_inc(segged, 1)
                run_steps(act, n, [(0, weigh)])

            @block.tensor
            def _(pe):
                def total(s, par):
                    pe.wait_ge(segged, s + 1)
                    if not first(s, 2):
                        pe.wait_ge(evac, s + (-1))
                    for j in range(KC):
                        ins = nc.tensor.matmul(C.bank[par][:, j * D:(j + 1) * D], seg[:, par, j, :],
                                               resident[:, bass.ds(s * KC + j, 1), :].rearrange("p o d -> p (o d)"), start=True, stop=True)
                    ins.then_inc(summed, 1)
                run_steps(pe, n, [(0, total)])

            @block.vector
            def _(dve):
                def evacuate(s, par):
                    dve.wait_ge(summed, s + 1)
                    if not first(s, 2):
                        dve.wait_ge(stored[par], landed(s - 2, par))
                    nc.vector.tensor_tensor(res[:, par, :, :], C.bank[par][:, :].rearrange("p (j d) -> p j d", j=KC),
                                            spread(bias, KC), ALU.add).then_inc(evac, 1)

                def coefs(s, par):
                    dve.wait_ge(comp_got[par], landed(s, par, KC))
                    for j in range(KC):
                        ins = nc.vector.tensor_scalar(C.coef[:, bass.ds(s * KC + j, 1), :].rearrange("p o k -> p (o k)"), comp[:, par, j, :],
                                                      C.decay[:, bass.ds(s * KC + j, 1)], None, ALU.mult)
                    ins.then_inc(prod, 1)
                run_steps(dve, n, [(1, coefs), (0, evacuate)])

            @block.sync
            def _(sp):
                def store(s, par):
                    wait_apart(sp, C, (evac, s + 1))
                    sp.dma_start(rows(table, s, KC), res[:, par, :, :]).then_inc(stored[par], 16)
                run_steps(sp, n, [(0, store)])
                all_landed(sp, stored, n)


def nodes_l1(nc, C, x1, table, x2, e0):
    n = NODE_STEPS
    with ExitStack() as ctx:
        m = Mem(nc, ctx)
        X, G, H = (m.sb(f"nb_{x}", [P, 2, KT, D]) for x in "XGH")
        X2 = m.sb("nb_X2", [P, 2, KT, D])
        slots = m.sb("nb_slots", [P, 2, KT], U32)
        norm = Norm(m, C, "nb_n", KT)
        summed, normed, slotted = m.sem("nb_summed"), m.sem("nb_normed"), m.sem("nb_slotted")
        xread = [m.sem(f"nb_xread{j}") for j in range(2)]
        got = [C.mem.sem(f"nb_got{j}") for j in range(2)]
        keep_x, keep_h = NodeStores(C, "nb_keepx", m), NodeStores(C, "nb_keeph", m)
        with nc.Block() as block:
            @block.sync
            def _(sp):
                def load(s, r):
                    if not first(s, 2):
                        wait_apart(sp, C, (summed, s + (-1)))
                    sp.dma_start(X[:, r, :, :], rows(x1, s, KT)).then_inc(xread[r], 16)
                run_steps(sp, n, [(0, load), (1, lambda s, r: keep_x.put(sp, s, r, summed, x2, X2[:, r, :, :])),
                                  (2, lambda s, r: keep_h.put(sp, s, r, normed, e0, H[:, r, :, :]))])
                keep_x.finish(sp)
                keep_h.finish(sp)

            @block.gpsimd
            def _(pool):
                def gather(s, r):
                    if not first(s, 2):
                        pool.wait_ge(summed, s + (-1))
                    copy_slots(nc, C, pool, s, r, slots, C.slot_of[0], slotted)
                    gather_sums(nc, pool, s, r, slots, table, G, got)
                run_steps(pool, n, [(0, gather)])

            @block.vector
            def _(dve):
                def add(s, r):
                    dve.wait_ge(xread[r], landed(s, r))
                    dve.wait_ge(got[r], landed(s, r, KT))
                    keep_x.free(dve, s, r)
                    if not first(s, 2):
                        dve.wait_ge(normed, s + (-1))
                    nc.vector.tensor_tensor(X2[:, r, :, :], X[:, r, :, :], G[:, r, :, :], ALU.add).then_inc(summed, 1)
                    dve.wait_ge(summed, s + 1)
                    norm.stats(nc, dve, s, r, X2[:, r, :, :])
                run_steps(dve, n, [(0, add), (1, lambda s, r: norm.finish(nc, dve, s, r))])

            @block.scalar
            def _(act):
                def apply(s, r):
                    keep_h.free(act, s, r)
                    act.wait_ge(norm.ready, s + 1)
                    norm.apply(nc, s, r, H[:, r, :, :], X2[:, r, :, :], ACT.Relu).then_inc(normed, 1)
                run_steps(act, n, [(0, lambda s, r: norm.root(nc, act, s, r)), (1, apply)])


def l2_edges(nc, C, A, layer, hin, table, bias, attr_d=None):
    n = EDGE_STEPS
    NB = 10
    tag = f"l2e{layer}"
    with ExitStack() as ctx:
        m = Mem(nc, ctx)
        B = [m.sb(f"{tag}_B{part}", [P, 2, NB, D], F32R) for part in ("high", "low")]
        with ExitStack() as load:
            raw = Mem(nc, load).sb(f"{tag}_raw", [P, 2, NB, D])
            load_all(nc, C, tag, [(raw[:, h, :, :], A[f"l2_basis{layer}"][:, h * P:(h + 1) * P, :].rearrange("b p d -> p b d")) for h in range(2)])
            split_in_two(nc, Mem(nc, load), f"{tag}_B", [(raw[:, h, :, :], B[0][:, h, :, :], B[1][:, h, :, :]) for h in range(2)])
        G = m.sb(f"{tag}_G", [P, 2, KC, D])
        gT = [m.sb(f"{tag}_gT{part}", [P, 2, KC * 2, P], F32R) for part in ("high", "low")]
        M = m.sb(f"{tag}_M", [P, 2, KC, D])
        Mp = [m.sb(f"{tag}_M{part}", [P, 2, KC, D], F32R) for part in ("high", "low")]
        seg = m.sb(f"{tag}_seg", [P, 2, KC, P], F32R)
        res = m.sb(f"{tag}_res", [P, 2, KC, D])
        idx = m.sb(f"{tag}_idx", [P, 2, KC], U32)
        idxed, turned, highs, lows, projected, weighed, mhigh, mlow, segged, summed, evac = (
            m.sem(f"{tag}_{x}") for x in ("idxed", "turned", "highs", "lows", "projected", "weighed", "mhigh", "mlow", "segged", "summed", "evac"))
        got = [C.mem.sem(f"{tag}_got{j}") for j in range(2)]
        stored = [m.sem(f"{tag}_stored{j}") for j in range(2)]
        if attr_d is not None:
            attr, attr_idx = m.sb("attr_rows", [P, 2, KC, D]), m.sb("attr_idx", [P, 2, KC], U32)
            attr_idxed = m.sem("attr_idxed")
            attr_got = [C.mem.sem(f"attr_got{j}") for j in range(2)]
            attr_put = [m.sem(f"attr_put{j}") for j in range(2)]
        PAIRS = NB // 2
        with nc.Block() as block:
            @block.gpsimd
            def _(pool):
                def gather(s, par):
                    if not first(s, 2):
                        pool.wait_ge(turned, s + (-1))
                    nc.gpsimd.tensor_copy(idx[:, par, :], C.rec[:, bass.ds(s * KC, KC), R_SRC].bitcast(U32)).then_inc(idxed, 1)
                    wait_apart(pool, C, (idxed, s + 1))
                    for j in range(KC):
                        nc.gpsimd.indirect_dma_start(out=G[:, par, j, :], out_offset=None, in_=hin,
                                                     in_offset=bass.IndirectOffsetOnAxis(ap=idx[:, par, j:j + 1], axis=0)
                                                     ).then_inc(got[par], 16)

                def gather_attr(s, par):
                    if not first(s, 2):
                        pool.wait_ge(attr_put[par], landed(s - 2, par))
                        settle(pool, C, s)
                    nc.gpsimd.tensor_copy(attr_idx[:, par, :], C.rec[:, bass.ds(s * KC, KC), R_EID].bitcast(U32)).then_inc(attr_idxed, 1)
                    wait_apart(pool, C, (attr_idxed, s + 1))
                    for j in range(KC):
                        nc.gpsimd.indirect_dma_start(out=attr[:, par, j, :], out_offset=None, in_=A["attr"],
                                                     in_offset=bass.IndirectOffsetOnAxis(ap=attr_idx[:, par, j:j + 1], axis=0)
                                                     ).then_inc(attr_got[par], 16)

                def low(s, par):
                    pool.wait_ge(mhigh, s + 1)
                    nc.gpsimd.tensor_tensor(Mp[1][:, par, :, :], M[:, par, :, :], Mp[0][:, par, :, :], ALU.subtract).then_inc(mlow, 1)
                run_steps(pool, n, [(0, gather)] + ([(0, gather_attr)] if attr_d is not None else []) + [(2, low)])

            @block.tensor
            def _(pe):
                def turn(s, par):
                    pe.wait_ge(got[par], landed(s, par, KC))
                    if not first(s, 1):
                        pe.wait_ge(lows, s)
                    for q in range(2 * KC):
                        ins = nc.tensor.transpose(C.bank[0][:, q * P:(q + 1) * P], G[:, par, q // 2, (q % 2) * P:(q % 2 + 1) * P], C.ident[:, :])
                    ins.then_inc(turned, 1)

                def project(s, par):
                    pe.wait_ge(lows, s + 1)
                    for p in range(PAIRS):
                        for j in range(KC):
                            i = p * KC + j
                            if not (first(s, 1) and p < 2):
                                pe.wait_ge(weighed, s * (KC * NB) + (2 * KC * (p - 2) + KC + j + 1))
                            for k, (h, x, y) in enumerate(PART_PRODUCTS):
                                ins = nc.tensor.matmul(C.bank[1 + (i + 2 * par) % 4][:, :], gT[x][:, par, 2 * j + h, :],
                                                       B[y][:, h, 2 * p:2 * p + 2, :].rearrange("p b d -> p (b d)"),
                                                       start=k == 0, stop=k == len(PART_PRODUCTS) - 1)
                            ins.then_inc(projected, 1)

                def total(s, par):
                    pe.wait_ge(segged, s + 1)
                    pe.wait_ge(mlow, s + 1)
                    if not first(s, 2):
                        pe.wait_ge(evac, s + (-1))
                    for j in range(KC):
                        for x in range(2):
                            ins = nc.tensor.matmul(C.bank[5 + par][:, j * D:(j + 1) * D], seg[:, par, j, :], Mp[x][:, par, j, :],
                                                   start=x == 0, stop=x == 1)
                    ins.then_inc(summed, 1)
                run_steps(pe, n, [(0, turn), (1, project), (3, total)])

            @block.scalar
            def _(act):
                def copy(s, par):
                    act.wait_ge(turned, s + 1)
                    if not first(s, 2):
                        act.wait_ge(projected, s * (KC * PAIRS) + (-KC * PAIRS))
                    nc.scalar.activation(gT[0][:, par, :, :].rearrange("p q e -> p (q e)"), C.bank[0][:, :], ACT.Copy).then_inc(highs, 1)

                def widen(s, par):
                    if not first(s, 2):
                        act.wait_ge(summed, s + (-1))
                    for j in range(KC):
                        ins = nc.scalar.activation(seg[:, par, j, :], C.same_d[:, bass.ds((s * KC + j) * P, P)], ACT.Copy)
                    ins.then_inc(segged, 1)

                def high(s, par):
                    act.wait_ge(weighed, s * (KC * NB) + KC * NB)
                    if not first(s, 2):
                        act.wait_ge(summed, s + (-1))
                    nc.scalar.activation(Mp[0][:, par, :, :], M[:, par, :, :], ACT.Copy).then_inc(mhigh, 1)
                run_steps(act, n, [(0, copy), (2, high), (2, widen)])

            @block.vector
            def _(dve):
                def rest(s, par):
                    dve.wait_ge(highs, s + 1)
                    nc.vector.tensor_tensor(gT[1][:, par, :, :].rearrange("p q e -> p (q e)"), C.bank[0][:, :],
                                            gT[0][:, par, :, :].rearrange("p q e -> p (q e)"), ALU.subtract).then_inc(lows, 1)

                def weigh(s, par):
                    if not first(s, 2):
                        dve.wait_ge(mlow, s + (-1))
                    for p in range(PAIRS):
                        for b in range(2):
                            for j in range(KC):
                                i, k = p * KC + j, 2 * p + b
                                if b == 0:
                                    dve.wait_ge(projected, s * (KC * PAIRS) + (i + 1))
                                bank = C.bank[1 + (i + 2 * par) % 4][:, b * D:(b + 1) * D]
                                c = C.coef[:, bass.ds(s * KC + j, 1), (layer - 1) * NB + k]
                                out = M[:, par, j, :]
                                if k == 0:
                                    ins = nc.vector.tensor_scalar(out, bank, c, None, ALU.mult)
                                else:
                                    dve.wait_ge(weighed, s * (KC * NB) + (KC * (k - 1) + j + 1))
                                    ins = nc.vector.scalar_tensor_tensor(out=out, in0=bank, scalar=c, in1=out, op0=ALU.mult, op1=ALU.add)
                                ins.then_inc(weighed, 1)

                def evacuate(s, par):
                    dve.wait_ge(summed, s + 1)
                    if not first(s, 2):
                        dve.wait_ge(stored[par], landed(s - 2, par))
                    nc.vector.tensor_tensor(res[:, par, :, :], C.bank[5 + par][:, :].rearrange("p (j d) -> p j d", j=KC),
                                            spread(bias, KC), ALU.add).then_inc(evac, 1)
                run_steps(dve, n, [(4, evacuate), (0, rest), (1, weigh)])

            @block.sync
            def _(sp):
                def store(s, par):
                    wait_apart(sp, C, (evac, s + 1))
                    sp.dma_start(rows(table, s, KC), res[:, par, :, :]).then_inc(stored[par], 16)

                def store_attr(s, par):
                    wait_apart(sp, C, (attr_got[par], landed(s, par, KC)))
                    sp.dma_start(rows(attr_d, s, KC), attr[:, par, :, :]).then_inc(attr_put[par], 16)
                run_steps(sp, n, ([(0, store_attr)] if attr_d is not None else []) + [(4, store)])
                all_landed(sp, stored, n)
                if attr_d is not None:
                    all_landed(sp, attr_put, n)
        carry_over(nc, C, f"l2c{layer}", 0, table, bias)


def nodes_l2a(nc, C, A, e0, table, h2):
    n = NODE_STEPS
    with ExitStack() as ctx:
        m = Mem(nc, ctx)
        W = m.sb("nc_W", [P, 2, D])
        load_all(nc, C, "nc", [(W[:, :, :], A["l2_lw1"].rearrange("(h p) d -> p h d", p=P))])
        X, G = (m.sb(f"nc_{x}", [P, 4, KT, D]) for x in "XG")
        H = m.sb("nc_H", [P, 2, KT, D])
        xT = m.sb("nc_xT", [P, 2, 2, KT * P])
        slots = m.sb("nc_slots", [P, 4, KT], U32)
        turned, copied, projected, summed, relued, slotted = (m.sem(f"nc_{x}") for x in ("turned", "copied", "projected", "summed", "relued", "slotted"))
        xread = [m.sem(f"nc_xread{j}") for j in range(4)]
        got = [C.mem.sem(f"nc_got{j}") for j in range(4)]
        keep = NodeStores(C, "nc_keep", m)
        with nc.Block() as block:
            @block.sync
            def _(sp):
                def load(s, r):
                    if not first(s, 4):
                        wait_apart(sp, C, (turned, s + (-3)))
                    sp.dma_start(X[:, r, :, :], rows(e0, s, KT)).then_inc(xread[r], 16)
                run_steps(sp, n, [(4, lambda s, r: keep.put(sp, s, r, relued, h2, H[:, r % 2, :, :])), (0, load)], 4)
                keep.finish(sp)

            @block.gpsimd
            def _(pool):
                def gather(s, r):
                    if not first(s, 4):
                        pool.wait_ge(relued, s + (-3))
                    copy_slots(nc, C, pool, s, r, slots, C.slot_of[0], slotted, ring=4)
                    gather_sums(nc, pool, s, r, slots, table, G, got)
                run_steps(pool, n, [(0, gather)], 4)

            @block.tensor
            def _(pe):
                def turn(s, r):
                    pe.wait_ge(xread[r], landed(s, r, ring=4))
                    if not first(s, 2):
                        pe.wait_ge(copied, s + (-1))
                    transpose_tiles(nc, C, 2 * (r % 2), X[:, r, :, :]).then_inc(turned, 1)

                def project(s, r):
                    pe.wait_ge(copied, s + 1)
                    if not first(s, 2):
                        pe.wait_ge(summed, s + (-1))
                    project_tiles(nc, C, 4 + 2 * (r % 2), xT[:, r % 2, :, :], W).then_inc(projected, 1)
                run_steps(pe, n, [(0, turn), (1, project)], 4)

            @block.scalar
            def _(act):
                def copy(s, r):
                    act.wait_ge(turned, s + 1)
                    if not first(s, 2):
                        act.wait_ge(projected, s + (-1))
                    nc.scalar.activation(xT[:, r % 2, :, :], C.banks(2 * (r % 2), 2, 2), ACT.Copy).then_inc(copied, 1)

                def relu(s, r):
                    act.wait_ge(summed, s + 1)
                    keep.free(act, s, r)
                    nc.scalar.activation(H[:, r % 2, :, :], G[:, r, :, :], ACT.Relu).then_inc(relued, 1)
                run_steps(act, n, [(0, copy), (2, relu)], 4)

            @block.vector
            def _(dve):
                def add(s, r):
                    dve.wait_ge(projected, s + 1)
                    dve.wait_ge(got[r], landed(s, r, KT, ring=4))
                    nc.vector.tensor_tensor(G[:, r, :, :], C.banks(4 + 2 * (r % 2), 2, KT), G[:, r, :, :], ALU.add).then_inc(summed, 1)
                run_steps(dve, n, [(1, add)], 4)


def nodes_l2b(nc, C, A, h2, e0, x2, table, x3, h3):
    n = NODE_STEPS
    with ExitStack() as ctx:
        m = Mem(nc, ctx)
        W, g, b = m.sb("nd_W", [P, 2, D]), m.sb("nd_g", [P, D]), m.sb("nd_b", [P, D])
        load_all(nc, C, "nd", [(W[:, :, :], A["l2_lw2"].rearrange("(h p) d -> p h d", p=P)),
                               (g[:, :], A["l2_g"].broadcast_to([P, D])), (b[:, :], A["l2_b"].broadcast_to([P, D]))])
        U, Z, X3, H3 = (m.sb(f"nd_{x}", [P, 2, KT, D]) for x in ("U", "Z", "X3", "H3"))
        H, G, X, E0 = (m.sb(f"nd_{x}", [P, 4, KT, D]) for x in ("H", "G", "X", "E0"))
        hT = m.sb("nd_hT", [P, 2, 2, KT * P])
        slots = m.sb("nd_slots", [P, 4, KT], U32)
        n1, n2 = Norm(m, C, "nd_n1", KT), Norm(m, C, "nd_n2", KT)
        turned, copied, projected, summed, biased, normed, scaled, added, normed2, slotted, mixed = (
            m.sem(f"nd_{x}") for x in ("turned", "copied", "projected", "summed", "biased", "normed", "scaled", "added", "normed2", "slotted", "mixed"))
        hread = [m.sem(f"nd_hread{j}") for j in range(4)]
        xread = [m.sem(f"nd_xread{j}") for j in range(4)]
        eread = [m.sem(f"nd_eread{j}") for j in range(4)]
        got = [C.mem.sem(f"nd_got{j}") for j in range(4)]
        keep_x, keep_h = NodeStores(C, "nd_keepx", m), NodeStores(C, "nd_keeph", m)
        with nc.Block() as block:
            @block.sync
            def _(sp):
                def load(s, r):
                    if not first(s, 4):
                        wait_apart(sp, C, (turned, s + (-3)))
                    sp.dma_start(H[:, r, :, :], rows(h2, s, KT)).then_inc(hread[r], 16)
                    if not first(s, 4):
                        wait_apart(sp, C, (mixed, s + (-3)))
                    sp.dma_start(E0[:, r, :, :], rows(e0, s, KT)).then_inc(eread[r], 16)
                    if not first(s, 4):
                        wait_apart(sp, C, (added, s + (-3)))
                    sp.dma_start(X[:, r, :, :], rows(x2, s, KT)).then_inc(xread[r], 16)
                run_steps(sp, n, [(0, load), (4, lambda s, r: keep_x.put(sp, s, r, added, x3, X3[:, r % 2, :, :])),
                                  (5, lambda s, r: keep_h.put(sp, s, r, normed2, h3, H3[:, r % 2, :, :]))], 4)
                keep_x.finish(sp)
                keep_h.finish(sp)

            @block.gpsimd
            def _(pool):
                def gather(s, r):
                    if not first(s, 4):
                        pool.wait_ge(summed, s + (-3))
                    copy_slots(nc, C, pool, s, r, slots, C.slot_of[0], slotted, ring=4)
                    gather_sums(nc, pool, s, r, slots, table, G, got)

                def add_bias(s, r):
                    pool.wait_ge(xread[r], landed(s, r, ring=4))
                    nc.gpsimd.tensor_tensor(X[:, r, :, :], X[:, r, :, :], spread(b, KT), ALU.add).then_inc(biased, 1)
                run_steps(pool, n, [(0, gather), (0, add_bias)], 4)

            @block.tensor
            def _(pe):
                def turn(s, r):
                    pe.wait_ge(hread[r], landed(s, r, ring=4))
                    if not first(s, 2):
                        pe.wait_ge(copied, s + (-1))
                    transpose_tiles(nc, C, 2 * (r % 2), H[:, r, :, :]).then_inc(turned, 1)

                def project(s, r):
                    pe.wait_ge(copied, s + 1)
                    if not first(s, 2):
                        pe.wait_ge(summed, s + (-1))
                    project_tiles(nc, C, 4 + 2 * (r % 2), hT[:, r % 2, :, :], W).then_inc(projected, 1)
                run_steps(pe, n, [(0, turn), (1, project)], 4)

            @block.scalar
            def _(act):
                def copy(s, r):
                    par = r % 2
                    act.wait_ge(turned, s + 1)
                    if not first(s, 2):
                        act.wait_ge(projected, s + (-1))
                    nc.scalar.activation(hT[:, par, :, :], C.banks(2 * par, 2, 2), ACT.Copy).then_inc(copied, 1)

                def apply1(s, r):
                    act.wait_ge(n1.ready, s + 1)
                    if not first(s, 2):
                        act.wait_ge(added, s + (-1))
                    n1.apply(nc, s, r % 2, Z[:, r % 2, :, :], U[:, r % 2, :, :], ACT.Identity).then_inc(normed, 1)

                def apply2(s, r):
                    keep_h.free(act, s, r)
                    act.wait_ge(n2.ready, s + 1)
                    n2.apply(nc, s, r % 2, H3[:, r % 2, :, :], X3[:, r % 2, :, :], ACT.Relu).then_inc(normed2, 1)
                run_steps(act, n, [(4, apply2), (2, apply1), (0, copy), (3, lambda s, r: n2.root(nc, act, s, r % 2)),
                                   (1, lambda s, r: n1.root(nc, act, s, r % 2))], 4)

            @block.vector
            def _(dve):
                def mix(s, r):
                    par = r % 2
                    dve.wait_ge(projected, s + 1)
                    dve.wait_ge(got[r], landed(s, r, KT, ring=4))
                    if not first(s, 2):
                        dve.wait_ge(normed, s + (-1))
                    nc.vector.tensor_tensor(U[:, par, :, :], C.banks(4 + 2 * par, 2, KT), G[:, r, :, :], ALU.add).then_inc(summed, 1)
                    dve.wait_ge(summed, s + 1)
                    dve.wait_ge(eread[r], landed(s, r, ring=4))
                    nc.vector.scalar_tensor_tensor(out=U[:, par, :, :], in0=U[:, par, :, :], scalar=0.0, in1=E0[:, r, :, :],
                                                   op0=ALU.max, op1=ALU.add).then_inc(mixed, 1)
                    dve.wait_ge(mixed, s + 1)
                    n1.stats(nc, dve, s, par, U[:, par, :, :])

                def add(s, r):
                    par = r % 2
                    dve.wait_ge(normed, s + 1)
                    nc.vector.tensor_tensor(Z[:, par, :, :], Z[:, par, :, :], spread(g, KT), ALU.mult).then_inc(scaled, 1)
                    dve.wait_ge(scaled, s + 1)
                    dve.wait_ge(biased, s + 1)
                    keep_x.free(dve, s, r)
                    if not first(s, 2):
                        dve.wait_ge(normed2, s + (-1))
                    nc.vector.tensor_tensor(X3[:, par, :, :], Z[:, par, :, :], X[:, r, :, :], ALU.add).then_inc(added, 1)
                    dve.wait_ge(added, s + 1)
                    n2.stats(nc, dve, s, par, X3[:, par, :, :])
                run_steps(dve, n, [(4, lambda s, r: n2.finish(nc, dve, s, r % 2)), (2, lambda s, r: n1.finish(nc, dve, s, r % 2)),
                                   (3, add), (1, mix)], 4)


def l3_edges(nc, C, attr_d, h3, by_src, table_d, table_s, zero):
    n = EDGE_STEPS
    with ExitStack() as ctx:
        m = Mem(nc, ctx)
        G = m.sb("l3_G", [P, 2, 3, KC, D])
        M = m.sb("l3_M", [P, 2, KC, D])
        res = m.sb("l3_res", [P, 2, KC, D])
        seg = m.sb("l3_seg", [P, 2, KC, P])
        idx = m.sb("l3_idx", [P, 2, 3, KC], U32)
        FIELDS = (R_SRC, R_DST, R_RANKS)
        idxed, summed0, added, relued, segged, summed, evac = (m.sem(f"l3_{x}") for x in
                                                               ("idxed", "summed0", "added", "relued", "segged", "summed", "evac"))
        got = [C.mem.sem(f"l3_got{j}") for j in range(2)]
        put = [C.mem.sem(f"l3_put{j}") for j in range(2)]
        attr_read = [m.sem(f"l3_attr_read{j}") for j in range(2)]
        stored = [m.sem(f"l3_stored{j}") for j in range(2)]
        with nc.Block() as block:
            @block.gpsimd
            def _(pool):
                def gather(s, par):
                    if not first(s, 2):
                        pool.wait_ge(added, s + (-1))
                        pool.wait_ge(put[par], landed(s - 2, par, KC))
                    for f, field in enumerate(FIELDS):
                        nc.gpsimd.tensor_copy(idx[:, par, f, :], C.rec[:, bass.ds(s * KC, KC), field].bitcast(U32)).then_inc(idxed, 1)
                    wait_apart(pool, C, (idxed, s * 3 + 3))
                    for f, t in enumerate((h3, h3)):
                        for j in range(KC):
                            nc.gpsimd.indirect_dma_start(out=G[:, par, f, j, :], out_offset=None, in_=t,
                                                         in_offset=bass.IndirectOffsetOnAxis(ap=idx[:, par, f, j:j + 1], axis=0)
                                                         ).then_inc(got[par], 16)

                def scatter(s, par):
                    wait_apart(pool, C, (relued, s + 1))
                    for j in range(KC):
                        nc.gpsimd.indirect_dma_start(out=by_src, out_offset=bass.IndirectOffsetOnAxis(ap=idx[:, par, 2, j:j + 1], axis=0),
                                                     in_=M[:, par, j, :], in_offset=None).then_inc(put[par], 16)
                run_steps(pool, n, [(0, gather), (1, scatter)])
                all_landed(pool, put, n, KC)

            @block.vector
            def _(dve):
                def add(s, par):
                    dve.wait_ge(got[par], landed(s, par, 2 * KC))
                    dve.wait_ge(attr_read[par], landed(s, par))
                    g = [G[:, par, f, :, :] for f in range(3)]
                    nc.vector.tensor_tensor(g[0], g[0], g[1], ALU.add).then_inc(summed0, 1)
                    dve.wait_ge(summed0, s + 1)
                    if not first(s, 2):
                        dve.wait_ge(relued, s + (-1))
                        dve.wait_ge(put[par], landed(s - 2, par, KC))
                        dve.wait_ge(summed, s + (-1))
                    nc.vector.tensor_tensor(M[:, par, :, :], g[0], g[2], ALU.add).then_inc(added, 1)

                def evacuate(s, par):
                    dve.wait_ge(summed, s + 1)
                    if not first(s, 2):
                        dve.wait_ge(stored[par], landed(s - 2, par))
                    nc.vector.tensor_copy(res[:, par, :, :], C.bank[par][:, :].rearrange("p (j d) -> p j d", j=KC)).then_inc(evac, 1)
                run_steps(dve, n, [(1, evacuate), (0, add)])

            @block.scalar
            def _(act):
                def relu(s, par):
                    act.wait_ge(added, s + 1)
                    nc.scalar.activation(M[:, par, :, :], M[:, par, :, :], ACT.Relu).then_inc(relued, 1)
                    for j in range(KC):
                        ins = nc.scalar.activation(seg[:, par, j, :], C.same_d[:, bass.ds((s * KC + j) * P, P)], ACT.Copy)
                    ins.then_inc(segged, 1)
                run_steps(act, n, [(0, relu)])

            @block.tensor
            def _(pe):
                def total(s, par):
                    pe.wait_ge(segged, s + 1)
                    if not first(s, 2):
                        pe.wait_ge(evac, s + (-1))
                    for j in range(KC):
                        ins = nc.tensor.matmul(C.bank[par][:, j * D:(j + 1) * D], seg[:, par, j, :], M[:, par, j, :], start=True, stop=True)
                    ins.then_inc(summed, 1)
                run_steps(pe, n, [(0, total)])

            @block.sync
            def _(sp):
                def read_attr(s, par):
                    if not first(s, 2):
                        wait_apart(sp, C, (added, s + (-1)))
                    sp.dma_start(G[:, par, 2, :, :], rows(attr_d, s, KC)).then_inc(attr_read[par], 16)

                def store(s, par):
                    wait_apart(sp, C, (evac, s + 1))
                    sp.dma_start(rows(table_d, s, KC), res[:, par, :, :]).then_inc(stored[par], 16)
                run_steps(sp, n, [(0, read_attr), (2, store)])
                all_landed(sp, stored, n)
        carry_over(nc, C, "l3c", 0, table_d, zero)

    with ExitStack() as ctx:
        m = Mem(nc, ctx)
        M = m.sb("l3s_M", [P, 4, KC, D])
        res = m.sb("l3s_res", [P, 2, KC, D])
        key = m.sb("l3s_key", [P, 2, KC])
        seg = m.sb("l3s_seg", [P, 2, KC, P])
        kept, shown, segged, summed, evac = (m.sem(f"l3s_{x}") for x in ("kept", "shown", "segged", "summed", "evac"))
        read = [m.sem(f"l3s_read{j}") for j in range(4)]
        stored = [m.sem(f"l3s_stored{j}") for j in range(2)]
        with nc.Block() as block:
            @block.sync
            def _(sp):
                def load(s, r):
                    if not first(s, 4):
                        wait_apart(sp, C, (summed, s + (-3)))
                    sp.dma_start(M[:, r, :, :], rows(by_src, s, KC)).then_inc(read[r], 16)

                def store(s, r):
                    par = r % 2
                    wait_apart(sp, C, (evac, s + 1))
                    sp.dma_start(rows(table_s, s, KC), res[:, par, :, :]).then_inc(stored[par], 16)
                run_steps(sp, n, [(0, load), (4, store)], 4)
                all_landed(sp, stored, n)

            @block.vector
            def _(dve):
                def keep(s, r):
                    par = r % 2
                    if not first(s, 2):
                        dve.wait_ge(shown, s + (-1))
                    nc.vector.tensor_copy(key[:, par, :], C.src_keys[:, bass.ds(s * KC, KC)]).then_inc(kept, 1)

                def compare(s, r):
                    par = r % 2
                    dve.wait_ge(shown, s + 1)
                    if not first(s, 2):
                        dve.wait_ge(summed, s + (-1))
                    for j in range(KC):
                        ins = nc.vector.tensor_scalar(seg[:, par, j, :], C.bank[2 + par][:, j * P:(j + 1) * P], key[:, par, j:j + 1], None, ALU.is_equal)
                    ins.then_inc(segged, 1)

                def evacuate(s, r):
                    par = r % 2
                    dve.wait_ge(summed, s + 1)
                    if not first(s, 2):
                        dve.wait_ge(stored[par], landed(s - 2, par))
                    nc.vector.tensor_copy(res[:, par, :, :], C.bank[par][:, :].rearrange("p (j d) -> p j d", j=KC)).then_inc(evac, 1)
                run_steps(dve, n, [(3, evacuate), (1, compare), (0, keep)], 4)

            @block.tensor
            def _(pe):
                def show(s, r):
                    par = r % 2
                    pe.wait_ge(kept, s + 1)
                    if not first(s, 2):
                        pe.wait_ge(segged, s + (-1))
                    for j in range(KC):
                        ins = nc.tensor.transpose(C.bank[2 + par][:, j * P:(j + 1) * P], key[:, par, j:j + 1].broadcast_to([P, P]), C.ident[:, :])
                    ins.then_inc(shown, 1)

                def total(s, r):
                    par = r % 2
                    pe.wait_ge(segged, s + 1)
                    pe.wait_ge(read[r], landed(s, r, ring=4))
                    if not first(s, 2):
                        pe.wait_ge(evac, s + (-1))
                    for j in range(KC):
                        ins = nc.tensor.matmul(C.bank[par][:, j * D:(j + 1) * D], seg[:, par, j, :], M[:, r, j, :], start=True, stop=True)
                    ins.then_inc(summed, 1)
                run_steps(pe, n, [(2, total), (0, show)], 4)
        carry_over(nc, C, "l3sc", 1, table_s, zero)


def nodes_l3(nc, C, A, h3, x3, table_d, table_s, out):
    n = NODE_STEPS
    KP = KT * P
    with ExitStack() as ctx:
        m = Mem(nc, ctx)
        W1p, W2p = ([m.sb(f"ne_{w}{part}", [P, k, k2], F32R) for part in ("high", "low")] for w, k, k2 in (("W1", 2, 2 * D), ("W2", 4, D)))
        with ExitStack() as load:
            W2 = Mem(nc, load).sb("ne_W2", [P, 4, D])
            load_all(nc, C, "ne_second", [(W2[:, :, :], A["l3_w2"].rearrange("(h p) d -> p h d", p=P))])
            split_in_two(nc, Mem(nc, load), "ne_W2", [(W2[:, :, :], W2p[0][:, :, :], W2p[1][:, :, :])])
        W1 = m.sb("ne_W1", [P, 2, 2 * D])
        g1, b1, g2, b2 = (m.sb(f"ne_{x}", [P, k]) for x, k in (("g1", 4), ("b1", 4), ("g2", 2), ("b2", 2)))
        eps1 = m.sb("ne_eps", [P, 1])
        load_all(nc, C, "ne", [(W1[:, :, :], A["l3_w1"].rearrange("(h p) d -> p h d", p=P)),
                               (g1[:, :], A["l3_g1"]), (b1[:, :], A["l3_b1"]), (g2[:, :], A["l3_g2"]), (b2[:, :], A["l3_b2"]),
                               (eps1[:, :], A["l3_eps"].broadcast_to([P, 1]))])
        T = m.sb("ne_T", [P, n, 2, KP])
        scale1, bias1, scale2, bias2 = (m.sb(f"ne_{x}", [P, k]) for x, k in (("sc1", 4), ("bi1", 4), ("sc2", 2), ("bi2", 2)))
        with ExitStack() as inner:
            m = Mem(nc, inner)
            split_in_two(nc, m, "ne_W1", [(W1[:, :, :], W1p[0][:, :, :], W1p[1][:, :, :])])
            tiles = inner.enter_context(ExitStack())
            mt = Mem(nc, tiles)
            H3 = mt.sb("ne_H3", [P, 2, KT, D])
            Gd, Gs = mt.sb("ne_Gd", [P, 2, KT, D]), mt.sb("ne_Gs", [P, 2, KT, D])
            H = mt.sb("ne_H", [P, 2, KT, D + 1])
            slots_d, slots_s = mt.sb("ne_slotsd", [P, 2, KT], U32), mt.sb("ne_slotss", [P, 2, KT], U32)
            prep, part, built, grammed, turned, copied, slotted, masked = (m.sem(f"ne_{x}") for x in
                                                                ("prep", "part", "built", "grammed", "turned", "copied", "slotted", "masked"))
            hread = [m.sem(f"ne_hread{j}") for j in range(2)]
            got = [C.mem.sem(f"ne_got{j}") for j in range(2)]
            with nc.Block() as block:
                @block.sync
                def _(sp):
                    def load(s, r):
                        if not first(s, 2):
                            wait_apart(sp, C, (part, s + (-1)))
                        sp.dma_start(H3[:, r, :, :], rows(h3, s, KT)).then_inc(hread[r], 16)
                    run_steps(sp, n, [(0, load)])

                @block.gpsimd
                def _(pool):
                    def gather(s, r):
                        if not first(s, 2):
                            pool.wait_ge(built, s + (-1))
                        nc.gpsimd.tensor_copy(slots_d[:, r, :], C.slot_of[0][:, bass.ds(s * KT, KT)]).then_inc(slotted, 1)
                        copy_slots(nc, C, pool, s, r, slots_s, C.slot_of[1], slotted, 2)
                        gather_sums(nc, pool, s, r, slots_d, table_d, Gd, got)
                        gather_sums(nc, pool, s, r, slots_s, table_s, Gs, got)
                    run_steps(pool, n, [(0, gather)])

                @block.vector
                def _(dve):
                    nc.vector.tensor_scalar(eps1[:, :], eps1[:, :], 1.0, None, ALU.add).then_inc(prep, 1)
                    nc.vector.memset(H[:, 0, :, D:D + 1], 1.0).then_inc(prep, 1)
                    nc.vector.memset(H[:, 1, :, D:D + 1], 1.0).then_inc(prep, 1)
                    dve.wait_ge(prep, 3)

                    def make(s, r):
                        dve.wait_ge(hread[r], landed(s, r))
                        dve.wait_ge(got[r], landed(s, r, 2 * KT))
                        nc.vector.scalar_tensor_tensor(out=Gd[:, r, :, :], in0=H3[:, r, :, :], scalar=eps1[:, 0:1], in1=Gd[:, r, :, :],
                                                       op0=ALU.mult, op1=ALU.add).then_inc(part, 1)
                        dve.wait_ge(part, s + 1)
                        if not first(s, 2):
                            dve.wait_ge(turned, s + (-1))
                        ins = nc.vector.tensor_tensor(H[:, r, :, 0:D], Gd[:, r, :, :], Gs[:, r, :, :], ALU.add)
                        if last_step(s, n):
                            ins.then_inc(masked, 1)
                            dve.wait_ge(masked, 1)
                            ins = nc.vector.tensor_scalar(H[:, r, KT - 1, :], H[:, r, KT - 1, :], C.node_ok[:, 0:1], None, ALU.mult)
                        ins.then_inc(built, 1)
                    run_steps(dve, n, [(0, make)])

                @block.tensor
                def _(pe):
                    pe.wait_ge(prep, 3)

                    def work(s, r):
                        pe.wait_ge(built, s + 1)
                        for k in range(KT):
                            for h in range(2):
                                nc.tensor.matmul(C.bank[h][:, 0:D + 1], H[:, r, k, h * P:(h + 1) * P], H[:, r, k, :],
                                                 start=first(s, 1) and k == 0, stop=last_step(s, n) and k == KT - 1)
                        if not first(s, 2):
                            pe.wait_ge(copied, s + (-1))
                        transpose_tiles(nc, C, 2 + 2 * r, H[:, r, :, :]).then_inc(turned, 1)
                    run_steps(pe, n, [(0, work)])

                @block.scalar
                def _(act):
                    def copy(s, r):
                        act.wait_ge(turned, s + 1)
                        nc.scalar.activation(T[:, bass.ds(s, 1), :, :].rearrange("p o h e -> p (o h) e"), C.banks(2 + 2 * r, 2, 2), ACT.Copy).then_inc(copied, 1)
                    run_steps(act, n, [(0, copy)])

            tiles.close()
            gram, prod, mean, ex2, tmp = m.sb("ne_gram", [P, 2, D + 1]), m.sb("ne_prod", [P, 2, 2 * D]), m.sb("ne_mean", [P, 4]), m.sb("ne_ex2", [P, 4]), m.sb("ne_tmp", [P, 4])
            v, t, a = m.sem("ne_v"), m.sem("ne_t"), m.sem("ne_a")
            with nc.Block() as block:
                @block.vector
                def _(dve):
                    k = [0]

                    def link(ins):
                        ins.then_inc(v, 1)
                        k[0] += 1
                        dve.wait_ge(v, k[0])

                    for h in range(2):
                        link(nc.vector.tensor_copy(gram[:, h, :], C.bank[h][:, 0:D + 1]))
                    dve.wait_ge(t, 1)
                    for h in range(2):
                        link(nc.vector.tensor_tensor(prod[:, h, :], C.bank[2 + h][:, :], W1[:, h, :], ALU.mult))
                    dve.wait_ge(t, 2)
                    link(nc.vector.tensor_scalar(mean[:, :], C.bank[4][:, 0:4], 1.0 / N, None, ALU.mult))
                    link(nc.vector.tensor_scalar(ex2[:, :], C.bank[5][:, 0:4], 1.0 / N, None, ALU.mult))
                    link(nc.vector.tensor_tensor(tmp[:, :], mean[:, :], mean[:, :], ALU.mult))
                    link(nc.vector.tensor_tensor(ex2[:, :], ex2[:, :], tmp[:, :], ALU.subtract))
                    link(nc.vector.tensor_scalar(ex2[:, :], ex2[:, :], 0.0, None, ALU.max))
                    dve.wait_ge(a, 1)
                    link(nc.vector.reciprocal(scale1[:, :], tmp[:, :]))
                    link(nc.vector.tensor_tensor(scale1[:, :], scale1[:, :], g1[:, :], ALU.mult))
                    link(nc.vector.tensor_tensor(tmp[:, :], scale1[:, :], mean[:, :], ALU.mult))
                    link(nc.vector.tensor_tensor(bias1[:, :], b1[:, :], tmp[:, :], ALU.subtract))

                @block.scalar
                def _(act):
                    act.wait_ge(v, 9)
                    nc.scalar.activation(tmp[:, :], ex2[:, :], ACT.Sqrt, bias=C.eps[:, 0:1]).then_inc(a, 1)

                @block.tensor
                def _(pe):
                    pe.wait_ge(v, 2)
                    for q in range(2):
                        for h in range(2):
                            ins = nc.tensor.matmul(C.bank[2 + q][:, :], gram[:, h, q * P:(q + 1) * P], W1[:, h, :], start=h == 0, stop=h == 1)
                    ins.then_inc(t, 1)
                    for o in range(4):
                        for h in range(2):
                            nc.tensor.matmul(C.bank[4][:, o:o + 1], W1[:, h, o * P:(o + 1) * P], gram[:, h, D:D + 1], start=h == 0, stop=h == 1)
                    pe.wait_ge(v, 4)
                    for o in range(4):
                        for h in range(2):
                            ins = nc.tensor.matmul(C.bank[5][:, o:o + 1], prod[:, h, o * P:(o + 1) * P], C.ones[:, 0:1], start=h == 0, stop=h == 1)
                    ins.then_inc(t, 1)

        with ExitStack() as inner:
            m = Mem(nc, inner)
            R1 = m.sb("nf_R1", [P, 2, KP])
            R = [m.sb(f"nf_R{part}", [P, 4, KP], F32R) for part in ("high", "low")]
            X = [m.sb(f"nf_X{part}", [P, 2, KP], F32R) for part in ("high", "low")]
            st = m.sb("nf_st", [P, 2, n, 6])
            xhigh, xlow, one, relued, rhigh, rlow, two, kept, sampled = (
                m.sem(f"nf_{x}") for x in ("xhigh", "xlow", "one", "relued", "rhigh", "rlow", "two", "kept", "sampled"))
            with nc.Block() as block:
                @block.tensor
                def _(pe):
                    def layer1(s, r):
                        pe.wait_ge(xlow, s + 1)
                        for o in range(4):
                            if not first(s, 1):
                                pe.wait_ge(relued, s * 4 + (o - 3))
                            for k, (h, x, y) in enumerate(PART_PRODUCTS):
                                ins = nc.tensor.matmul(C.bank[o][:, :], W1p[y][:, h, o * P:(o + 1) * P], X[x][:, h, :],
                                                       start=k == 0, stop=k == len(PART_PRODUCTS) - 1)
                            ins.then_inc(one, 1)

                    def layer2(s, r):
                        if not first(s, 2):
                            pe.wait_ge(kept, s * 2 + (-2))
                        for o in range(4):
                            pe.wait_ge(rlow, s * 4 + (o + 1))
                            for q in range(2):
                                for k, (x, y) in enumerate(((0, 0), (0, 1), (1, 0))):
                                    ins = nc.tensor.matmul(C.bank[4 + 2 * r + q][:, :], W2p[y][:, o, q * P:(q + 1) * P], R[x][:, o, :],
                                                           start=o == 0 and k == 0, stop=o == 3 and k == 2)
                            ins.then_inc(two, 1)
                    run_steps(pe, n, [(0, layer1), (1, layer2)])

                @block.scalar
                def _(act):
                    def high_x(s, r):
                        if not first(s, 1):
                            act.wait_ge(one, s * 4)
                        nc.scalar.activation(X[0][:, :, :], T[:, bass.ds(s, 1), :, :].rearrange("p o h e -> p (o h) e"), ACT.Copy).then_inc(xhigh, 1)

                    def relu(s, r):
                        for o in range(4):
                            act.wait_ge(one, s * 4 + (o + 1))
                            if not (first(s, 1) and o < 2):
                                act.wait_ge(rlow, s * 4 + (o - 1))
                            nc.scalar.activation(R1[:, o % 2, :], C.bank[o][:, :], ACT.Relu, bias=bias1[:, o:o + 1], scale=scale1[:, o:o + 1]).then_inc(relued, 1)
                            act.wait_ge(relued, s * 4 + (o + 1))
                            if not first(s, 1):
                                act.wait_ge(two, s * 4 + (o - 3))
                            nc.scalar.activation(R[0][:, o, :], R1[:, o % 2, :], ACT.Copy).then_inc(rhigh, 1)
                    run_steps(act, n, [(0, high_x), (1, relu)])

                @block.vector
                def _(dve):
                    def low_x(s, r):
                        dve.wait_ge(xhigh, s + 1)
                        nc.vector.tensor_tensor(X[1][:, :, :], T[:, bass.ds(s, 1), :, :].rearrange("p o h e -> p (o h) e"),
                                                X[0][:, :, :], ALU.subtract).then_inc(xlow, 1)

                    def low_r(s, r):
                        for o in range(4):
                            dve.wait_ge(rhigh, s * 4 + (o + 1))
                            nc.vector.tensor_tensor(R[1][:, o, :], R1[:, o % 2, :], R[0][:, o, :], ALU.subtract).then_inc(rlow, 1)

                    def keep(s, r):
                        for q in range(2):
                            if q == 0:
                                dve.wait_ge(two, s * 4 + 4)
                            nc.vector.tensor_copy(T[:, bass.ds(s, 1), q, :].rearrange("p o e -> p (o e)"), C.bank[4 + 2 * r + q][:, :]).then_inc(kept, 1)
                        for q in range(2):
                            wait_apart(dve, C, (kept, s * 2 + (q + 1)))
                            w = KP - P + LAST_NODES if last_step(s, n) else KP
                            nc.vector.bn_stats(st[:, q, bass.ds(s, 1), :].rearrange("p o k -> p (o k)"),
                                               T[:, bass.ds(s, 1), q, 0:w].rearrange("p o e -> p (o e)")).then_inc(sampled, 1)
                    run_steps(dve, n, [(0, low_x), (1, low_r), (2, keep)])

            mv, sd, tmp = m.sb("nf_mv", [P, 2, 2]), m.sb("nf_sd", [P, 2]), m.sb("nf_tmp", [P, 2])
            v, a = m.sem("nf_v"), m.sem("nf_a")
            with nc.Block() as block:
                @block.vector
                def _(dve):
                    for q in range(2):
                        nc.vector.bn_aggr(mv[:, q, :], st[:, q, :, :]).then_inc(v, 1)
                    dve.wait_ge(a, 1)
                    nc.vector.reciprocal(scale2[:, :], sd[:, :]).then_inc(v, 1)
                    dve.wait_ge(v, 3)
                    nc.vector.tensor_tensor(scale2[:, :], scale2[:, :], g2[:, :], ALU.mult).then_inc(v, 1)
                    dve.wait_ge(v, 4)
                    nc.vector.tensor_tensor(tmp[:, :], scale2[:, :], mv[:, :, 0], ALU.mult).then_inc(v, 1)
                    dve.wait_ge(v, 5)
                    nc.vector.tensor_tensor(bias2[:, :], b2[:, :], tmp[:, :], ALU.subtract).then_inc(v, 1)

                @block.scalar
                def _(act):
                    act.wait_ge(v, 2)
                    nc.scalar.activation(sd[:, :], mv[:, :, 1], ACT.Sqrt, bias=C.eps[:, 0:1]).then_inc(a, 1)

        m = Mem(nc, ctx)
        R2 = m.sb("ng_R2", [P, 2, 2, KP])
        X, O = m.sb("ng_X", [P, 2, KT, D]), m.sb("ng_O", [P, 2, KT, D])
        relued, turned, added = (m.sem(f"ng_{x}") for x in ("relued", "turned", "added"))
        xread = [m.sem(f"ng_xread{j}") for j in range(2)]
        stored = [m.sem(f"ng_stored{j}") for j in range(2)]
        tail_put = m.sem("ng_tail")
        with nc.Block() as block:
            @block.sync
            def _(sp):
                def load(s, r):
                    if not first(s, 2):
                        wait_apart(sp, C, (added, s + (-1)))
                    sp.dma_start(X[:, r, :, :], rows(x3, s, KT)).then_inc(xread[r], 16)

                def store(s, r):
                    wait_apart(sp, C, (added, s + 1))
                    if last_step(s, n):
                        full = s * KT * P
                        sp.dma_start(out[full:full + (KT - 1) * P, :].rearrange("(j p) d -> p j d", p=P), O[:, r, 0:KT - 1, :]).then_inc(stored[r], 16)
                        sp.dma_start(out[full + (KT - 1) * P:N, :], O[0:LAST_NODES, r, KT - 1, :]).then_inc(tail_put, 16)
                    else:
                        sp.dma_start(rows(out, s, KT), O[:, r, :, :]).then_inc(stored[r], 16)
                run_steps(sp, n, [(0, load), (1, store)])
                all_landed(sp, stored, n)
                sp.wait_ge(tail_put, 16)

            @block.scalar
            def _(act):
                def relu(s, r):
                    if not first(s, 2):
                        act.wait_ge(turned, s + (-1))
                    for q in range(2):
                        ins = nc.scalar.activation(R2[:, r, q, :], T[:, bass.ds(s, 1), q, :].rearrange("p o e -> p (o e)"), ACT.Relu,
                                                   bias=bias2[:, q:q + 1], scale=scale2[:, q:q + 1])
                    ins.then_inc(relued, 1)
                run_steps(act, n, [(0, relu)])

            @block.tensor
            def _(pe):
                def turn(s, r):
                    pe.wait_ge(relued, s + 1)
                    if not first(s, 2):
                        pe.wait_ge(added, s + (-1))
                    for k in range(KT):
                        for q in range(2):
                            ins = nc.tensor.transpose(C.bank[2 * r + k // 2][:, (k % 2) * D + q * P:(k % 2) * D + (q + 1) * P],
                                                      R2[:, r, q, k * P:(k + 1) * P], C.ident[:, :])
                    ins.then_inc(turned, 1)
                run_steps(pe, n, [(0, turn)])

            @block.vector
            def _(dve):
                def add(s, r):
                    dve.wait_ge(turned, s + 1)
                    dve.wait_ge(xread[r], landed(s, r))
                    if not first(s, 2):
                        dve.wait_ge(stored[r], landed(s - 2, r))
                    nc.vector.tensor_tensor(O[:, r, :, :], C.banks(2 * r, 2, KT), X[:, r, :, :], ALU.add).then_inc(added, 1)
                run_steps(dve, n, [(0, add)])


class Constants:
    pass


def build(nc, A, out):
    with ExitStack() as ctx:
        m = Mem(nc, ctx, clear=False)
        C = Constants()
        psum = m.ps("psum", [P, 8, 512])
        C.bank = [psum[:, k, :] for k in range(8)]
        C.banks = lambda k, nb, parts: psum[:, k:k + nb, :].rearrange("p b e -> p (b e)").rearrange("p (j d) -> p j d", j=parts)
        C.ones, C.ident, C.upper, C.lower = (m.sb(x, [P, P]) for x in ("ones", "ident", "upper", "lower"))
        C.eps, C.part, C.node_ok, C.edge_ok = (m.sb(x, [P, 1]) for x in ("eps", "part", "node_ok", "edge_ok"))
        C.iota, C.chunk0 = m.sb("iota", [P, NT]), m.sb("chunk0", [P, NT])
        C.slot_of = [m.sb(f"slot_of{k}", [P, NT], U32) for k in range(2)]
        edges = ctx.enter_context(ExitStack())
        me = Mem(nc, edges)
        C.rec = me.sb("sorted_rec", [P, NC, REC], I32)
        C.weight, C.lock, C.decay, C.src_keys = (me.sb(x, [P, NC]) for x in ("weight", "lock", "decay_f", "src_keys"))
        C.same_d = me.sb("same_d", [P, EP], BF16)
        C.carry = [me.sb(f"carry{k}", [P, NC]) for k in range(2)]
        C.fix_row = [me.sb(f"fix_row{k}", [P, 1], U32) for k in range(2)]
        C.passed = m.sem("passed")
        C.mem = m
        rec_d, rec_s = m.dram("rec_d", [EP, REC], I32), m.dram("rec_s", [EP, REC], I32)
        tables = [m.dram(f"sums{k}", [ZROW + 1, D]) for k in range(10)]
        by_src, attr_d = m.dram("by_src", [EP, D]), m.dram("attr_d", [EP, D])
        x1, h1, x2, e0, h2, x3, h3 = (m.dram(x, [NP, D]) for x in ("x1", "h1", "x2", "e0", "h2", "x3", "h3"))

        make_constants(nc, C)
        index_nodes(nc, C, A, rec_d, rec_s)
        sort_tables(nc, C, A, rec_d, rec_s)

        with ExitStack() as l0:
            ml = Mem(nc, l0)
            Y, R, conv_bias = ml.sb("Y", [P, NC, D]), ml.sb("R", [P, NC, D]), ml.sb("conv_bias", [P, D])
            for i in range(4):
                l0_layer(nc, C, A, i, tables[i], tables[i - 1] if i else None, Y, R, conv_bias)
                carry_over(nc, C, f"l0c{i}", 0, tables[i], conv_bias)
            l0_total(nc, C, tables[3], tables[4], A["l0_cb"], R)
        biases = me.sb("layer_bias", [P, 5, D])
        load_all(nc, C, "bias", [(biases[:, 0, :], A["l1_b"].broadcast_to([P, D])), (biases[:, 1, :], A["l2_bias1"].broadcast_to([P, D])),
                                 (biases[:, 2, :], A["l2_bias2"].broadcast_to([P, D]))])
        zs = m.sem("zero_made")
        with nc.Block() as block:
            @block.vector
            def _(dve):
                nc.vector.memset(biases[:, 3, :], 0.0).then_inc(zs, 1)
        C.coef = me.sb("coef", [P, NC, 20])
        nodes_l0(nc, C, A, tables[4], x1, h1)
        with ExitStack() as l1:
            Wt = Mem(nc, l1).sb("Wt", [P, 2, D])
            l1_weights(nc, C, A, Wt)
            l1_edges(nc, C, A, h1, tables[5], biases[:, 0, :], Wt)
        nodes_l1(nc, C, x1, tables[5], x2, e0)
        l2_edges(nc, C, A, 1, e0, tables[6], biases[:, 1, :], attr_d)
        nodes_l2a(nc, C, A, e0, tables[6], h2)
        l2_edges(nc, C, A, 2, h2, tables[7], biases[:, 2, :])
        nodes_l2b(nc, C, A, h2, e0, x2, tables[7], x3, h3)
        l3_edges(nc, C, attr_d, h3, by_src, tables[8], tables[9], biases[:, 3, :])
        edges.close()
        nodes_l3(nc, C, A, h3, x3, tables[8], tables[9], out)


def lay(inputs):
    import numpy as _np
    get = lambda k: _np.asarray(inputs[k])
    src, dst, typ, w, lock = (get(k) for k in ("src", "dst", "edge_type_240", "edge_weight", "L1_gnn_node_lock"))

    def filled(a, fill, n):
        return _np.concatenate([a, _np.full((n - len(a),) + a.shape[1:], fill, a.dtype)])

    def cols(a, fill, n):
        return filled(a, fill, n).reshape(-1, P).T

    def by_part(v):
        return v.reshape(-1, P).T
    out = {
        "keys": _np.concatenate([cols(dst, PAD_KEY, EP), cols(src, PAD_KEY, EP), cols(lock, NO_KEY, LC * P)], axis=1),
        "fields": _np.stack([cols(src, PAD_KEY, EP), cols(dst, PAD_KEY, EP), cols(w, 0, EP).view(_np.int32), cols(typ, 0, EP)], axis=2),
        "x": filled(get("x"), 0, NP), "attr": filled(get("edge_attr_256"), 0, EP),
        "comp": _np.concatenate([get("L2_gnn_comp1"), get("L2_gnn_comp2")], axis=1),
        "now": get("L2_gnn_current_time").reshape(1, 1),
        "l0_cb": get("L0_gnn_conv_b"), "l0_lb": get("L0_gnn_ln_bias"),
        "l0_ls": get("L0_gnn_ln_scale"), "l0_w": get("L0_gnn_conv_w"),
        "l0_pw": get("L0_gnn_post_w"), "l0_pb": get("L0_gnn_post_b").reshape(1, D),
        "l1_wt": get("L1_gnn_W").T, "l1_b": get("L1_gnn_b").reshape(1, D),
        "l2_basis1": get("L2_gnn_basis1"), "l2_basis2": get("L2_gnn_basis2"),
        "l2_bias1": get("L2_gnn_bias1").reshape(1, D), "l2_bias2": get("L2_gnn_bias2").reshape(1, D),
        "l2_lw1": get("L2_gnn_loop_w1"), "l2_lw2": get("L2_gnn_loop_w2"),
        "l2_g": get("L2_gnn_ln_g").reshape(1, D), "l2_b": get("L2_gnn_ln_b").reshape(1, D),
        "l3_w1": get("L3_gnn_W1"), "l3_w2": get("L3_gnn_W2"), "l3_eps": get("L3_gnn_epsilon").reshape(1, 1),
        "l3_g1": by_part(get("L3_gnn_gamma1")), "l3_b1": by_part(get("L3_gnn_beta1")),
        "l3_g2": by_part(get("L3_gnn_gamma2")), "l3_b2": by_part(get("L3_gnn_beta2")),
    }
    return {"in_" + k: _np.ascontiguousarray(a) for k, a in out.items()}


def kernel(**inputs):
    import concourse.bacc as _bacc
    from concourse import mybir as _mybir
    from concourse.bass_utils import run_bass_kernel_spmd as _run
    nc = _bacc.Bacc("TRN2", target_bir_lowering=False, num_devices=1)
    arrays = lay(inputs)
    A = {k[3:]: nc.dram_tensor(k, a.shape, _mybir.dt.from_np(a.dtype), kind="ExternalInput").ap() for k, a in arrays.items()}
    out = nc.dram_tensor("out", (N, D), _mybir.dt.float32, kind="ExternalOutput").ap()
    build(nc, A, out)
    r = _run(nc, [arrays], core_ids=[0])
    return r.results[0]["out"]
```
